# Optimizing a Trainium2 kernel written in Bass

```python
import numpy as np
import jax
import jax.numpy as jnp

def _softmax(x, axis=-1):
    return jax.nn.softmax(x, axis=axis)

def _gelu(x):
    return jax.nn.gelu(x, approximate=True)

def _silu(x):
    return jax.nn.silu(x)

def _sigmoid(x):
    return jax.nn.sigmoid(x)

def _layernorm(x, axis=-1, eps=1e-05):
    m = jnp.mean(x, axis=axis, keepdims=True)
    v = jnp.var(x, axis=axis, keepdims=True)
    return (x - m) / jnp.sqrt(v + eps)

def _scatter_add(tgt, idx, src, axis=0):
    return tgt.at[idx].add(src)

def _segment_sum(src, seg, n):
    return jax.ops.segment_sum(src, seg, n)
kernel_name = 'mk_seq_postln_d2_jaxref_r8_742803'

def setup_inputs(seed: int=0):
    np.random.seed(seed)
    _w = jnp.asarray

    def _L0_attn_setup():
        import jax, jax.numpy as jnp
        import numpy as np
        B, N, C, H, K = (4, 512, 128, 16, 2)
        D = C // H

        def _kernel(x):
            return jax.nn.silu(x) + 0.5
        key = jax.random.key(seed)
        ks = jax.random.split(key, 8)
        s = 0.02
        x = jax.random.normal(ks[0], (B, N, C), jnp.float32)
        Wq = jax.random.normal(ks[1], (C, C), jnp.float32) * s
        bq = jnp.zeros((C,), jnp.float32)
        Wk = jax.random.normal(ks[2], (K, C, C), jnp.float32) * s
        bk = jnp.zeros((K, C), jnp.float32)
        Wv = jax.random.normal(ks[3], (K, C, C), jnp.float32) * s
        bv = jnp.zeros((K, C), jnp.float32)
        Wo = jax.random.normal(ks[4], (C, C), jnp.float32) * s
        bo = jnp.zeros((C,), jnp.float32)
        ln_g = jnp.ones((C,), jnp.float32)
        ln_b = jnp.zeros((C,), jnp.float32)
        return dict(x=x, Wq=Wq, bq=bq, Wk=Wk, bk=bk, Wv=Wv, bv=bv, Wo=Wo, bo=bo, ln_g=ln_g, ln_b=ln_b)
    _L0_attn_in = _L0_attn_setup()

    def _L0_ffn_setup():
        import jax, jax.numpy as jnp
        import numpy as np
        DIM = 128
        DEPTH = 2
        HEADS = 8
        DIM_HEAD = 64
        WINDOW = 64
        INNER = HEADS * DIM_HEAD
        HID = int(DIM * 4 * 2 / 3)
        B, N = (2, 1024)
        QK_SCALE = 8.0

        def shift_token(t):
            t1, t2 = jnp.split(t, 2, axis=-1)
            t2 = jnp.pad(t2, ((0, 0), (1, 0), (0, 0)))[:, :-1]
            return jnp.concatenate([t1, t2], axis=-1)

        def l2norm(t):
            return t / jnp.clip(jnp.linalg.norm(t, axis=-1, keepdims=True), 1e-12)

        def rotate_half(x):
            x1, x2 = jnp.split(x, 2, axis=-1)
            return jnp.concatenate([-x2, x1], axis=-1)

        def rotary_xpos(q, k):
            n = q.shape[-2]
            half_idx = jnp.arange(0, DIM_HEAD, 2, dtype=jnp.float32)
            inv_freq = 1.0 / 10000.0 ** (half_idx / DIM_HEAD)
            t = jnp.arange(n, dtype=jnp.float32)
            freqs = t[:, None] * inv_freq[None, :]
            freqs = jnp.concatenate([freqs, freqs], axis=-1)
            base = (half_idx + 0.4 * DIM_HEAD) / (1.4 * DIM_HEAD)
            power = (t - n // 2) / float(WINDOW // 2)
            scale = base[None, :] ** power[:, None]
            scale = jnp.concatenate([scale, scale], axis=-1)
            cos, sin = (jnp.cos(freqs), jnp.sin(freqs))
            q = q * cos * scale + rotate_half(q) * sin * scale
            k = k * cos / scale + rotate_half(k) * sin / scale
            return (q, k)

        def local_attention(q, k, v):
            b, h, n, d = q.shape
            w = n // WINDOW
            bq = q.reshape(b, h, w, WINDOW, d) * QK_SCALE
            bk = k.reshape(b, h, w, WINDOW, d)
            bv = v.reshape(b, h, w, WINDOW, d)

            def look_around(t):
                p = jnp.pad(t, ((0, 0), (0, 0), (1, 0), (0, 0), (0, 0)))
                return jnp.concatenate([p[:, :, :w], p[:, :, 1:]], axis=3)
            bk, bv = (look_around(bk), look_around(bv))
            bt = jnp.arange(n).reshape(w, WINDOW)
            btp = jnp.pad(bt, ((1, 0), (0, 0)), constant_values=-1)
            btk = jnp.concatenate([btp[:w], btp[1:]], axis=1)
            sim = jnp.einsum('bhwid,bhwjd->bhwij', bq, bk)
            i = bt[:, :, None]
            j = btk[:, None, :]
            mask = (i < j) | (i > j + WINDOW) | (j == -1)
            sim = jnp.where(mask, -jnp.finfo(sim.dtype).max, sim)
            attn = jax.nn.softmax(sim, axis=-1)
            out = jnp.einsum('bhwij,bhwjd->bhwid', attn, bv)
            return out.reshape(b, h, n, d)

        def _layer(x, wqkv, qs, ksc, wo, lg, lb, w1, b1, w2, b2):
            b, n, _ = x.shape
            h = shift_token(x)
            qkv = h @ wqkv
            q, k, v = jnp.split(qkv, 3, axis=-1)
            to_heads = lambda t: t.reshape(b, n, HEADS, DIM_HEAD).transpose(0, 2, 1, 3)
            q, k, v = (to_heads(q), to_heads(k), to_heads(v))
            q = l2norm(q) * qs
            k = l2norm(k) * ksc
            q, k = rotary_xpos(q, k)
            o = local_attention(q, k, v)
            o = o.transpose(0, 2, 1, 3).reshape(b, n, INNER)
            x = x + o @ wo
            h = shift_token(x)
            mu = h.mean(-1, keepdims=True)
            var = h.var(-1, keepdims=True)
            h = (h - mu) / jnp.sqrt(var + 1e-05) * lg + lb
            h = h @ w1 + b1
            a, g = jnp.split(h, 2, axis=-1)
            h = a * jax.nn.gelu(g, approximate=False)
            x = x + h @ w2 + b2
            return x
        key = jax.random.key(seed)
        ks = jax.random.split(key, 6)
        return {'x': jax.random.normal(ks[0], (B, N, DIM), jnp.float32), 'wqkv': jax.random.normal(ks[1], (DEPTH, DIM, 3 * INNER), jnp.float32) * 0.02, 'q_scale': jnp.ones((DEPTH, DIM_HEAD), jnp.float32), 'k_scale': jnp.ones((DEPTH, DIM_HEAD), jnp.float32), 'wo': jax.random.normal(ks[2], (DEPTH, INNER, DIM), jnp.float32) * 0.02, 'ln_g': jnp.ones((DEPTH, DIM), jnp.float32), 'ln_b': jnp.zeros((DEPTH, DIM), jnp.float32), 'w1': jax.random.normal(ks[3], (DEPTH, DIM, 2 * HID), jnp.float32) * 0.02, 'b1': jnp.zeros((DEPTH, 2 * HID), jnp.float32), 'w2': jax.random.normal(ks[4], (DEPTH, HID, DIM), jnp.float32) * 0.02, 'b2': jnp.zeros((DEPTH, DIM), jnp.float32)}
    _L0_ffn_in = _L0_ffn_setup()

    def _L1_attn_setup():
        import math
        import jax, jax.numpy as jnp
        import numpy as np
        B, T, C, H, DQK, DV = (2, 256, 128, 16, 64, 64)
        key = jax.random.key(seed)
        ks = jax.random.split(key, 5)
        x = jax.random.normal(ks[0], (B, T, C), dtype=jnp.float32)
        w_q = jax.random.normal(ks[1], (H, DQK, C), dtype=jnp.float32) / math.sqrt(C)
        w_k = jax.random.normal(ks[2], (H, DQK, C), dtype=jnp.float32) / math.sqrt(C)
        w_v = jax.random.normal(ks[3], (H, DV, C), dtype=jnp.float32) / math.sqrt(C)
        w_o = jax.random.normal(ks[4], (DV * H, C), dtype=jnp.float32) / math.sqrt(C)
        return {'x': x, 'w_q': w_q, 'w_k': w_k, 'w_v': w_v, 'w_o': w_o}
    _L1_attn_in = _L1_attn_setup()

    def _L1_ffn_setup():
        import jax, jax.numpy as jnp
        import numpy as np
        import math
        EMBED_DIM = 128
        FFN_DIM = 512
        N_EXPERTS = 8
        TOP_K = 2
        CAP_FACTOR = 1.25
        key = jax.random.key(seed)
        k0, k1, k2, k3 = jax.random.split(key, 4)
        B, S = (4, 256)
        x = jax.random.normal(k0, (B, S, EMBED_DIM), dtype=jnp.float32)
        Wr = jax.random.normal(k1, (EMBED_DIM, N_EXPERTS), dtype=jnp.float32) * 0.02
        W1 = jax.random.normal(k2, (N_EXPERTS, EMBED_DIM, FFN_DIM), dtype=jnp.float32) * 0.02
        W2 = jax.random.normal(k3, (N_EXPERTS, FFN_DIM, EMBED_DIM), dtype=jnp.float32) * 0.02
        return {'x': x, 'Wr': Wr, 'W1': W1, 'W2': W2}
    _L1_ffn_in = _L1_ffn_setup()
    _d = {'L0_attn_x': _L0_attn_in['x'], 'L0_attn_Wq': _L0_attn_in['Wq'], 'L0_attn_bq': _L0_attn_in['bq'], 'L0_attn_Wk': _L0_attn_in['Wk'], 'L0_attn_bk': _L0_attn_in['bk'], 'L0_attn_Wv': _L0_attn_in['Wv'], 'L0_attn_bv': _L0_attn_in['bv'], 'L0_attn_Wo': _L0_attn_in['Wo'], 'L0_attn_bo': _L0_attn_in['bo'], 'L0_attn_ln_g': _L0_attn_in['ln_g'], 'L0_attn_ln_b': _L0_attn_in['ln_b'], 'L0_ffn_wqkv': _L0_ffn_in['wqkv'], 'L0_ffn_q_scale': _L0_ffn_in['q_scale'], 'L0_ffn_k_scale': _L0_ffn_in['k_scale'], 'L0_ffn_wo': _L0_ffn_in['wo'], 'L0_ffn_ln_g': _L0_ffn_in['ln_g'], 'L0_ffn_ln_b': _L0_ffn_in['ln_b'], 'L0_ffn_w1': _L0_ffn_in['w1'], 'L0_ffn_b1': _L0_ffn_in['b1'], 'L0_ffn_w2': _L0_ffn_in['w2'], 'L0_ffn_b2': _L0_ffn_in['b2'], 'L1_attn_w_q': _L1_attn_in['w_q'], 'L1_attn_w_k': _L1_attn_in['w_k'], 'L1_attn_w_v': _L1_attn_in['w_v'], 'L1_attn_w_o': _L1_attn_in['w_o'], 'L1_ffn_Wr': _L1_ffn_in['Wr'], 'L1_ffn_W1': _L1_ffn_in['W1'], 'L1_ffn_W2': _L1_ffn_in['W2']}
    _x0 = _d['L0_attn_x']
    _d['L0_attn_x'] = jax.random.normal(jax.random.fold_in(jax.random.key(seed), 1), (16, 256, 128), dtype=_x0.dtype)
    del _x0
    return _d

def reference(L0_attn_x, L0_attn_Wq, L0_attn_bq, L0_attn_Wk, L0_attn_bk, L0_attn_Wv, L0_attn_bv, L0_attn_Wo, L0_attn_bo, L0_attn_ln_g, L0_attn_ln_b, L0_ffn_wqkv, L0_ffn_q_scale, L0_ffn_k_scale, L0_ffn_wo, L0_ffn_ln_g, L0_ffn_ln_b, L0_ffn_w1, L0_ffn_b1, L0_ffn_w2, L0_ffn_b2, L1_attn_w_q, L1_attn_w_k, L1_attn_w_v, L1_attn_w_o, L1_ffn_Wr, L1_ffn_W1, L1_ffn_W2):

    def _L0_attn_ref(x, Wq, bq, Wk, bk, Wv, bv, Wo, bo, ln_g, ln_b):
        import jax, jax.numpy as jnp
        import numpy as np
        B, N, C, H, K = (4, 512, 128, 16, 2)
        D = C // H

        def _kernel(x):
            return jax.nn.silu(x) + 0.5
        dtype = x.dtype
        Bn, Nn, Cn = x.shape
        q = x + x @ Wq.T + bq
        ks = x[None] + jnp.einsum('bnc,kdc->kbnd', x, Wk) + bk[:, None, None, :]
        vs = x[None] + jnp.einsum('bnc,kdc->kbnd', x, Wv) + bv[:, None, None, :]
        q = q.reshape(Bn, Nn, H, D).transpose(0, 2, 1, 3)
        ks = ks.reshape(K, Bn, Nn, H, D).transpose(0, 1, 3, 2, 4)
        vs = vs.reshape(K, Bn, Nn, H, D).transpose(0, 1, 3, 2, 4)
        q = _kernel(q)
        ks = _kernel(ks)
        q = q / (jnp.linalg.norm(q, axis=-1, keepdims=True) + 1e-06)
        ks = ks / (jnp.linalg.norm(ks, axis=-1, keepdims=True) + 1e-06)
        scale = Nn ** (-0.5)
        ks = ks.astype(jnp.float32) * scale
        vs = vs.astype(jnp.float32) * scale
        states = jnp.einsum('kbhnd,kbhne->kbhde', ks, vs)
        state = jnp.prod(states, axis=0)
        out = jnp.einsum('bhnd,bhde->bhne', q.astype(jnp.float32), state)
        out = out.astype(dtype)
        out = out.transpose(0, 2, 1, 3).reshape(Bn, Nn, Cn)
        mu = out.mean(axis=-1, keepdims=True)
        var = out.var(axis=-1, keepdims=True)
        out = (out - mu) * jax.lax.rsqrt(var + 1e-05) * ln_g + ln_b
        out = out @ Wo.T + bo
        return out

    def _L0_ffn_ref(x, wqkv, q_scale, k_scale, wo, ln_g, ln_b, w1, b1, w2, b2):
        import jax, jax.numpy as jnp
        import numpy as np
        DIM = 128
        DEPTH = 2
        HEADS = 8
        DIM_HEAD = 64
        WINDOW = 64
        INNER = HEADS * DIM_HEAD
        HID = int(DIM * 4 * 2 / 3)
        B, N = (2, 1024)
        QK_SCALE = 8.0

        def shift_token(t):
            t1, t2 = jnp.split(t, 2, axis=-1)
            t2 = jnp.pad(t2, ((0, 0), (1, 0), (0, 0)))[:, :-1]
            return jnp.concatenate([t1, t2], axis=-1)

        def l2norm(t):
            return t / jnp.clip(jnp.linalg.norm(t, axis=-1, keepdims=True), 1e-12)

        def rotate_half(x):
            x1, x2 = jnp.split(x, 2, axis=-1)
            return jnp.concatenate([-x2, x1], axis=-1)

        def rotary_xpos(q, k):
            n = q.shape[-2]
            half_idx = jnp.arange(0, DIM_HEAD, 2, dtype=jnp.float32)
            inv_freq = 1.0 / 10000.0 ** (half_idx / DIM_HEAD)
            t = jnp.arange(n, dtype=jnp.float32)
            freqs = t[:, None] * inv_freq[None, :]
            freqs = jnp.concatenate([freqs, freqs], axis=-1)
            base = (half_idx + 0.4 * DIM_HEAD) / (1.4 * DIM_HEAD)
            power = (t - n // 2) / float(WINDOW // 2)
            scale = base[None, :] ** power[:, None]
            scale = jnp.concatenate([scale, scale], axis=-1)
            cos, sin = (jnp.cos(freqs), jnp.sin(freqs))
            q = q * cos * scale + rotate_half(q) * sin * scale
            k = k * cos / scale + rotate_half(k) * sin / scale
            return (q, k)

        def local_attention(q, k, v):
            b, h, n, d = q.shape
            w = n // WINDOW
            bq = q.reshape(b, h, w, WINDOW, d) * QK_SCALE
            bk = k.reshape(b, h, w, WINDOW, d)
            bv = v.reshape(b, h, w, WINDOW, d)

            def look_around(t):
                p = jnp.pad(t, ((0, 0), (0, 0), (1, 0), (0, 0), (0, 0)))
                return jnp.concatenate([p[:, :, :w], p[:, :, 1:]], axis=3)
            bk, bv = (look_around(bk), look_around(bv))
            bt = jnp.arange(n).reshape(w, WINDOW)
            btp = jnp.pad(bt, ((1, 0), (0, 0)), constant_values=-1)
            btk = jnp.concatenate([btp[:w], btp[1:]], axis=1)
            sim = jnp.einsum('bhwid,bhwjd->bhwij', bq, bk)
            i = bt[:, :, None]
            j = btk[:, None, :]
            mask = (i < j) | (i > j + WINDOW) | (j == -1)
            sim = jnp.where(mask, -jnp.finfo(sim.dtype).max, sim)
            attn = jax.nn.softmax(sim, axis=-1)
            out = jnp.einsum('bhwij,bhwjd->bhwid', attn, bv)
            return out.reshape(b, h, n, d)

        def _layer(x, wqkv, qs, ksc, wo, lg, lb, w1, b1, w2, b2):
            b, n, _ = x.shape
            h = shift_token(x)
            qkv = h @ wqkv
            q, k, v = jnp.split(qkv, 3, axis=-1)
            to_heads = lambda t: t.reshape(b, n, HEADS, DIM_HEAD).transpose(0, 2, 1, 3)
            q, k, v = (to_heads(q), to_heads(k), to_heads(v))
            q = l2norm(q) * qs
            k = l2norm(k) * ksc
            q, k = rotary_xpos(q, k)
            o = local_attention(q, k, v)
            o = o.transpose(0, 2, 1, 3).reshape(b, n, INNER)
            x = x + o @ wo
            h = shift_token(x)
            mu = h.mean(-1, keepdims=True)
            var = h.var(-1, keepdims=True)
            h = (h - mu) / jnp.sqrt(var + 1e-05) * lg + lb
            h = h @ w1 + b1
            a, g = jnp.split(h, 2, axis=-1)
            h = a * jax.nn.gelu(g, approximate=False)
            x = x + h @ w2 + b2
            return x
        for l in range(DEPTH):
            x = _layer(x, wqkv[l], q_scale[l], k_scale[l], wo[l], ln_g[l], ln_b[l], w1[l], b1[l], w2[l], b2[l])
        return x

    def _L1_attn_ref(x, w_q, w_k, w_v, w_o):
        import math
        import jax, jax.numpy as jnp
        import numpy as np
        B, T, C, H, DQK, DV = (2, 256, 128, 16, 64, 64)
        n, t, c = x.shape
        q = jnp.einsum('ntc,hdc->nhtd', x, w_q)
        k = jnp.einsum('ntc,hdc->nhtd', x, w_k)
        v = jnp.einsum('ntc,hdc->nhtd', x, w_v)
        scale = 1.0 / math.sqrt(w_q.shape[1])
        a = jnp.einsum('nhtd,nhsd->nhts', q, k) * scale
        causal = jnp.arange(t)[:, None] < jnp.arange(t)[None, :]
        a = jnp.where(causal[None, None, :, :], -jnp.inf, a)
        a = jax.nn.softmax(a, axis=3)
        y = jnp.einsum('nhts,nhsd->nthd', a, v).reshape(n, t, -1)
        return y @ w_o

    def _L1_ffn_ref(x, Wr, W1, W2):
        import jax, jax.numpy as jnp
        import numpy as np
        import math
        EMBED_DIM = 128
        FFN_DIM = 512
        N_EXPERTS = 8
        TOP_K = 2
        CAP_FACTOR = 1.25
        B, S, D = x.shape
        t = B * S
        xf = x.reshape(t, D)
        probs = jax.nn.softmax(xf.astype(jnp.float32) @ Wr, axis=-1)
        topk_probs, topk_experts = jax.lax.top_k(probs, TOP_K)
        cap = max(math.ceil(t * TOP_K * CAP_FACTOR / N_EXPERTS), 1)
        y = jnp.zeros_like(xf)
        for e in range(N_EXPERTS):
            mask = topk_experts == e
            gate = jnp.sum(jnp.where(mask, topk_probs, 0.0), axis=-1)
            has = jnp.any(mask, axis=-1)
            g_masked = jnp.where(has, gate, -jnp.inf)
            vals, idx = jax.lax.top_k(g_masked, cap)
            g = jnp.where(jnp.isfinite(vals), vals, 0.0)
            xe = xf[idx]
            h = jax.nn.relu(xe @ W1[e]) @ W2[e]
            y = y.at[idx].add(g[:, None] * h)
        return y.reshape(B, S, D)
    x = L0_attn_x
    x = _layernorm(x + _L0_attn_ref(x, L0_attn_Wq, L0_attn_bq, L0_attn_Wk, L0_attn_bk, L0_attn_Wv, L0_attn_bv, L0_attn_Wo, L0_attn_bo, L0_attn_ln_g, L0_attn_ln_b), axis=-1)
    x = _layernorm(x + _L0_ffn_ref(x, L0_ffn_wqkv, L0_ffn_q_scale, L0_ffn_k_scale, L0_ffn_wo, L0_ffn_ln_g, L0_ffn_ln_b, L0_ffn_w1, L0_ffn_b1, L0_ffn_w2, L0_ffn_b2), axis=-1)
    x = _layernorm(x + _L1_attn_ref(x, L1_attn_w_q, L1_attn_w_k, L1_attn_w_v, L1_attn_w_o), axis=-1)
    x = _layernorm(x + _L1_ffn_ref(x, L1_ffn_Wr, L1_ffn_W1, L1_ffn_W2), axis=-1)
    return x

_drawn_inputs = setup_inputs


def setup_inputs(seed=0):
    import zlib

    import numpy as np

    out = dict(_drawn_inputs(seed))
    spreads = {'L0_attn_bq': (0.0, 0.1),
     'L0_attn_bk': (0.0, 0.1),
     'L0_attn_bv': (0.0, 0.1),
     'L0_attn_bo': (0.0, 0.1),
     'L0_attn_ln_g': (1.0, 0.2),
     'L0_attn_ln_b': (0.0, 0.1),
     'L0_ffn_q_scale': (1.0, 0.6),
     'L0_ffn_k_scale': (1.0, 0.6),
     'L0_ffn_ln_g': (1.0, 0.6),
     'L0_ffn_ln_b': (0.0, 0.8),
     'L0_ffn_b1': (0.0, 0.8),
     'L0_ffn_b2': (0.0, 0.1)}
    factors = {'L0_ffn_w1': 5.551,
     'L0_ffn_w2': 5.266,
     'L1_ffn_Wr': 3.906,
     'L1_ffn_W1': 4.285,
     'L1_ffn_W2': 3.581}
    for name, (base, spread) in spreads.items():
        noise = np.random.default_rng([zlib.crc32(name.encode()), seed]).standard_normal(out[name].shape)
        drawn = base * np.exp(spread * noise) if base else spread * noise
        out[name] = jnp.asarray(drawn.astype(out[name].dtype))
    for name, factor in factors.items():
        out[name] = (out[name] * factor).astype(out[name].dtype)
    return out
```

```python
from contextlib import ExitStack

import concourse.bass as bass
from concourse import mybir

F32 = mybir.dt.float32
BF16 = mybir.dt.bfloat16
I32 = mybir.dt.int32
ACT = mybir.ActivationFunctionType
ALU = mybir.AluOpType
AX = mybir.AxisListType.X

P = 128
BANK = 512
C = 4
SEQ, TOK, DIM = 16, 256, 128
TILES = TOK // P
EPS = 1e-5
SILU_SET, LN_EXP_SET, GELU_SET = "silu_and_others", "natural_log_exp_and_others", "gelu_and_others"

LA_H, LA_D = 16, 8
LO_H, LO_D, LAYERS = 8, 64, 2
WINDOW = 64
HID = DIM * 4 * 2 // 3
HID_CUT = [(0, 128), (128, 128), (256, HID - 256)]
CA_H, CA_D = 16, 64
EXPERTS, FFN, CAP = 8, 512, 1280
BLK = 512
NBLK = SEQ * TOK // BLK
NT = SEQ * TILES


class Steps:

    def __init__(self, eng, sem, per_round):
        self.eng, self.sem, self.per, self.k = eng, sem, per_round, 0

    def at(self, rounds):
        self.before, self.k = rounds * self.per, 0

    def done(self, ins):
        ins.then_inc(self.sem, 1)
        self.k += 1
        assert self.k <= self.per, "more steps in a round than per_round says"
        return self.k

    def wait(self, place):
        self.eng.wait_ge(self.sem, self.before + place)

    def wait_alone(self, place):
        self.eng.wait_ge(self.sem, self.before + place)
        self.eng.sem_inc(self.sem, 1)
        self.k += 1

    def link(self, ins):
        self.wait(self.done(ins))

    def end(self):
        assert self.k == self.per, (self.sem, self.k, self.per)


def gate(eng, spare):
    eng.sem_inc(spare, 1)


def heads_wide(ap, width):
    return ap.unsqueeze(len(ap.shape)).broadcast_to(list(ap.shape) + [width])


def linear_attention(nc, M, dram):
    ctx = ExitStack()
    with ctx:
        sb = lambda name, shape, dt=F32: ctx.enter_context(nc.sbuf_tensor(name, shape, dt))
        sem = lambda name: ctx.enter_context(nc.semaphore(name))
        HALF = LA_H * 2 * LA_D
        x_tok = [sb(f"x_tok{u}", [P, TILES, DIM]) for u in range(2)]
        x_fea = [sb(f"x_fea{u}", [P, TOK]) for u in range(2)]
        kv = [sb(f"kv{u}", [P, TILES, 2 * HALF]) for u in range(2)]
        q = [sb(f"q{u}", [P, TOK]) for u in range(2)]
        k_sq = [sb(f"k_sq{u}", [P, TILES, HALF]) for u in range(2)]
        q_sq = [sb(f"q_sq{u}", [P, TOK]) for u in range(2)]
        norm = [sb(f"norm{u}", [P, TILES, 3 * LA_H]) for u in range(2)]
        inv = [sb(f"inv{u}", [P, TILES, 3 * LA_H]) for u in range(2)]
        state0 = [sb(f"state0{u}", [P, P]) for u in range(2)]
        state = [sb(f"state{u}", [P, P]) for u in range(2)]
        o = [sb(f"o{u}", [P, TILES, DIM]) for u in range(2)]
        on = [sb(f"on{u}", [P, TILES, DIM]) for u in range(2)]
        o_fea = [sb(f"o_fea{u}", [P, TOK]) for u in range(2)]
        r = [sb(f"r{u}", [P, TILES, DIM]) for u in range(2)]
        st = [sb(f"stats{u}", [P, TILES, 6]) for u in range(2)]
        mv = [sb(f"mv{u}", [P, TILES, 2]) for u in range(2)]
        lnv = [sb(f"lnv{u}", [P, TILES]) for u in range(2)]
        rstd = [sb(f"rstd{u}", [P, TILES]) for u in range(2)]

        x_loaded = [sem(f"a_x_loaded{u}") for u in range(2)]
        kv_made, q_made, kv_biased = sem("a_kv_made"), sem("a_q_made"), sem("a_kv_biased")
        k_silu, q_silu, halves = sem("a_k_silu"), sem("a_q_silu"), sem("a_halves_added")
        squares, q_norm2, k_norm2 = sem("a_squares"), sem("a_q_norm2"), sem("a_k_norm2")
        norms, k_scaled, states, state_ready = sem("a_norms"), sem("a_k_scaled"), sem("a_states"), sem("a_state_ready")
        out_made, o_var, o_rstd, o_normed = sem("a_out_made"), sem("a_o_var"), sem("a_o_rstd"), sem("a_o_normed")
        o_turned, o_fea_ready, f_made = sem("a_o_turned"), sem("a_o_fea_ready"), sem("a_f_made")
        r_var, r_rstd, x1_ready, x1_turned = sem("a_r_var"), sem("a_r_rstd"), sem("a_x1_ready"), sem("a_x1_turned")
        x1_stored, own_v, own_a = sem("a_x1_stored"), sem("a_vector_steps"), sem("a_scalar_steps")
        K0 = lambda u: 2 * u
        X = lambda u: 4 + u
        Y = lambda u: 6 + u
        bank = M.bank
        block = ctx.enter_context(nc.Block())

        @block.sync
        def _(sp):
            xf_v = dram["x_fea"].rearrange("c (s t) -> s c t", t=TOK)
            xt_v = dram["x"].rearrange("s (j p) c -> s p j c", p=P)
            with sp.Fori(0, SEQ // 2) as i:
                for u in range(2):
                    n = i * 2 + u
                    sp.wait_ge(x1_ready, C + n - 1)
                    sp.dma_start(x_fea[u][:, :], xf_v[n, :, :]).then_inc(x_loaded[u], 16)
                    sp.dma_start(x_tok[u][:, :, :], xt_v[n, :, :, :]).then_inc(x_loaded[u], 16)

        @block.gpsimd
        def _(pool):
            pool.sem_inc(squares, C)
            with pool.Fori(0, SEQ // 2) as i:
                for u in range(2):
                    n = i * 2 + u
                    pool.wait_ge(halves, C + 2 * n + 2)
                    nc.gpsimd.tensor_tensor(k_sq[u][:, :, :], kv[u][:, :, 0:HALF], kv[u][:, :, 0:HALF], ALU.mult).then_inc(squares, 1)
                    nc.gpsimd.tensor_tensor(q_sq[u][:, :], q[u][:, :], q[u][:, :], ALU.mult).then_inc(squares, 1)

        @block.tensor
        def _(pe):
            for s in (kv_made, q_made, q_norm2, states, out_made, o_turned, f_made, x1_turned):
                pe.sem_inc(s, C)
            pe.wait_ge(M.ready_a, M.READY_A)
            mm = nc.tensor.matmul
            with pe.Fori(0, SEQ // 2) as i:
                for u in range(2):
                    n = i * 2 + u
                    pe.wait_ge(x_loaded[u], i * 32 + 32)
                    pe.wait_ge(x1_stored, C + n - 1)
                    mm(bank(X(u))[:, 0:TOK], M.a_wq[:, :], x_fea[u][:, :], start=True, stop=True).then_inc(q_made, 1)
                    for j in range(TILES):
                        last = mm(bank(K0(u) + j), x_fea[u][:, j * P:(j + 1) * P], M.a_wkv[:, :], start=True, stop=True)
                    last.then_inc(kv_made, 1)
                for u in range(2):
                    n = i * 2 + u
                    pe.wait_ge(squares, C + 2 * n + 2)
                    for j in range(TILES):
                        last = mm(bank(Y(u))[:, j * LA_H:(j + 1) * LA_H], q_sq[u][:, j * P:(j + 1) * P], M.head_sum[:, :],
                                  start=True, stop=True)
                    last.then_inc(q_norm2, 1)
                for u in range(2):
                    n = i * 2 + u
                    pe.wait_ge(k_scaled, C + n + 1)
                    for k in range(2):
                        for j in range(TILES):
                            last = mm(bank(X(u))[:, k * P:(k + 1) * P], kv[u][:, j, k * P:(k + 1) * P],
                                      kv[u][:, j, HALF + k * P:HALF + (k + 1) * P], start=(j == 0), stop=(j == TILES - 1))
                    last.then_inc(states, 1)
                for u in range(2):
                    n = i * 2 + u
                    pe.wait_ge(state_ready, C + n + 1)
                    for j in range(TILES):
                        last = mm(bank(K0(u))[:, j * P:(j + 1) * P], q[u][:, j * P:(j + 1) * P], state[u][:, :], start=True, stop=True)
                    last.then_inc(out_made, 1)
                for u in range(2):
                    n = i * 2 + u
                    pe.wait_ge(o_normed, C + n + 1)
                    for j in range(TILES):
                        last = nc.tensor.transpose(bank(Y(u))[:, j * P:(j + 1) * P], on[u][:, j, :], M.ident[:, :])
                    last.then_inc(o_turned, 1)
                for u in range(2):
                    n = i * 2 + u
                    pe.wait_ge(o_fea_ready, C + n + 1)
                    for j in range(TILES):
                        last = mm(bank(K0(u) + 1)[:, j * P:(j + 1) * P], o_fea[u][:, j * P:(j + 1) * P], M.a_wo[:, :], start=True, stop=True)
                    last.then_inc(f_made, 1)
                for u in range(2):
                    n = i * 2 + u
                    pe.wait_ge(x1_ready, C + n + 1)
                    for j in range(TILES):
                        last = nc.tensor.transpose(bank(X(u))[:, j * P:(j + 1) * P], r[u][:, j, :], M.ident[:, :])
                    last.then_inc(x1_turned, 1)

        @block.scalar
        def _(act):
            for s in (k_silu, q_silu, norms, o_rstd, r_rstd, x1_stored):
                act.sem_inc(s, C)
            a = nc.scalar.activation
            own = Steps(act, own_a, 8)
            nc.scalar.preload_act_table_set(SILU_SET)

            def root(var, out_sem, n, u, ready):
                act.wait_ge(ready, C + n + 1)
                own.link(a(lnv[u][:, :], mv[u][:, :, 1], ACT.Ln, bias=M.eps[:, :]))
                a(rstd[u][:, :], lnv[u][:, :], ACT.Exp, scale=-0.5).then_inc(out_sem, 1)

            with act.Fori(0, SEQ // 2) as i:
                own.at(i)
                for u in range(2):
                    n = i * 2 + u
                    act.wait_ge(q_made, C + n + 1)
                    a(q[u][:, :], bank(X(u))[:, 0:TOK], ACT.Silu, bias=M.a_bq[:, :]).then_inc(q_silu, 1)
                    act.wait_ge(kv_biased, C + n + 1)
                    a(kv[u][:, :, 0:HALF], kv[u][:, :, 0:HALF], ACT.Silu).then_inc(k_silu, 1)
                nc.scalar.preload_act_table_set(LN_EXP_SET)
                for u in range(2):
                    n = i * 2 + u
                    act.wait_ge(k_norm2, C + n + 1)
                    act.wait_ge(q_norm2, C + n + 1)
                    first = own.done(a(norm[u][:, :, 0:2 * LA_H], norm[u][:, :, 0:2 * LA_H], ACT.Ln))
                    second = own.done(a(norm[u][:, :, 2 * LA_H:], bank(Y(u))[:, 0:TILES * LA_H].rearrange("p (j h) -> p j h", j=TILES), ACT.Ln))
                    own.wait(second)
                    a(norm[u][:, :, :], norm[u][:, :, :], ACT.Exp, scale=0.5).then_inc(norms, 1)
                for u in range(2):
                    root(mv, o_rstd, i * 2 + u, u, o_var)
                for u in range(2):
                    root(mv, r_rstd, i * 2 + u, u, r_var)
                for u in range(2):
                    n = i * 2 + u
                    act.wait_ge(x1_turned, C + n + 1)
                    a(M.xb[:, 0, bass.ts(n, TOK)], bank(X(u))[:, 0:TOK], ACT.Copy).then_inc(x1_stored, 1)
                own.end()

        @block.vector
        def _(dve):
            for s in (kv_biased, halves, k_norm2, k_scaled, state_ready, o_var, o_normed, o_fea_ready, r_var, x1_ready):
                dve.sem_inc(s, C)
            v = nc.vector
            own = Steps(dve, own_v, 26)

            def stats(src, u, sig):
                for j in range(TILES):
                    place = own.done(v.bn_stats(st[u][:, j, :], src[:, j, :]))
                own.wait_alone(place)
                v.bn_aggr(mv[u][:, 0, :], st[u][:, 0, :])
                v.bn_aggr(mv[u][:, 1, :], st[u][:, 1, :]).then_inc(sig, 1)

            def normed(out, src, u, sig):
                for j in range(TILES):
                    last = v.tensor_scalar(out[:, j, :], src[:, j, :], mv[u][:, j, 0:1], rstd[u][:, j:j + 1], ALU.subtract, ALU.mult)
                last.then_inc(sig, 1)

            with dve.Fori(0, SEQ // 2) as i:
                own.at(i)
                for u in range(2):
                    n = i * 2 + u
                    dve.wait_ge(kv_made, C + n + 1)
                    dve.wait_ge(states, C + n - 1)
                    v.tensor_tensor(kv[u][:, :, :], M.psum[:, K0(u):K0(u) + 2, :],
                                    M.a_bkv[:, :].unsqueeze(1).broadcast_to([P, 2, 2 * HALF]), ALU.add).then_inc(kv_biased, 1)
                for u in range(2):
                    n = i * 2 + u
                    dve.wait_ge(q_silu, C + n + 1)
                    v.tensor_scalar(q[u][:, :], q[u][:, :], 0.5, None, ALU.add).then_inc(halves, 1)
                    dve.wait_ge(k_silu, C + n + 1)
                    v.tensor_scalar(kv[u][:, :, 0:HALF], kv[u][:, :, 0:HALF], 0.5, None, ALU.add).then_inc(halves, 1)
                for u in range(2):
                    n = i * 2 + u
                    dve.wait_ge(squares, C + 2 * n + 1)
                    for j in range(TILES):
                        last = v.tensor_reduce(norm[u][:, j, 0:2 * LA_H], k_sq[u][:, j, :].rearrange("p (h d) -> p h d", d=LA_D), AX, ALU.add)
                    last.then_inc(k_norm2, 1)
                for u in range(2):
                    n = i * 2 + u
                    dve.wait_ge(norms, C + n + 1)
                    own.link(v.tensor_scalar(norm[u][:, :, :], norm[u][:, :, :], 1e-6, None, ALU.add))
                    own.link(v.reciprocal(inv[u][:, :, :], norm[u][:, :, :]))
                    for j in range(TILES):
                        k_v = kv[u][:, j, 0:HALF].rearrange("p (h d) -> p h d", d=LA_D)
                        last = v.tensor_tensor(k_v, k_v, heads_wide(inv[u][:, j, 0:2 * LA_H], LA_D), ALU.mult)
                    last.then_inc(k_scaled, 1)
                for u in range(2):
                    n = i * 2 + u
                    dve.wait_ge(states, C + n + 1)
                    own.link(v.tensor_tensor(state0[u][:, :], bank(X(u))[:, 0:P], M.state_mask[:, :], ALU.mult))
                    v.tensor_tensor(state[u][:, :], bank(X(u))[:, P:2 * P], state0[u][:, :], ALU.mult).then_inc(state_ready, 1)
                for u in range(2):
                    n = i * 2 + u
                    dve.wait_ge(out_made, C + n + 1)
                    for j in range(TILES):
                        place = own.done(v.tensor_tensor(o[u][:, j, :].rearrange("p (h d) -> p h d", d=LA_D),
                                                         bank(K0(u))[:, j * P:(j + 1) * P].rearrange("p (h d) -> p h d", d=LA_D),
                                                         heads_wide(inv[u][:, j, 2 * LA_H:], LA_D), ALU.mult))
                    own.wait(place)
                    stats(o[u], u, o_var)
                for u in range(2):
                    n = i * 2 + u
                    dve.wait_ge(o_rstd, C + n + 1)
                    normed(on[u], o[u], u, o_normed)
                for u in range(2):
                    n = i * 2 + u
                    dve.wait_ge(o_turned, C + n + 1)
                    v.tensor_scalar(o_fea[u][:, :], bank(Y(u))[:, 0:TOK], M.a_lng[:, :], M.a_lnb[:, :], ALU.mult, ALU.add).then_inc(o_fea_ready, 1)
                for u in range(2):
                    n = i * 2 + u
                    dve.wait_ge(f_made, C + n + 1)
                    own.link(v.tensor_tensor(r[u][:, :, :], bank(K0(u) + 1)[:, 0:TOK].rearrange("p (j c) -> p j c", j=TILES), x_tok[u][:, :, :], ALU.add))
                    own.link(v.tensor_tensor(r[u][:, :, :], r[u][:, :, :], M.a_bo[:, :].unsqueeze(1).broadcast_to([P, TILES, DIM]), ALU.add))
                    stats(r[u], u, r_var)
                for u in range(2):
                    n = i * 2 + u
                    dve.wait_ge(r_rstd, C + n + 1)
                    normed(r[u], r[u], u, x1_ready)
                own.end()


class Channel:

    def __init__(self, eng, filled, read):
        self.eng, self.filled, self.read = eng, filled, read

    def at(self, uses):
        self.uses = uses

    def filling(self):
        self.eng.wait_ge(self.read, C + self.uses)
        self.uses = self.uses + 1

    def reading(self):
        self.uses = self.uses + 1
        self.eng.wait_ge(self.filled, C + self.uses)


def over_sequences(eng, heads, lag, pre, head, tail, layer=0):
    def body(s, u, first=False, last=False):
        for h in range(heads + lag):
            head(layer, s, u, h, first, last)
            if not first:
                tail(layer, s - 1, 1 - u, h)
            if not last:
                pre(layer, s + 1, 1 - u, h, first)
        if not last:
            pre(layer, s + 1, 1 - u, None, first)
    for h in list(range(heads + lag)) + [None]:
        pre(layer, 0, 0, h, None)
    body(0, 0, first=True)
    with eng.Fori(0, SEQ // 2 - 1) as i:
        body(2 * i + 1, 1)
        body(2 * i + 2, 0)
    body(SEQ - 1, 1, last=True)
    for h in range(heads + lag):
        tail(layer, SEQ - 1, 1, h)


def local_transformer(nc, M, dram):
    ctx = ExitStack()
    with ctx:
        sb = lambda name, shape, dt=F32: ctx.enter_context(nc.sbuf_tensor(name, shape, dt))
        sem = lambda name: ctx.enter_context(nc.semaphore(name))
        INNER = LO_H * LO_D
        CH = INNER // P
        LAG = 2
        S1 = P + WINDOW
        PW = P + TOK
        tables = sb("b_tables", [P, LAYERS, 4, TILES, LO_D])
        table_scale = sb("b_table_scale", [P, LAYERS, 4, LO_D])
        h_fea = [sb(f"b_h{u}", [P, TOK]) for u in range(2)]
        sq = sb("b_sq", [P, 2 * INNER])
        ss = sb("b_ss", [P, 2 * LO_H])
        ln_ss = sb("b_ln_ss", [P, 2 * LO_H])
        root = sb("b_root", [P, 2 * LO_H])
        q_scale = [sb(f"b_q_scale{u}", [P, TILES, LO_H]) for u in range(2)]
        k_scale = sb("b_k_scale", [P, LO_H])
        k_unit = sb("b_k_unit", [P, INNER])
        rot_q = [sb(f"b_rot_q{j}", [P, 2, INNER]) for j in range(TILES)]
        rot_k = [sb(f"b_rot_k{j}", [P, 2, INNER]) for j in range(TILES)]
        v_tok = [sb(f"b_v{u}", [P, TILES, INNER]) for u in range(2)]
        q_fea = sb("b_q_fea", [P, CH, TOK])
        k_fea = sb("b_k_fea", [P, CH, TOK])
        mx = [sb(f"b_mx{p}", [P, TILES]) for p in range(2)]
        neg = [sb(f"b_neg{p}", [P, TILES]) for p in range(2)]
        prob = [sb(f"b_prob{p}", [P, PW]) for p in range(2)]
        prob_t = [sb(f"b_prob_t{p}", [P, PW]) for p in range(2)]
        row_sum = [sb(f"b_row_sum{u}", [P, TILES, LO_H]) for u in range(2)]
        inv_sum = sb("b_inv_sum", [P, TILES, LO_H])
        o = sb("b_o", [P, TILES, INNER])
        o_fea = sb("b_o_fea", [P, CH, TOK])
        h_ffn = [sb(f"b_hf{u}", [P, BLK]) for u in range(2)]
        c_sq = [sb(f"b_csq{u}", [P, BLK]) for u in range(2)]
        lnv = [sb(f"b_lnv{u}", [P, BLK]) for u in range(2)]
        rstd = [sb(f"b_rstd{u}", [P, BLK]) for u in range(2)]
        hn = sb("b_hn", [P, SEQ * TOK])
        gelu = [sb(f"b_gelu{k}", [P, BLK]) for k in range(3)]
        hid = [sb(f"b_hid{k}", [P, BLK]) for k in range(3)]
        wo, w1, w2, cols = M.b_wo, M.b_w1, M.b_w2, M.b_cols

        tables_ready, table_loaded = sem("b_tables_ready"), sem("b_table_loaded")
        h_ready, qk_made, v_made = sem("b_h_ready"), sem("b_qk_made"), sem("b_v_made")
        squared, summed, rooted, v_copied = sem("b_squared"), sem("b_summed"), sem("b_rooted"), sem("b_v_copied")
        k_unit_ready, q_rotated, k_rotated = sem("b_k_unit_ready"), sem("b_q_rotated"), sem("b_k_rotated")
        five_filled, five_read = sem("b_five_filled"), sem("b_five_read")
        two_filled, two_read = sem("b_two_filled"), sem("b_two_read")
        scored, neg_ready, exped, pv_made, scaled = sem("b_scored"), sem("b_neg_ready"), sem("b_exped"), sem("b_pv_made"), sem("b_scaled")
        own_squares, own_scale, own_max, own_inv, own_ln = (sem("b_own_" + s) for s in ("squares", "scale", "max", "inv", "ln"))
        spare = sem("b_spare")
        wo_loaded, ffn_loaded = sem("b_wo_loaded"), sem("b_ffn_loaded")
        hf_ready, centered, csquared, var_made, rstd_ready, hn_ready, own_var, own_hn = (sem("b_" + s) for s in (
            "hf_ready", "centered", "csquared", "var_made", "rstd_ready", "hn_ready", "own_var", "own_hn"))
        ag_made, gelued, hid_ready, y_made, ffn_written = (sem("b_" + s) for s in ("ag_made", "gelued", "hid_ready", "y_made", "ffn_written"))
        bank = M.bank
        block = ctx.enter_context(nc.Block())
        tile = lambda l, s, j: (l * SEQ + s) * TILES + j
        swapped = lambda ap: ap.rearrange("p (h t d) -> p h t d", t=2, d=LO_D // 2)[:, :, ::-1, :]
        by_head = lambda ap: ap.rearrange("p (h d) -> p h d", d=LO_D)

        def table(l, kind, j):
            return tables[:, l, kind, j, :].unsqueeze(1).broadcast_to([P, LO_H, LO_D])

        def table_half(l, kind, j, t):
            half = LO_D // 2
            return tables[:, l, kind, j, t * half:(t + 1) * half].unsqueeze(1).broadcast_to([P, LO_H, half])

        def half_heads(ap, t):
            return ap.rearrange("p (h t d) -> p t h d", t=2, d=LO_D // 2)[:, t, :, :]

        FIVE_USES, TWO_USES = SEQ * 7, SEQ * 8

        def five_before(l, s, first):
            return l * FIVE_USES + (2 if first else s * 7 + 1)

        def two_before(l, s, first):
            return l * TWO_USES + (2 if first else s * 8)

        @block.sync
        def _(sp):
            sp.dma_start(table_scale[:, :, :, :], dram["b_table_scale"].partition_broadcast(P)).then_inc(table_loaded, 16)
            with sp.Fori(0, LAYERS) as l:
                sp.wait_ge(two_read, C + l * TWO_USES)
                sp.dma_start(wo[:, :, :], dram["b_wo"][bass.ds(l, 1), :, :, :].rearrange("l p c n -> p (l c) n")).then_inc(wo_loaded, 16)
                sp.wait_ge(ffn_written, C + l * NBLK)
                sp.dma_start(w1[:, :], dram["b_w1"][bass.ds(l, 1), :, :].rearrange("l p n -> p (l n)")).then_inc(ffn_loaded, 16)
                sp.dma_start(w2[:, :, :], dram["b_w2"][bass.ds(l, 1), :, :, :].rearrange("l p c n -> p (l c) n")).then_inc(ffn_loaded, 16)
                sp.dma_start(cols[:, :], dram["b_cols"][bass.ds(l, 1), :, :].rearrange("l p n -> p (l n)")).then_inc(ffn_loaded, 16)

        @block.gpsimd
        def _(pool):
            for s in (h_ready, k_rotated, hf_ready):
                pool.sem_inc(s, C)
            for u in range(2):
                nc.gpsimd.memset(h_fea[u][:, :], 0.0).then_inc(tables_ready, 1)
                nc.gpsimd.memset(h_ffn[u][:, :], 0.0).then_inc(tables_ready, 1)
            pool.wait_ge(tables_ready, 5 + LAYERS)

            def pre(l, s, u, h, first):
                if h == 0:
                    pool.wait_ge(v_made, C + tile(l, s, 0) - 2)
                    pool.wait_ge(k_rotated, C + tile(l, s, 0))
                    gate(pool, spare)
                    nc.gpsimd.tensor_copy(h_fea[u][0:64, :], M.xb[0:64, l, bass.ts(s, TOK)]).then_inc(h_ready, 1)
                    pool.wait_ge(h_ready, C + 2 * (l * SEQ + s) + 1)
                    gate(pool, spare)
                    nc.gpsimd.tensor_copy(h_fea[u][64:P, 1:TOK], M.xb[64:P, l, bass.ds(s * TOK, TOK - 1)]).then_inc(h_ready, 1)
                if h in (2, 6):
                    j = h // 4
                    pool.wait_ge(k_unit_ready, C + tile(l, s, j) + 1)
                    if h == 2:
                        pool.wait_ge(h_ready, C + 2 * (l * SEQ + s) + 2)
                    if first is not None:
                        pool.wait_ge(two_filled, C + two_before(l, s - 1, first))
                    gate(pool, spare)
                    nc.gpsimd.tensor_tensor(by_head(rot_k[j][:, 0, :]), by_head(k_unit[:, :]), table(l, 2, j), ALU.mult)
                    for t in range(2):
                        last = nc.gpsimd.tensor_tensor(half_heads(rot_k[j][:, 1, :], t), half_heads(k_unit[:, :], 1 - t), table_half(l, 3, j, t), ALU.mult)
                    last.then_inc(k_rotated, 1)

            with pool.Fori(0, LAYERS) as l:
                pool.wait_ge(ffn_written, C + l * NBLK)
                pool.wait_ge(hf_ready, C + 2 * (l * NBLK))
                gate(pool, spare)
                over_sequences(pool, LO_H, LAG, pre, lambda *a: None, lambda *a: None, l)
                pool.wait_ge(two_read, C + l * TWO_USES + TWO_USES)
                gate(pool, spare)
                with pool.Fori(0, NBLK // 2) as i:
                    for u in range(2):
                        b = i * 2 + u
                        pool.wait_ge(centered, C + l * NBLK + b - 1)
                        pool.wait_ge(hf_ready, C + 2 * (l * NBLK + b))
                        gate(pool, spare)
                        nc.gpsimd.tensor_copy(h_ffn[u][0:64, :], M.xb[0:64, 1, bass.ts(b, BLK)]).then_inc(hf_ready, 1)
                        pool.wait_ge(hf_ready, C + 2 * (l * NBLK + b) + 1)
                        gate(pool, spare)
                        nc.gpsimd.tensor_copy(h_ffn[u][64:P, :].rearrange("p (s t) -> p s t", t=TOK)[:, :, 1:TOK],
                                              M.xb[64:P, 1, bass.ts(b, BLK)].rearrange("p (s t) -> p s t", t=TOK)[:, :, 0:TOK - 1]).then_inc(hf_ready, 1)

        @block.tensor
        def _(pe):
            for s in (qk_made, v_made, five_filled, two_filled, scored, pv_made, centered, var_made, ag_made, y_made):
                pe.sem_inc(s, C)
            mm = nc.tensor.matmul
            five, two = Channel(pe, five_filled, five_read), Channel(pe, two_filled, two_read)
            pe.wait_ge(M.loaded_b, M.LOADED_B)
            turned_at = [None]

            def pre(l, s, u, h, first):
                if first is None and h == 0:
                    five.at(l * FIVE_USES)
                    two.at(l * TWO_USES)
                if h in (0, 4):
                    j = h // 4
                    pe.wait_ge(h_ready, C + 2 * (l * SEQ + s) + 2)
                    pe.wait_ge(v_copied, C + tile(l, s, j))
                    pe.wait_ge(k_unit_ready, C + tile(l, s, j))
                    for part in range(2):
                        last = mm(bank(part), h_fea[u][:, j * P:(j + 1) * P], M.b_wqkv[:, l, part * INNER:(part + 1) * INNER], start=True, stop=True)
                    last.then_inc(qk_made, 1)
                if h in (3, 7):
                    j = h // 4
                    pe.wait_ge(q_rotated, C + tile(l, s, j) + 1)
                    mm(bank(0), h_fea[u][:, j * P:(j + 1) * P], M.b_wqkv[:, l, 2 * INNER:3 * INNER], start=True, stop=True).then_inc(v_made, 1)
                if h is None:
                    for j in range(TILES):
                        for src, ch, b, sig, made in ((rot_q[j], five, 5, five_filled, q_rotated), (rot_k[j], two, 2, two_filled, k_rotated)):
                            pe.wait_ge(made, C + tile(l, s, j) + 1)
                            ch.filling()
                            for c in range(CH):
                                for w in range(2):
                                    last = mm(bank(b)[:, c * P:(c + 1) * P], src[:, w, c * P:(c + 1) * P], M.ident[:, :], is_transpose=True,
                                              start=(w == 0), stop=(w == 1))
                            last.then_inc(sig, 1)

            def head(l, s, u, h, first, last_seq):
                if h == 0:
                    five.at(five_before(l, s, first))
                    two.at(two_before(l, s, first))
                    pe.wait_ge(five_read, C + five_before(l, s, first))
                    pe.wait_ge(two_read, C + two_before(l, s, first))
                n = l * SEQ + s
                if h < LO_H:
                    c, rows, b = h // 2, slice((h % 2) * LO_D, (h % 2 + 1) * LO_D), 3 + h % 2
                    pe.wait_ge(exped, C + n * LO_H + h - 1)
                    mm(bank(b)[:, 0:P], q_fea[rows, c, 0:P], k_fea[rows, c, 0:P], start=True, stop=False)
                    mm(bank(b)[:, 0:P], M.identb[:, :], M.mask_lo0[:, :], start=False, stop=True)
                    mm(bank(b)[:, P:P + S1], q_fea[rows, c, P:TOK], k_fea[rows, c, TOK - S1:TOK], start=True, stop=False)
                    mm(bank(b)[:, P:P + S1], M.identb[:, :], M.mask_lo1[:, :], start=False, stop=True).then_inc(scored, 1)
                g = h - 1
                if 0 <= g < LO_H:
                    pe.wait_ge(exped, C + n * LO_H + g + 1)
                    ch, b, sig = (five, 5, five_filled) if g % 2 == 0 else (two, 2, two_filled)
                    ch.filling()
                    for t in range(3):
                        last = nc.tensor.transpose(bank(b)[:, t * P:(t + 1) * P], prob[g % 2][:, t * P:(t + 1) * P], M.ident[:, :])
                    last.then_inc(sig, 1)
                g = h - 2
                if 0 <= g < LO_H:
                    if g % 2 == 0:
                        pe.wait_ge(five_read, C + five.uses)
                    else:
                        pe.wait_ge(two_read, C + two.uses)
                    if g == 0:
                        pe.wait_ge(v_copied, C + tile(l, s, 1) + 1)
                        pe.wait_ge(scaled, C + n)
                    cut = slice(g * LO_D, (g + 1) * LO_D)
                    mm(bank(6)[:, cut], prob_t[g % 2][:, 0:P], v_tok[u][:, 0, cut], start=True, stop=True)
                    mm(bank(7)[:, cut], prob_t[g % 2][:, P:2 * P], v_tok[u][:, 0, cut], start=True, stop=False)
                    mm(bank(7)[:, cut], prob_t[g % 2][:, 2 * P:3 * P], v_tok[u][:, 1, cut], start=False, stop=True).then_inc(pv_made, 1)

            def tail(l, s, u, h):
                n = l * SEQ + s
                if h in (2, 3):
                    j = h - 2
                    ch, b, sig = (five, 5, five_filled) if j == 0 else (two, 2, two_filled)
                    pe.wait_ge(scaled, C + n + 1)
                    ch.filling()
                    for c in range(CH):
                        last = nc.tensor.transpose(bank(b)[:, c * P:(c + 1) * P], o[:, j, c * P:(c + 1) * P], M.ident[:, :])
                    last.then_inc(sig, 1)
                    if j == 0:
                        turned_at[0] = five.uses
                if h == 5:
                    pe.wait_ge(wo_loaded, l * 16 + 16)
                    pe.wait_ge(five_read, C + turned_at[0])
                    two.filling()
                    for c in range(CH):
                        last = mm(bank(2)[:, 0:TOK], wo[:, c, :], o_fea[:, c, :], start=(c == 0), stop=(c == CH - 1))
                    last.then_inc(two_filled, 1)

            with pe.Fori(0, LAYERS) as l:
                over_sequences(pe, LO_H, LAG, pre, head, tail, l)
                pe.wait_ge(two_read, C + l * TWO_USES + TWO_USES)
                gate(pe, spare)
                f0 = l * NBLK
                with pe.Fori(0, NBLK // 2) as i:
                    for u in range(2):
                        b = i * 2 + u
                        pe.wait_ge(hf_ready, C + 2 * (f0 + b) + 2)
                        pe.wait_ge(hn_ready, C + f0 + b - 1)
                        mm(bank(u), M.center[:, :], h_ffn[u][:, :], start=True, stop=True).then_inc(centered, 1)
                    for u in range(2):
                        b = i * 2 + u
                        pe.wait_ge(csquared, C + f0 + b + 1)
                        mm(bank(2 + u), M.mean[:, :], c_sq[u][:, :], start=True, stop=True).then_inc(var_made, 1)
                pe.wait_ge(hn_ready, C + f0 + NBLK)
                pe.wait_ge(ffn_loaded, l * 48 + 48)
                gate(pe, spare)
                with pe.Fori(0, NBLK) as b:
                    for k, (off, w) in enumerate(HID_CUT):
                        pe.wait_ge(hid_ready, C + 3 * (f0 + b) + k - 2)
                        mm(bank(2 * k)[0:w, :], w1[:, HID + off:HID + off + w], hn[:, bass.ts(b, BLK)], start=True, stop=True)
                        mm(bank(2 * k + 1)[0:w, :], w1[:, off:off + w], hn[:, bass.ts(b, BLK)], start=True, stop=True).then_inc(ag_made, 1)
                    pe.wait_ge(ffn_written, C + f0 + b)
                    for k, (off, w) in enumerate(HID_CUT):
                        pe.wait_ge(hid_ready, C + 3 * (f0 + b) + k + 1)
                        last = mm(bank(6), w2[0:w, k, :], hid[k][0:w, :], start=(k == 0), stop=(k == 2))
                    last.then_inc(y_made, 1)
                pe.wait_ge(ffn_written, C + f0 + NBLK)
                gate(pe, spare)

        @block.scalar
        def _(act):
            for s in (squared, rooted, v_copied, five_read, exped, csquared, rstd_ready, gelued):
                act.sem_inc(s, C)
            a = nc.scalar.activation
            five = Channel(act, five_filled, five_read)
            own, own_l = Steps(act, own_ln, 1), Steps(act, own_var, 1)
            act.wait_ge(tables_ready, 5 + LAYERS)

            def pre(l, s, u, h, first):
                if first is None and h == 0:
                    five.at(l * FIVE_USES)
                if h in (0, 4):
                    j = h // 4
                    act.wait_ge(qk_made, C + tile(l, s, j) + 1)
                    act.wait_ge(summed, C + tile(l, s, j))
                    a(sq[:, :].rearrange("p (b n) -> p b n", b=2), M.psum[:, 0:2, :], ACT.Square).then_inc(squared, 1)
                if h in (1, 5):
                    j = h // 4
                    own.at(tile(l, s, j))
                    act.wait_ge(summed, C + tile(l, s, j) + 1)
                    own.link(a(ln_ss[:, :], ss[:, :], ACT.Ln, scale=65536.0))
                    a(root[:, :], ln_ss[:, :], ACT.Exp, scale=-0.5).then_inc(rooted, 1)
                if h in (3, 7):
                    j = h // 4
                    act.wait_ge(v_made, C + tile(l, s, j) + 1)
                    if first is not None:
                        act.wait_ge(pv_made, C + (l * SEQ + s - 1) * LO_H)
                    a(v_tok[u][:, j, :], bank(0), ACT.Copy).then_inc(v_copied, 1)
                if h is None:
                    act.wait_ge(scored, C + (l * SEQ + s) * LO_H)
                    for j in range(TILES):
                        five.reading()
                        a(q_fea[:, :, j * P:(j + 1) * P], bank(5).rearrange("p (c n) -> p c n", c=CH), ACT.Copy).then_inc(five_read, 1)

            def head(l, s, u, h, first, last_seq):
                n = l * SEQ + s
                if h == 0:
                    five.at(five_before(l, s, first))
                if h < LO_H:
                    b = 3 + h % 2
                    act.wait_ge(neg_ready, C + n * LO_H + h + 1)
                    act.wait_ge(pv_made, C + n * LO_H + h - 2)
                    if h == 0:
                        act.wait_ge(scaled, C + n - 1)
                    a(prob[h % 2][:, 0:P], bank(b)[:, 0:P], ACT.Exp, bias=neg[h % 2][:, 0:1], scale=q_scale[u][:, 0, h:h + 1],
                      accum_out=row_sum[u][:, 0, h:h + 1])
                    a(prob[h % 2][:, PW - S1:PW], bank(b)[:, P:P + S1], ACT.Exp, bias=neg[h % 2][:, 1:2], scale=q_scale[u][:, 1, h:h + 1],
                      accum_out=row_sum[u][:, 1, h:h + 1]).then_inc(exped, 1)
                g = h - 1
                if 0 <= g < LO_H and g % 2 == 0:
                    five.reading()
                    act.wait_ge(pv_made, C + n * LO_H + g - 1)
                    a(prob_t[0][:, :], bank(5)[:, 0:PW], ACT.Copy).then_inc(five_read, 1)

            def tail(l, s, u, h):
                if h == 2:
                    five.reading()
                    act.wait_ge(two_filled, C + two_before(l, s, False) + 6)
                    a(o_fea[:, :, 0:P], bank(5).rearrange("p (c n) -> p c n", c=CH), ACT.Copy).then_inc(five_read, 1)

            with act.Fori(0, LAYERS) as l:
                nc.scalar.preload_act_table_set(LN_EXP_SET)
                over_sequences(act, LO_H, LAG, pre, head, tail, l)
                f0 = l * NBLK
                with act.Fori(0, NBLK // 2) as i:
                    for u in range(2):
                        b = i * 2 + u
                        act.wait_ge(centered, C + f0 + b + 1)
                        act.wait_ge(var_made, C + f0 + b - 1)
                        a(c_sq[u][:, :], bank(u), ACT.Square).then_inc(csquared, 1)
                    for u in range(2):
                        b = i * 2 + u
                        own_l.at(f0 + b)
                        act.wait_ge(var_made, C + f0 + b + 1)
                        act.wait_ge(hn_ready, C + f0 + b - 1)
                        own_l.link(a(lnv[u][:, :], bank(2 + u), ACT.Ln, bias=M.eps[:, :]))
                        a(rstd[u][:, :], lnv[u][:, :], ACT.Exp, scale=-0.5).then_inc(rstd_ready, 1)
                nc.scalar.preload_act_table_set(GELU_SET)
                act.wait_ge(ffn_loaded, l * 48 + 48)
                gate(act, spare)
                with act.Fori(0, NBLK) as b:
                    for k, (off, w) in enumerate(HID_CUT):
                        act.wait_ge(ag_made, C + 3 * (f0 + b) + k + 1)
                        act.wait_ge(hid_ready, C + 3 * (f0 + b) + k - 2)
                        a(gelu[k][0:w, :], bank(2 * k)[0:w, :], ACT.Gelu, bias=cols[0:w, 3 + k:4 + k]).then_inc(gelued, 1)

        @block.vector
        def _(dve):
            for s in (summed, k_unit_ready, q_rotated, two_read, neg_ready, scaled, hn_ready, hid_ready, ffn_written):
                dve.sem_inc(s, C)
            v = nc.vector
            for p in range(2):
                last = v.memset(prob[p][:, P:2 * P], 0.0)
            last.then_inc(tables_ready, 1)
            dve.wait_ge(table_loaded, 16)
            dve.wait_ge(M.loaded_b, M.LOADED_B)
            for l in range(LAYERS):
                v.tensor_tensor(tables[:, l, :, :, :], M.rotary[:, :, :, :], table_scale[:, l, :, :].unsqueeze(2).broadcast_to([P, 4, TILES, LO_D]),
                                ALU.mult).then_inc(tables_ready, 1)
            dve.wait_ge(tables_ready, 5 + LAYERS)
            two = Channel(dve, two_filled, two_read)
            own_s, own_k, own_m, own_i, own_h = (Steps(dve, s, 1) for s in (own_squares, own_scale, own_max, own_inv, own_hn))

            def pre(l, s, u, h, first):
                if first is None and h == 0:
                    two.at(l * TWO_USES)
                if h in (0, 4):
                    j = h // 4
                    own_s.at(tile(l, s, j))
                    dve.wait_ge(squared, C + tile(l, s, j) + 1)
                    own_s.link(v.tensor_reduce(ss[:, :], by_head(sq[:, :]), AX, ALU.add))
                    v.tensor_scalar(ss[:, :], ss[:, :], 1e-24, None, ALU.max).then_inc(summed, 1)
                if h in (2, 6):
                    j = h // 4
                    own_k.at(tile(l, s, j))
                    dve.wait_ge(rooted, C + tile(l, s, j) + 1)
                    v.tensor_scalar(q_scale[u][:, j, :], root[:, 0:LO_H], 256.0 * 8.0, None, ALU.mult)
                    own_k.link(v.tensor_scalar(k_scale[:, :], root[:, LO_H:], 256.0, None, ALU.mult))
                    dve.wait_ge(k_rotated, C + tile(l, s, j))
                    v.tensor_tensor(by_head(k_unit[:, :]), by_head(bank(1)), heads_wide(k_scale[:, :], LO_D), ALU.mult).then_inc(k_unit_ready, 1)
                    if first is not None:
                        dve.wait_ge(five_filled, C + five_before(l, s - 1, first))
                    v.tensor_tensor(by_head(rot_q[j][:, 0, :]), by_head(bank(0)), table(l, 0, j), ALU.mult)
                    for t in range(2):
                        last = v.tensor_tensor(half_heads(rot_q[j][:, 1, :], t), half_heads(bank(0), 1 - t), table_half(l, 1, j, t), ALU.mult)
                    last.then_inc(q_rotated, 1)
                if h is None:
                    dve.wait_ge(scored, C + (l * SEQ + s) * LO_H)
                    for j in range(TILES):
                        two.reading()
                        v.tensor_copy(k_fea[:, :, j * P:(j + 1) * P], bank(2).rearrange("p (c n) -> p c n", c=CH)).then_inc(two_read, 1)

            def head(l, s, u, h, first, last_seq):
                n = l * SEQ + s
                if h == 0:
                    two.at(two_before(l, s, first))
                if h < LO_H:
                    b = 3 + h % 2
                    own_m.at(n * LO_H + h)
                    dve.wait_ge(scored, C + n * LO_H + h + 1)
                    dve.wait_ge(exped, C + n * LO_H + h - 1)
                    v.tensor_reduce(mx[h % 2][:, 0:1], bank(b)[:, 0:P], AX, ALU.max)
                    own_m.link(v.tensor_reduce(mx[h % 2][:, 1:2], bank(b)[:, P:P + S1], AX, ALU.max))
                    v.scalar_tensor_tensor(neg[h % 2][:, :], mx[h % 2][:, :], -1.0, q_scale[u][:, :, h], ALU.mult, ALU.mult).then_inc(neg_ready, 1)
                g = h - 1
                if 0 <= g < LO_H and g % 2 == 1:
                    two.reading()
                    dve.wait_ge(pv_made, C + n * LO_H + g - 1)
                    v.tensor_copy(prob_t[1][:, :], bank(2)[:, 0:PW]).then_inc(two_read, 1)
                if h == LO_H + LAG - 1:
                    dve.wait_ge(exped, C + n * LO_H + LO_H)
                    own_i.at(n)
                    own_i.link(v.reciprocal(inv_sum[:, :, :], row_sum[u][:, :, :]))
                    dve.wait_ge(pv_made, C + n * LO_H + LO_H)
                    for j in range(TILES):
                        last = v.tensor_tensor(o[:, j, :].rearrange("p (h d) -> p h d", d=LO_D), bank(6 + j).rearrange("p (h d) -> p h d", d=LO_D),
                                               heads_wide(inv_sum[:, j, :], LO_D), ALU.mult)
                    last.then_inc(scaled, 1)

            def tail(l, s, u, h):
                n = l * SEQ + s
                if h == 3:
                    two.reading()
                    v.tensor_copy(o_fea[:, :, P:TOK], bank(2).rearrange("p (c n) -> p c n", c=CH)).then_inc(two_read, 1)
                if h == 5:
                    two.reading()
                    v.tensor_tensor(M.xb[:, 1, bass.ts(s, TOK)], bank(2)[:, 0:TOK], M.xb[:, l, bass.ts(s, TOK)], ALU.add).then_inc(two_read, 1)

            with dve.Fori(0, LAYERS) as l:
                over_sequences(dve, LO_H, LAG, pre, head, tail, l)
                f0 = l * NBLK
                dve.wait_ge(ffn_loaded, l * 48 + 48)
                gate(dve, spare)
                with dve.Fori(0, NBLK // 2) as i:
                    for u in range(2):
                        b = i * 2 + u
                        own_h.at(f0 + b)
                        dve.wait_ge(rstd_ready, C + f0 + b + 1)
                        own_h.link(v.scalar_tensor_tensor(hn[:, bass.ts(b, BLK)], bank(u), cols[:, 0:1], rstd[u][:, :], ALU.mult, ALU.mult))
                        v.tensor_scalar(hn[:, bass.ts(b, BLK)], hn[:, bass.ts(b, BLK)], cols[:, 1:2], None, ALU.add).then_inc(hn_ready, 1)
                with dve.Fori(0, NBLK) as b:
                    dve.wait_ge(y_made, C + f0 + b)
                    for k, (off, w) in enumerate(HID_CUT):
                        dve.wait_ge(gelued, C + 3 * (f0 + b) + k + 1)
                        v.scalar_tensor_tensor(hid[k][0:w, :], bank(2 * k + 1)[0:w, :], cols[0:w, 6 + k:7 + k], gelu[k][0:w, :],
                                               ALU.add, ALU.mult).then_inc(hid_ready, 1)
                    dve.wait_ge(y_made, C + f0 + b + 1)
                    v.scalar_tensor_tensor(M.xb[:, 1, bass.ts(b, BLK)], bank(6), cols[:, 2:3], M.xb[:, 1, bass.ts(b, BLK)],
                                           ALU.add, ALU.add).then_inc(ffn_written, 1)


def causal_attention(nc, M, dram):
    ctx = ExitStack()
    with ctx:
        sb = lambda name, shape, dt=F32: ctx.enter_context(nc.sbuf_tensor(name, shape, dt))
        sem = lambda name: ctx.enter_context(nc.semaphore(name))
        HC = CA_H // 2
        LAG = 2
        HALF = 8 * CA_D
        PW = P + TOK
        z = sb("c_z", [P, TOK])
        x2 = [sb(f"c_x2{u}", [P, TILES, DIM]) for u in range(2)]
        x2_fea = [sb(f"c_x2_fea{u}", [P, TOK]) for u in range(2)]
        v_tok = [sb(f"c_v{u}", [P, TILES, CA_H * CA_D]) for u in range(2)]
        qk = [sb(f"c_qk{p}", [P, 2, TOK]) for p in range(2)]
        neg = [sb(f"c_neg{p}", [P, TILES]) for p in range(2)]
        prob = [sb(f"c_prob{p}", [P, PW]) for p in range(2)]
        prob_t = [sb(f"c_prob_t{p}", [P, PW]) for p in range(2)]
        row_sum = [sb(f"c_row_sum{u}", [P, TILES, CA_H]) for u in range(2)]
        inv_sum = [sb(f"c_inv_sum{e}", [P, TILES, 8]) for e in range(2)]
        o = sb("c_o", [P, TILES, CA_H * CA_D])
        o_fea = sb("c_o_fea", [P, HC, TOK])
        r = sb("c_r", [P, TILES, DIM])
        x3 = sb("c_x3", [P, TILES, DIM])
        x3_fea = sb("c_x3_fea", [P, TOK])
        st, mv = [sb(f"c_st{k}", [P, TILES, 6]) for k in range(2)], [sb(f"c_mv{k}", [P, TILES, 2]) for k in range(2)]
        lnv, rstd = [sb(f"c_lnv{k}", [P, TILES]) for k in range(2)], [sb(f"c_rstd{k}", [P, TILES]) for k in range(2)]

        names = ("wq_scaled qk_made qk_read scored neg_ready exped even_made even_read odd_made odd_read pv_made scaled "
                 "z_ready z_turned z_var z_rstd x2_ready x2_turned x2_fea_ready v_made v_copied "
                 "o_turned o_read y_made r_var r_rstd x3_ready x3_turned x3_fea_ready routed logits_read stored "
                 "own_inv own_r own_st own_st2 own_ln own_ln2 spare").split()
        S = {}
        for name in names:
            S[name] = sem("c_" + name)
        bank = M.bank
        block = ctx.enter_context(nc.Block())

        def before_start(eng, names):
            for name in names.split():
                eng.sem_inc(S[name], C)

        @block.sync
        def _(sp):
            for dst, src in M.d_loads:
                sp.dma_start(dst, src).then_inc(M.loaded_d, 16)

        @block.gpsimd
        def _(pool):
            before_start(pool, "z_ready stored")

            def pre(l, s, u, h, first):
                if h == 9:
                    pool.wait_ge(S["z_turned"], C + s)
                    gate(pool, S["spare"])
                    nc.gpsimd.tensor_tensor(z[:, :], M.xb[:, 0, bass.ts(s, TOK)], M.xb[:, 1, bass.ts(s, TOK)], ALU.add).then_inc(S["z_ready"], 1)

            def tail(l, s, u, h):
                if h == 8:
                    pool.wait_ge(S["x3_ready"], C + s + 1)
                    pool.wait_ge(S["x3_fea_ready"], C + s + 1)
                    gate(pool, S["spare"])
                    nc.gpsimd.tensor_copy(M.xb[:, 1, bass.ts(s, TOK)], x3[:, :, :].rearrange("p j c -> p (j c)")).then_inc(S["stored"], 1)
                    nc.gpsimd.tensor_copy(M.xb[:, 0, bass.ts(s, TOK)], x3_fea[:, :]).then_inc(S["stored"], 1)

            over_sequences(pool, CA_H, LAG, pre, lambda *a: None, tail, 0)

        @block.tensor
        def _(pe):
            before_start(pe, "qk_made scored even_made odd_made pv_made z_turned x2_turned v_made o_turned y_made x3_turned routed")
            mm = nc.tensor.matmul
            pe.wait_ge(M.loaded_c, M.LOADED_C)
            pe.wait_ge(S["wq_scaled"], 1)

            def project(n, c, u):
                pe.wait_ge(S["qk_read"], C + n * HC + c)
                for part in range(2):
                    last = mm(bank(2)[:, part * TOK:(part + 1) * TOK], M.c_w[:, part, c * P:(c + 1) * P], x2_fea[u][:, :], start=True, stop=True)
                last.then_inc(S["qk_made"], 1)

            def pre(l, s, u, h, first):
                if h == 10:
                    pe.wait_ge(S["z_ready"], C + s + 1)
                    if first is not None:
                        pe.wait_ge(S["logits_read"], C + s - 1)
                        pe.wait_ge(S["v_copied"], C + 4 * s)
                    for j in range(TILES):
                        last = nc.tensor.transpose(bank(7)[:, j * P:(j + 1) * P], z[:, j * P:(j + 1) * P], M.ident[:, :])
                    last.then_inc(S["z_turned"], 1)
                if h == 14:
                    pe.wait_ge(S["x2_ready"], C + s + 1)
                    for j in range(TILES):
                        last = nc.tensor.transpose(bank(7)[:, j * P:(j + 1) * P], x2[u][:, j, :], M.ident[:, :])
                    last.then_inc(S["x2_turned"], 1)
                if h is None or h >= 15:
                    k = 3 if h is None else h - 15
                    if k == 0:
                        pe.wait_ge(S["x2_fea_ready"], C + s + 1)
                    j, e = k // 2, k % 2
                    pe.wait_ge(S["v_copied"], C + 4 * s + k)
                    mm(bank(7), x2_fea[u][:, j * P:(j + 1) * P], M.c_w[:, 2, e * HALF:(e + 1) * HALF], start=True, stop=True).then_inc(S["v_made"], 1)
                if h is None:
                    project(s, 0, u)

            def head(l, n, u, h, first, last_seq):
                if h < CA_H:
                    c, rows, b = h // 2, slice((h % 2) * CA_D, (h % 2 + 1) * CA_D), h % 2
                    q_f, k_f = qk[c % 2][rows, 0, :], qk[c % 2][rows, 1, :]
                    pe.wait_ge(S["exped"], C + n * CA_H + h - 1)
                    pe.wait_ge(S["qk_read"], C + n * HC + c + 1)
                    if h == 0:
                        pe.wait_ge(S["v_copied"], C + 4 * n + 4)
                    mm(bank(b)[:, 0:P], q_f[:, 0:P], k_f[:, 0:P], start=True, stop=False)
                    mm(bank(b)[:, 0:P], M.identb[:, :], M.mask_causal[:, :], start=False, stop=True)
                    mm(bank(b)[:, P:PW], q_f[:, P:TOK], k_f[:, :], start=True, stop=False, skip_group_check=True)
                    mm(bank(b)[:, 2 * P:PW], M.identb[:, :], M.mask_causal[:, :], start=False, stop=True, skip_group_check=True).then_inc(S["scored"], 1)
                    if h % 2 == 0 and c + 1 < HC:
                        project(n, c + 1, u)
                g = h - 1
                if 0 <= g < CA_H:
                    b, sig, read = (3, S["even_made"], S["even_read"]) if g % 2 == 0 else (4, S["odd_made"], S["odd_read"])
                    pe.wait_ge(S["exped"], C + n * CA_H + g + 1)
                    pe.wait_ge(read, C + n * HC + g // 2)
                    for t in range(3):
                        last = nc.tensor.transpose(bank(b)[:, t * P:(t + 1) * P], prob[g % 2][:, t * P:(t + 1) * P], M.ident[:, :])
                    last.then_inc(sig, 1)
                g = h - 2
                if 0 <= g < CA_H:
                    pe.wait_ge(S["even_read"] if g % 2 == 0 else S["odd_read"], C + n * HC + g // 2 + 1)
                    if g % 8 == 0:
                        pe.wait_ge(S["scaled"], C + 2 * n + g // 8)
                    cut, vc = slice((g % 8) * CA_D, (g % 8 + 1) * CA_D), slice(g * CA_D, (g + 1) * CA_D)
                    mm(bank(5)[:, cut], prob_t[g % 2][:, 0:P], v_tok[u][:, 0, vc], start=True, stop=True)
                    mm(bank(6)[:, cut], prob_t[g % 2][:, P:2 * P], v_tok[u][:, 0, vc], start=True, stop=False)
                    mm(bank(6)[:, cut], prob_t[g % 2][:, 2 * P:3 * P], v_tok[u][:, 1, vc], start=False, stop=True).then_inc(S["pv_made"], 1)

            def tail(l, s, u, h):
                if h < 4:
                    j, e = h // 2, h % 2
                    pe.wait_ge(S["scaled"], C + 2 * s + 2)
                    pe.wait_ge(S["o_read"], C + 4 * s + h)
                    if h == 0:
                        pe.wait_ge(S["logits_read"], C + s)
                    for c in range(4):
                        last = nc.tensor.transpose(bank(7)[:, c * P:(c + 1) * P], o[:, j, (4 * e + c) * P:(4 * e + c + 1) * P], M.ident[:, :])
                    last.then_inc(S["o_turned"], 1)
                if h == 4:
                    pe.wait_ge(S["o_read"], C + 4 * s + 4)
                    for j in range(TILES):
                        for c in range(HC):
                            last = mm(bank(7)[:, j * P:(j + 1) * P], o_fea[:, c, j * P:(j + 1) * P], M.c_wo[:, c, :], start=(c == 0), stop=(c == HC - 1))
                    last.then_inc(S["y_made"], 1)
                if h == 8:
                    pe.wait_ge(S["x3_ready"], C + s + 1)
                    for j in range(TILES):
                        last = nc.tensor.transpose(bank(7)[:, j * P:(j + 1) * P], x3[:, j, :], M.ident[:, :])
                    last.then_inc(S["x3_turned"], 1)
                if h == 9:
                    pe.wait_ge(S["x3_fea_ready"], C + s + 1)
                    for j in range(TILES):
                        last = mm(bank(7)[:, j * EXPERTS:(j + 1) * EXPERTS], x3_fea[:, j * P:(j + 1) * P], M.d_wr[:, :], start=True, stop=True)
                    last.then_inc(S["routed"], 1)

            over_sequences(pe, CA_H, LAG, pre, head, tail, 0)

        @block.scalar
        def _(act):
            before_start(act, "exped even_read z_rstd x2_fea_ready v_copied o_read r_rstd x3_fea_ready")
            a = nc.scalar.activation
            nc.scalar.preload_act_table_set(LN_EXP_SET)
            own = [Steps(act, S["own_ln"], 1), Steps(act, S["own_ln2"], 1)]

            def rsqrt(k, s, ready, sig):
                own[k].at(s)
                act.wait_ge(ready, C + s + 1)
                own[k].link(a(lnv[k][:, :], mv[k][:, :, 1], ACT.Ln, bias=M.eps[:, :]))
                a(rstd[k][:, :], lnv[k][:, :], ACT.Exp, scale=-0.5).then_inc(sig, 1)

            def pre(l, s, u, h, first):
                if h == 12:
                    rsqrt(0, s, S["z_var"], S["z_rstd"])
                if h == 14:
                    act.wait_ge(S["x2_turned"], C + s + 1)
                    a(x2_fea[u][:, :], bank(7)[:, 0:TOK], ACT.Copy).then_inc(S["x2_fea_ready"], 1)
                if h is None or h >= 15:
                    k = 3 if h is None else h - 15
                    j, e = k // 2, k % 2
                    act.wait_ge(S["v_made"], C + 4 * s + k + 1)
                    a(v_tok[u][:, j, e * HALF:(e + 1) * HALF], bank(7), ACT.Copy).then_inc(S["v_copied"], 1)

            def head(l, n, u, h, first, last_seq):
                if h < CA_H:
                    b = h % 2
                    act.wait_ge(S["neg_ready"], C + n * CA_H + h + 1)
                    act.wait_ge(S["pv_made"], C + n * CA_H + h - 2)
                    if h == 0:
                        act.wait_ge(S["scaled"], C + 2 * n - 2)
                    a(prob[b][:, 0:P], bank(b)[:, 0:P], ACT.Exp, bias=neg[b][:, 0:1], accum_out=row_sum[u][:, 0, h:h + 1])
                    a(prob[b][:, P:PW], bank(b)[:, P:PW], ACT.Exp, bias=neg[b][:, 1:2], accum_out=row_sum[u][:, 1, h:h + 1]).then_inc(S["exped"], 1)
                g = h - 1
                if 0 <= g < CA_H and g % 2 == 0:
                    act.wait_ge(S["even_made"], C + n * HC + g // 2 + 1)
                    act.wait_ge(S["pv_made"], C + n * CA_H + g - 1)
                    a(prob_t[0][:, :], bank(3)[:, 0:PW], ACT.Copy).then_inc(S["even_read"], 1)

            def tail(l, s, u, h):
                if h < 4:
                    j, e = h // 2, h % 2
                    act.wait_ge(S["o_turned"], C + 4 * s + h + 1)
                    if h == 0:
                        act.wait_ge(S["y_made"], C + s)
                    a(o_fea[:, 4 * e:4 * e + 4, j * P:(j + 1) * P], bank(7).rearrange("p (c n) -> p c n", c=4), ACT.Copy).then_inc(S["o_read"], 1)
                if h == 6:
                    rsqrt(1, s, S["r_var"], S["r_rstd"])
                if h == 8:
                    act.wait_ge(S["x3_turned"], C + s + 1)
                    act.wait_ge(S["stored"], C + 2 * s)
                    a(x3_fea[:, :], bank(7)[:, 0:TOK], ACT.Copy).then_inc(S["x3_fea_ready"], 1)

            over_sequences(act, CA_H, LAG, pre, head, tail, 0)

        @block.vector
        def _(dve):
            before_start(dve, "qk_read neg_ready odd_read scaled z_var x2_ready r_var x3_ready logits_read")
            v = nc.vector
            dve.wait_ge(M.loaded_c, M.LOADED_C)
            v.tensor_scalar(M.c_w[:, 0, :], M.c_w[:, 0, :], CA_D ** -0.5, None, ALU.mult).then_inc(S["wq_scaled"], 1)
            own_i, own_r = Steps(dve, S["own_inv"], 2), Steps(dve, S["own_r"], 1)
            own_s = [Steps(dve, S["own_st"], 3), Steps(dve, S["own_st2"], 3)]

            def stats(k, s, src, sig):
                own_s[k].at(s)
                for j in range(TILES):
                    place = own_s[k].done(v.bn_stats(st[k][:, j, :], src[:, j * P:(j + 1) * P]))
                own_s[k].wait_alone(place)
                v.bn_aggr(mv[k][:, 0, :], st[k][:, 0, :])
                v.bn_aggr(mv[k][:, 1, :], st[k][:, 1, :]).then_inc(sig, 1)

            def normed(k, out, src, sig):
                for j in range(TILES):
                    last = v.tensor_scalar(out[:, j, :], src[:, j * P:(j + 1) * P], mv[k][:, j, 0:1], rstd[k][:, j:j + 1], ALU.subtract, ALU.mult)
                last.then_inc(sig, 1)

            def take(n, c):
                dve.wait_ge(S["qk_made"], C + n * HC + c + 1)
                dve.wait_ge(S["scored"], C + n * CA_H + 2 * c - 2)
                v.tensor_copy(qk[c % 2][:, :, :], bank(2).rearrange("p (w t) -> p w t", w=2)).then_inc(S["qk_read"], 1)

            def pre(l, s, u, h, first):
                if h == 11:
                    dve.wait_ge(S["z_turned"], C + s + 1)
                    stats(0, s, bank(7), S["z_var"])
                if h == 13:
                    dve.wait_ge(S["z_rstd"], C + s + 1)
                    normed(0, x2[u], bank(7), S["x2_ready"])
                if h is None:
                    take(s, 0)

            def head(l, n, u, h, first, last_seq):
                if h in (10, CA_H + LAG - 1):
                    e = 0 if h == 10 else 1
                    own_i.at(n)
                    own_i.k = e
                    dve.wait_ge(S["exped"], C + n * CA_H + 8 * e + 8)
                    own_i.link(v.reciprocal(inv_sum[e][:, :, :], row_sum[u][:, :, 8 * e:8 * e + 8]))
                    dve.wait_ge(S["pv_made"], C + n * CA_H + 8 * e + 8)
                    dve.wait_ge(S["o_turned"], C + 4 * n)
                    for j in range(TILES):
                        last = v.tensor_tensor(o[:, j, e * HALF:(e + 1) * HALF].rearrange("p (h d) -> p h d", d=CA_D),
                                               bank(5 + j).rearrange("p (h d) -> p h d", d=CA_D), heads_wide(inv_sum[e][:, j, :], CA_D), ALU.mult)
                    last.then_inc(S["scaled"], 1)
                if h < CA_H:
                    b = h % 2
                    dve.wait_ge(S["scored"], C + n * CA_H + h + 1)
                    dve.wait_ge(S["exped"], C + n * CA_H + h - 1)
                    v.tensor_reduce(neg[b][:, 0:1], bank(b)[:, 0:P], AX, ALU.max, negate=True)
                    v.tensor_reduce(neg[b][:, 1:2], bank(b)[:, P:PW], AX, ALU.max, negate=True).then_inc(S["neg_ready"], 1)
                    if h % 2 == 0 and h // 2 + 1 < HC:
                        take(n, h // 2 + 1)
                g = h - 1
                if 0 <= g < CA_H and g % 2 == 1:
                    dve.wait_ge(S["odd_made"], C + n * HC + g // 2 + 1)
                    dve.wait_ge(S["pv_made"], C + n * CA_H + g - 1)
                    v.tensor_copy(prob_t[1][:, :], bank(4)[:, 0:PW]).then_inc(S["odd_read"], 1)

            def tail(l, s, u, h):
                if h == 5:
                    own_r.at(s)
                    dve.wait_ge(S["y_made"], C + s + 1)
                    own_r.link(v.tensor_tensor(r[:, :, :], bank(7)[:, 0:TOK].rearrange("p (j c) -> p j c", j=TILES), x2[u][:, :, :], ALU.add))
                    stats(1, s, r[:, :, :].rearrange("p j c -> p (j c)"), S["r_var"])
                if h == 7:
                    dve.wait_ge(S["r_rstd"], C + s + 1)
                    dve.wait_ge(S["stored"], C + 2 * s)
                    normed(1, x3, r[:, :, :].rearrange("p j c -> p (j c)"), S["x3_ready"])
                if h == 10:
                    dve.wait_ge(S["routed"], C + s + 1)
                    v.tensor_copy(M.logits[:, bass.ts(s, TILES), :], bank(7)[:, 0:TILES * EXPERTS].rearrange("p (j e) -> p j e", j=TILES)).then_inc(S["logits_read"], 1)

            over_sequences(dve, CA_H, LAG, pre, head, tail, 0)


def experts(nc, M, dram):
    ctx = ExitStack()
    with ctx:
        sb = lambda name, shape, dt=F32: ctx.enter_context(nc.sbuf_tensor(name, shape, dt))
        sem = lambda name: ctx.enter_context(nc.semaphore(name))
        KF = FFN // P
        TB = BLK // P
        TOP_BIT = 29
        wide = [P, NT, EXPERTS]
        row = lambda ap: ap.unsqueeze(2).broadcast_to(wide)
        col = lambda ap: ap.unsqueeze(1).broadcast_to(wide)
        by_expert = lambda ap: ap.rearrange("p t e -> p e t")
        t1 = [sb(f"d_row{k}", [P, NT]) for k in range(6)]
        prob, w_a, w_b = sb("d_prob", wide), sb("d_wa", wide), sb("d_wb", wide)
        first, second, gate_w = sb("d_first", wide), sb("d_second", wide), sb("d_gate", wide)
        order = sb("d_order", [P, EXPERTS])
        thr, cand, bit, take = (sb(f"d_{s}", [P, EXPERTS], I32) for s in ("thr", "cand", "bit", "take"))
        bit_f, count = sb("d_bit_f", [P, EXPERTS]), sb("d_count", [P, EXPERTS])
        room = sb("d_room", [P, EXPERTS])
        equal_b = sb("d_equal_b", wide, BF16)
        ones_b, before_b = sb("d_ones_b", [P, P], BF16), sb("d_before_b", [P, P], BF16)
        hid = [sb(f"d_hid{p}", [P, KF, BLK]) for p in range(2)]
        gates = sb("d_gates", wide)
        g_blk = [sb(f"d_g_blk{p}", [P, TB, EXPERTS]) for p in range(2)]
        acc = [sb(f"d_acc{p}", [P, TB, DIM]) for p in range(2)]
        res = [sb(f"d_res{p}", [P, TB, DIM]) for p in range(2)]
        st, mv = [sb(f"d_st{p}", [P, TB, 6]) for p in range(2)], [sb(f"d_mv{p}", [P, TB, 2]) for p in range(2)]
        lnv, rstd = [sb(f"d_lnv{p}", [P, TB]) for p in range(2)], [sb(f"d_rstd{p}", [P, TB]) for p in range(2)]

        STORE0 = 32
        names = ("shifted exped counted summed equal_ready ranked own h_made h_even h_odd y_made combined var rstd res_ready "
                 "own_ln own_st loop spare").split()
        S = {}
        for name in names:
            S[name] = sem("d_" + name)
        stored = [sem(f"d_stored{u}") for u in range(2)]
        bank = M.bank
        block = ctx.enter_context(nc.Block())

        @block.sync
        def _(sp):
            out_v = dram["out"].rearrange("(b s) (j p) c -> b p (s j) c", s=BLK // TOK, p=P)
            with sp.Fori(0, NBLK // 2) as i:
                for u in range(2):
                    b = i * 2 + u
                    sp.wait_ge(S["res_ready"], C + b + 1)
                    sp.dma_start(out_v[bass.ds(b, 1), :, :, :].rearrange("b p t c -> p (b t) c"), res[u][:, :, :]).then_inc(stored[u], 16)
            for u in range(2):
                sp.wait_ge(stored[u], STORE0 + NBLK // 2 * 16)

        @block.tensor
        def _(pe):
            mm = nc.tensor.matmul
            for s in (S["summed"], S["h_made"], S["y_made"]):
                pe.sem_inc(s, C)
            pe.wait_ge(M.loaded_d, M.LOADED_D)
            with pe.Fori(0, TOP_BIT + 1) as k:
                pe.wait_ge(S["counted"], C + k + 1)
                mm(bank(6)[:, 0:EXPERTS], M.ones[:, :], count[:, :], start=True, stop=True).then_inc(S["summed"], 1)
            pe.wait_ge(S["equal_ready"], 1)
            mm(bank(6)[:, 0:EXPERTS], M.ones[:, :], count[:, :], start=True, stop=True)
            flat = lambda ap: ap.rearrange("p t e -> p (t e)")
            mm(bank(7)[:, 0:NT * EXPERTS], before_b[:, :], flat(equal_b[:, :, :]), start=True, stop=False)
            for t in range(NT - 1):
                last = mm(bank(7)[:, (t + 1) * EXPERTS:NT * EXPERTS], ones_b[:, :],
                          equal_b[:, t, :].unsqueeze(1).broadcast_to([P, NT - 1 - t, EXPERTS]), start=False, stop=(t == NT - 2))
            last.then_inc(S["ranked"], 1)

            with pe.Fori(0, NBLK) as b:
                x_blk = M.xb[:, 0, bass.ts(b, BLK)]

                def up(e):
                    g = b * EXPERTS + e
                    for k in range(KF):
                        pe.wait_ge(S["h_even"] if k % 2 == 0 else S["h_odd"], C + 2 * (g - 1) + k // 2 + 1)
                        mm(bank(k), M.d_w1[:, e, k * P:(k + 1) * P], x_blk, start=True, stop=True).then_inc(S["h_made"], 1)

                def down(e):
                    g = b * EXPERTS + e
                    pe.wait_ge(S["h_even"], C + 2 * g + 2)
                    pe.wait_ge(S["h_odd"], C + 2 * g + 2)
                    pe.wait_ge(S["combined"], C + g - 1)
                    for t in range(TB):
                        for k in range(KF):
                            last = mm(bank(4 + e % 2)[:, t * P:(t + 1) * P], hid[e % 2][:, k, t * P:(t + 1) * P], M.d_w2[:, e, k, :],
                                      start=(k == 0), stop=(k == KF - 1))
                    last.then_inc(S["y_made"], 1)

                up(0)
                for e in range(1, EXPERTS):
                    up(e)
                    down(e - 1)
                down(EXPERTS - 1)

        @block.scalar
        def _(act):
            a = nc.scalar.activation
            nc.scalar.preload_act_table_set(LN_EXP_SET)
            act.sem_inc(S["h_even"], C)
            act.sem_inc(S["rstd"], C)
            act.wait_ge(S["shifted"], 1)
            a(w_b[:, :, :], w_a[:, :, :], ACT.Exp).then_inc(S["exped"], 1)
            own = Steps(act, S["own_ln"], 1)
            with act.Fori(0, NBLK // 2) as i:
                for u in range(2):
                    b = i * 2 + u
                    for e in range(EXPERTS):
                        g = b * EXPERTS + e
                        act.wait_ge(S["y_made"], C + g - 1)
                        for k in (0, 2):
                            act.wait_ge(S["h_made"], C + KF * g + k + 1)
                            a(hid[e % 2][:, k, :], bank(k), ACT.Relu).then_inc(S["h_even"], 1)
                    own.at(b)
                    act.wait_ge(S["var"], C + b + 1)
                    own.link(a(lnv[u][:, :], mv[u][:, :, 1], ACT.Ln, bias=M.eps[:, :]))
                    a(rstd[u][:, :], lnv[u][:, :], ACT.Exp, scale=-0.5).then_inc(S["rstd"], 1)

        @block.vector
        def _(dve):
            v = nc.vector
            for s in (S["counted"], S["h_odd"], S["combined"], S["var"], S["res_ready"]):
                dve.sem_inc(s, C)
            for u in range(2):
                dve.sem_inc(stored[u], STORE0)
            own = Steps(dve, S["own"], 1000)
            own.at(0)
            own.link(v.tensor_reduce(t1[0][:, :], M.logits[:, :, :], AX, ALU.max))
            v.tensor_tensor(w_a[:, :, :], M.logits[:, :, :], row(t1[0][:, :]), ALU.subtract).then_inc(S["shifted"], 1)
            for e in range(EXPERTS):
                own.done(v.memset(order[:, e:e + 1], float(EXPERTS - e)))
            own.done(v.memset(thr[:, :], 0))
            own.done(v.memset(bit[:, :], 1 << TOP_BIT))
            own.done(v.memset(bit_f[:, :], float(1 << TOP_BIT)))
            dve.wait_ge(M.loaded_d, M.LOADED_D)
            own.done(v.tensor_copy(ones_b[:, :], M.ones[:, :]))
            own.done(v.tensor_copy(before_b[:, :], M.before[:, :]))
            dve.wait_ge(S["exped"], 1)
            own.link(v.tensor_reduce(t1[1][:, :], w_b[:, :, :], AX, ALU.add))
            own.link(v.reciprocal(t1[2][:, :], t1[1][:, :]))
            own.link(v.tensor_tensor(prob[:, :, :], w_b[:, :, :], row(t1[2][:, :]), ALU.mult))

            def pick(out, src, k):
                own.link(v.tensor_reduce(t1[k][:, :], src, AX, ALU.max))
                own.link(v.tensor_tensor(w_a[:, :, :], src, row(t1[k][:, :]), ALU.is_equal))
                own.link(v.tensor_tensor(w_a[:, :, :], w_a[:, :, :], col(order[:, :]), ALU.mult))
                own.link(v.tensor_reduce(t1[k + 1][:, :], w_a[:, :, :], AX, ALU.max))
                own.link(v.tensor_tensor(out, w_a[:, :, :], row(t1[k + 1][:, :]), ALU.is_equal))

            pick(first[:, :, :], prob[:, :, :], 2)
            own.link(v.scalar_tensor_tensor(w_b[:, :, :], first[:, :, :], -2.0, prob[:, :, :], ALU.mult, ALU.add))
            pick(second[:, :, :], w_b[:, :, :], 4)
            own.link(v.tensor_tensor(first[:, :, :], first[:, :, :], second[:, :, :], ALU.add))
            own.link(v.tensor_tensor(gate_w[:, :, :], prob[:, :, :], first[:, :, :], ALU.mult))

            loop = Steps(dve, S["loop"], 4)
            with dve.Fori(0, TOP_BIT + 1) as k:
                loop.at(k)
                loop.link(v.tensor_tensor(cand[:, :], thr[:, :], bit[:, :], ALU.bitwise_or))
                loop.link(v.tensor_tensor(w_a[:, :, :], gate_w[:, :, :], col(cand[:, :].bitcast(F32)), ALU.is_ge))
                v.tensor_reduce(count[:, :], by_expert(w_a[:, :, :]), AX, ALU.add).then_inc(S["counted"], 1)
                dve.wait_ge(S["summed"], C + k + 1)
                v.tensor_single_scalar(bit[:, :], bit[:, :], 1, ALU.logical_shift_right)
                loop.link(v.scalar_tensor_tensor(take[:, :], bank(6)[:, 0:EXPERTS], float(CAP), bit_f[:, :], ALU.is_ge, ALU.mult))
                v.tensor_scalar(bit_f[:, :], bit_f[:, :], 0.5, None, ALU.mult)
                loop.link(v.tensor_tensor(thr[:, :], thr[:, :], take[:, :], ALU.bitwise_or))
            thr_f = col(thr[:, :].bitcast(F32))
            own.link(v.tensor_tensor(w_a[:, :, :], gate_w[:, :, :], thr_f, ALU.is_gt))
            own.link(v.tensor_reduce(count[:, :], by_expert(w_a[:, :, :]), AX, ALU.add))
            v.tensor_tensor(equal_b[:, :, :], gate_w[:, :, :], thr_f, ALU.is_equal).then_inc(S["equal_ready"], 1)
            dve.wait_ge(S["ranked"], 1)
            own.link(v.tensor_scalar(room[:, :], bank(6)[:, 0:EXPERTS], -1.0, float(CAP), ALU.mult, ALU.add))
            own.link(v.tensor_tensor(w_b[:, :, :], bank(7)[:, 0:NT * EXPERTS].rearrange("p (t e) -> p t e", e=EXPERTS), col(room[:, :]), ALU.is_lt))
            own.link(v.tensor_tensor(w_b[:, :, :], w_b[:, :, :], equal_b[:, :, :], ALU.mult))
            own.link(v.tensor_tensor(w_b[:, :, :], w_b[:, :, :], w_a[:, :, :], ALU.add))
            own.link(v.tensor_tensor(gates[:, :, :], gate_w[:, :, :], w_b[:, :, :], ALU.mult))

            own_s = Steps(dve, S["own_st"], TB + 2)
            with dve.Fori(0, NBLK // 2) as i:
                for u in range(2):
                    b = i * 2 + u
                    own_s.at(b)
                    place = own_s.done(v.tensor_copy(g_blk[u][:, :, :], gates[:, bass.ts(b, TB), :]))

                    def combine(e, place):
                        g = b * EXPERTS + e
                        dve.wait_ge(S["y_made"], C + g + 1)
                        dve.wait_ge(S["combined"], C + g)
                        if e == 0:
                            own_s.wait(place)
                        for t in range(TB):
                            before = M.xb[:, 1, bass.ds(b * BLK + t * P, P)] if e == 0 else acc[(e + 1) % 2][:, t, :]
                            last = v.scalar_tensor_tensor(acc[e % 2][:, t, :], bank(4 + e % 2)[:, t * P:(t + 1) * P], g_blk[u][:, t, e:e + 1],
                                                          before, ALU.mult, ALU.add)
                        last.then_inc(S["combined"], 1)

                    for e in range(EXPERTS):
                        g = b * EXPERTS + e
                        dve.wait_ge(S["y_made"], C + g - 1)
                        for k in (1, 3):
                            dve.wait_ge(S["h_made"], C + KF * g + k + 1)
                            v.tensor_scalar(hid[e % 2][:, k, :], bank(k), 0.0, None, ALU.max).then_inc(S["h_odd"], 1)
                        if e:
                            combine(e - 1, place)
                    combine(EXPERTS - 1, place)
                    fin = acc[(EXPERTS - 1) % 2]
                    dve.wait_ge(S["combined"], C + b * EXPERTS + EXPERTS)
                    for t in range(TB):
                        place = own_s.done(v.bn_stats(st[u][:, t, :], fin[:, t, :]))
                    own_s.wait_alone(place)
                    for t in range(TB):
                        last = v.bn_aggr(mv[u][:, t, :], st[u][:, t, :])
                    last.then_inc(S["var"], 1)
                    dve.wait_ge(S["rstd"], C + b + 1)
                    dve.wait_ge(stored[u], STORE0 + 16 * i)
                    for t in range(TB):
                        last = v.tensor_scalar(res[u][:, t, :], fin[:, t, :], mv[u][:, t, 0:1], rstd[u][:, t:t + 1], ALU.subtract, ALU.mult)
                    last.then_inc(S["res_ready"], 1)


class Memory:
    pass


def program(nc, dram):
    ctx = ExitStack()
    with ctx:
        sb = lambda name, shape, dt=F32: ctx.enter_context(nc.sbuf_tensor(name, shape, dt))
        sem = lambda name: ctx.enter_context(nc.semaphore(name))
        M = Memory()
        M.psum = ctx.enter_context(nc.psum_tensor("banks", [P, 8, BANK], F32))
        M.bank = lambda b: M.psum[:, b, :]
        M.xb = sb("xb", [P, 2, SEQ * TOK])
        M.ident = sb("ident", [P, P])
        M.head_sum = sb("head_sum", [P, LA_H])
        M.state_mask = sb("state_mask", [P, P])
        M.eps = sb("eps", [P, 1])
        M.a_wkv = sb("a_wkv", [P, 4 * DIM])
        M.a_wq = sb("a_wq", [P, DIM])
        M.a_wo = sb("a_wo", [P, DIM])
        M.a_bkv = sb("a_bkv", [P, 4 * DIM])
        M.a_bo = sb("a_bo", [P, DIM])
        M.a_cols = sb("a_cols", [P, 3])
        M.a_bq, M.a_lng, M.a_lnb = (M.a_cols[:, k:k + 1] for k in range(3))
        M.masks = sb("masks", [P, 4 * P + WINDOW], BF16)
        masks = sb("masks32", [P, 4 * P + WINDOW])
        cuts = [0, P, 2 * P + WINDOW, 3 * P + WINDOW, 4 * P + WINDOW]
        M.mask_lo0, M.mask_lo1, M.mask_causal, M.identb = (M.masks[:, a:b] for a, b in zip(cuts, cuts[1:]))
        M.center, M.mean = sb("center", [P, P]), sb("mean", [P, P])
        M.rotary = sb("rotary", [P, 4, TILES, LO_D])
        M.b_wqkv = sb("b_wqkv", [P, LAYERS, 3 * LO_H * LO_D])
        M.b_wo = sb("b_wo", [P, LO_H * LO_D // P, DIM])
        M.b_w1 = sb("b_w1", [P, 2 * HID])
        M.b_w2 = sb("b_w2", [P, 3, DIM])
        M.b_cols = sb("b_cols", [P, 9])
        M.loaded_b, M.LOADED_B = sem("loaded_b"), 4 * 16
        M.c_w = sb("c_w", [P, 3, CA_H * CA_D])
        M.c_wo = sb("c_wo", [P, CA_H * CA_D // P, DIM])
        M.d_wr = sb("d_wr", [P, EXPERTS])
        M.ones = sb("ones", [P, P])
        M.before = sb("before", [P, P])
        M.logits = sb("logits", [P, NT, EXPERTS])
        M.loaded_c, M.LOADED_C = sem("loaded_c"), 4 * 16
        loaded_a, M.ready_a = sem("loaded_a"), sem("ready_a")
        M.READY_A = 4
        block = nc.Block()
        with block:
            @block.sync
            def _(sp):
                for dst, src in ((M.a_wkv[:, :], dram["a_wkv"]), (M.a_wq[:, :], dram["a_wq"]), (M.ident[:, :], dram["ident"]),
                                 (M.a_wo[:, :], dram["a_wo"]), (M.head_sum[:, :], dram["head_sum"]),
                                 (M.state_mask[:, :], dram["state_mask"]), (M.a_cols[:, :], dram["a_cols"]),
                                 (masks[:, :], dram["masks"]), (M.a_bkv[:, :], dram["a_bkv"].partition_broadcast(P)), (M.a_bo[:, :], dram["a_bo"].partition_broadcast(P))):
                    sp.dma_start(dst, src).then_inc(loaded_a, 16)
                for dst, src in ((M.b_wqkv[:, :, :], dram["b_wqkv"]), (M.rotary[:, :, :, :], dram["rotary"]),
                                 (M.center[:, :], dram["center"]), (M.mean[:, :], dram["mean"])):
                    sp.dma_start(dst, src).then_inc(M.loaded_b, 16)
                for dst, src in ((M.c_w[:, :, :], dram["c_w"]), (M.c_wo[:, :, :], dram["c_wo"]), (M.d_wr[:, :], dram["d_wr"]), (M.before[:, :], dram["before"])):
                    sp.dma_start(dst, src).then_inc(M.loaded_c, 16)

            @block.vector
            def _(dve):
                nc.vector.memset(M.eps[:, :], EPS).then_inc(M.ready_a, 1)
                dve.wait_ge(loaded_a, 10 * 16)
                nc.vector.tensor_tensor(M.a_wkv[:, :].rearrange("p (k c) -> p k c", k=4), M.a_wkv[:, :].rearrange("p (k c) -> p k c", k=4),
                                        M.ident[:, :].unsqueeze(1).broadcast_to([P, 4, DIM]), ALU.add).then_inc(M.ready_a, 1)
                nc.vector.tensor_copy(M.masks[:, :], masks[:, :]).then_inc(M.ready_a, 1)
                nc.vector.tensor_tensor(M.a_wq[:, :], M.a_wq[:, :], M.ident[:, :], ALU.add).then_inc(M.ready_a, 1)
        linear_attention(nc, M, dram)
        local_transformer(nc, M, dram)
        M.d_w1, M.d_w2 = sb("d_w1", [P, EXPERTS, FFN]), sb("d_w2", [P, EXPERTS, FFN // P, DIM])
        M.loaded_d, M.LOADED_D = sem("loaded_d"), 3 * 16
        M.d_loads = ((M.ones[:, 0:P], dram["ones"]), (M.d_w1[:, :, :], dram["d_w1"]), (M.d_w2[:, :, :, :], dram["d_w2"]))
        causal_attention(nc, M, dram)
        experts(nc, M, dram)

def later_arrays(g, T):
    import numpy as np
    swap = lambda a: np.roll(a, LO_D // 2, -1)
    def by_cut(a, rows):
        out = np.zeros((len(a), P, 3) + a.shape[2:], a.dtype)
        for k, (off, w) in enumerate(HID_CUT):
            out[:, :w, k] = a[:, off:off + w]
        return out
    b1 = g["L0_ffn_b1"]
    cols = np.concatenate([g["L0_ffn_ln_g"][:, :, None], g["L0_ffn_ln_b"][:, :, None], g["L0_ffn_b2"][:, :, None],
                           by_cut(b1[:, HID:], 0), by_cut(b1[:, :HID], 0)], 2)
    qs, ks = g["L0_ffn_q_scale"], g["L0_ffn_k_scale"]
    chunked = lambda a: a.reshape(a.shape[:-2] + (-1, P, a.shape[-1])).swapaxes(-3, -2)
    return {
        "b_wqkv": g["L0_ffn_wqkv"].transpose(1, 0, 2),
        "b_table_scale": np.stack([qs, swap(qs), ks, swap(ks)], 1),
        "b_wo": chunked(g["L0_ffn_wo"]),
        "b_w1": g["L0_ffn_w1"],
        "b_w2": by_cut(g["L0_ffn_w2"], 0),
        "b_cols": cols,
        "c_w": np.stack([g[k].reshape(-1, DIM).T for k in ("L1_attn_w_q", "L1_attn_w_k", "L1_attn_w_v")], 1),
        "c_wo": chunked(g["L1_attn_w_o"]),
        "d_wr": g["L1_ffn_Wr"],
        "d_w1": g["L1_ffn_W1"].transpose(1, 0, 2),
        "d_w2": g["L1_ffn_W2"].reshape(EXPERTS, FFN // P, P, DIM).transpose(2, 0, 1, 3),
    }


def constants():
    import numpy as np
    d = np.arange(P)
    tri = lambda keep: np.where(keep, 0.0, -1e30).astype(np.float32)
    half = np.arange(0, LO_D, 2, dtype=np.float64)
    freq = np.arange(TOK)[:, None] * (1.0 / 10000.0 ** (half / LO_D))[None, :]
    base = (half + 0.4 * LO_D) / (1.4 * LO_D)
    scale = base[None, :] ** ((np.arange(TOK) - TOK // 2) / float(WINDOW // 2))[:, None]
    two = lambda a: np.concatenate([a, a], 1)
    sin = np.concatenate([-np.sin(freq), np.sin(freq)], 1)
    rotary = np.stack([two(np.cos(freq) * scale), sin * two(scale), two(np.cos(freq) / scale), sin / two(scale)], 1)
    rotary = rotary.reshape(TILES, P, 4, LO_D).transpose(1, 2, 0, 3)
    q_at, k_at = d[:, None], d[None, :]
    k_wide = np.arange(P + WINDOW)[None, :]
    return {
        "ident": np.eye(P, dtype=np.float32),
        "head_sum": (d[:, None] // LA_D == np.arange(LA_H)[None, :]).astype(np.float32),
        "state_mask": (d[:, None] // LA_D == d[None, :] // LA_D).astype(np.float32) / TOK ** 2,
        "rotary": rotary.astype(np.float32),
        "center": (np.eye(P) - 1.0 / P).astype(np.float32),
        "mean": np.full((P, P), 1.0 / P, np.float32),
        "ones": np.ones((P, P), np.float32),
        "before": (d[:, None] < d[None, :]).astype(np.float32),
        "masks": np.concatenate([tri((k_at <= q_at) & (k_at >= q_at - WINDOW)), tri((k_wide >= q_at) & (k_wide <= q_at + WINDOW)),
                                 tri(k_at <= q_at), np.eye(P, dtype=np.float32)], 1),
    }


def kernel(**inputs):
    import numpy as np
    import concourse.bacc as bacc
    from concourse.bass_utils import run_bass_kernel_spmd as run

    g = {k: np.asarray(v) for k, v in inputs.items()}
    x = g["L0_attn_x"]
    T = lambda a: np.ascontiguousarray(np.swapaxes(a, -1, -2))
    arrays = {
        "x": x,
        "x_fea": T(x.reshape(SEQ * TOK, DIM)),
        "a_wkv": np.concatenate([T(g["L0_attn_Wk"][0]), T(g["L0_attn_Wk"][1]), T(g["L0_attn_Wv"][0]), T(g["L0_attn_Wv"][1])], 1),
        "a_wq": T(g["L0_attn_Wq"]),
        "a_wo": T(g["L0_attn_Wo"]),
        "a_cols": np.stack([g["L0_attn_bq"], g["L0_attn_ln_g"], g["L0_attn_ln_b"]], 1),
        "a_bkv": np.concatenate([g["L0_attn_bk"].reshape(-1), g["L0_attn_bv"].reshape(-1)]),
        "a_bo": g["L0_attn_bo"],
    }
    arrays.update(constants())
    arrays.update(later_arrays(g, T))
    arrays = {k: np.ascontiguousarray(v) for k, v in arrays.items()}
    nc = bacc.Bacc("TRN2", target_bir_lowering=False, num_devices=1)
    dram = {}
    for name, a in arrays.items():
        dram[name] = nc.dram_tensor("in_" + name, a.shape, mybir.dt.from_np(a.dtype), kind="ExternalInput").ap()
    dram["out"] = nc.dram_tensor("out_x", x.shape, F32, kind="ExternalOutput").ap()
    program(nc, dram)
    return run(nc, [{"in_" + k: a for k, a in arrays.items()}], core_ids=[0]).results[0]["out_x"]
```

```python
from contextlib import ExitStack

import concourse.bass as bass
from concourse import mybir

F32 = mybir.dt.float32
F32R = mybir.dt.float32r
BF16 = mybir.dt.bfloat16
I32 = mybir.dt.int32
ACT = mybir.ActivationFunctionType
ALU = mybir.AluOpType
AX = mybir.AxisListType.X

P = 128
BANK = 512
C = 6
SEQ, TOK, DIM = 16, 256, 128
TILES = TOK // P
EPS = 1e-5
SILU_SET, LN_EXP_SET, GELU_SET = "silu_and_others", "natural_log_exp_and_others", "gelu_and_others"

LA_H, LA_D = 16, 8
LO_H, LO_D, LAYERS = 8, 64, 2
WINDOW = 64
HID = DIM * 4 * 2 // 3
HID_CUT = [(0, 128), (128, 128), (256, HID - 256)]
CA_H, CA_D = 16, 64
EXPERTS, FFN, CAP = 8, 512, 1280
BLK = 512
NBLK = SEQ * TOK // BLK
NT = SEQ * TILES


class Steps:

    def __init__(self, eng, sem, per_round):
        self.eng, self.sem, self.per, self.k = eng, sem, per_round, 0

    def at(self, rounds):
        self.before, self.k = rounds * self.per, 0

    def done(self, ins):
        ins.then_inc(self.sem, 1)
        self.k += 1
        assert self.k <= self.per, "more steps in a round than per_round says"
        return self.k

    def wait(self, place):
        self.eng.wait_ge(self.sem, self.before + place)

    def wait_alone(self, place):
        self.eng.wait_ge(self.sem, self.before + place)
        self.eng.sem_inc(self.sem, 1)
        self.k += 1

    def link(self, ins):
        self.wait(self.done(ins))

    def end(self):
        assert self.k == self.per, (self.sem, self.k, self.per)


def gate(eng, spare):
    eng.sem_inc(spare, 1)


def heads_wide(ap, width):
    return ap.unsqueeze(len(ap.shape)).broadcast_to(list(ap.shape) + [width])


def linear_attention(nc, M, dram):
    ctx = ExitStack()
    with ctx:
        sb = lambda name, shape, dt=F32: ctx.enter_context(nc.sbuf_tensor(name, shape, dt))
        sem = lambda name: ctx.enter_context(nc.semaphore(name))
        HALF = LA_H * 2 * LA_D
        x_tok = [sb(f"x_tok{u}", [P, TILES, DIM]) for u in range(2)]
        x_fea = [sb(f"x_fea{u}", [P, TOK]) for u in range(2)]
        kv = [sb(f"kv{u}", [P, TILES, 2 * HALF]) for u in range(2)]
        q = [sb(f"q{u}", [P, TOK]) for u in range(2)]
        k_sq = [sb(f"k_sq{u}", [P, TILES, HALF]) for u in range(2)]
        q_sq = [sb(f"q_sq{u}", [P, TOK]) for u in range(2)]
        norm = [sb(f"norm{u}", [P, TILES, 3 * LA_H]) for u in range(2)]
        inv = [sb(f"inv{u}", [P, TILES, 3 * LA_H]) for u in range(2)]
        state0 = [sb(f"state0{u}", [P, P]) for u in range(2)]
        state = [sb(f"state{u}", [P, P]) for u in range(2)]
        o = [sb(f"o{u}", [P, TILES, DIM]) for u in range(2)]
        on = [sb(f"on{u}", [P, TILES, DIM]) for u in range(2)]
        o_fea = [sb(f"o_fea{u}", [P, TOK]) for u in range(2)]
        r = [sb(f"r{u}", [P, TILES, DIM]) for u in range(2)]
        st = [sb(f"stats{u}", [P, TILES, 6]) for u in range(2)]
        mv = [sb(f"mv{u}", [P, TILES, 2]) for u in range(2)]
        lnv = [sb(f"lnv{u}", [P, TILES]) for u in range(2)]
        rstd = [sb(f"rstd{u}", [P, TILES]) for u in range(2)]

        x_loaded = [sem(f"a_x_loaded{u}") for u in range(2)]
        kv_made, q_made, kv_biased = sem("a_kv_made"), sem("a_q_made"), sem("a_kv_biased")
        k_silu, q_silu, halves = sem("a_k_silu"), sem("a_q_silu"), sem("a_halves_added")
        squares, q_norm2, k_norm2 = sem("a_squares"), sem("a_q_norm2"), sem("a_k_norm2")
        norms, k_scaled, states, state_ready = sem("a_norms"), sem("a_k_scaled"), sem("a_states"), sem("a_state_ready")
        out_made, o_var, o_rstd, o_normed = sem("a_out_made"), sem("a_o_var"), sem("a_o_rstd"), sem("a_o_normed")
        o_turned, o_fea_ready, f_made = sem("a_o_turned"), sem("a_o_fea_ready"), sem("a_f_made")
        r_var, r_rstd, x1_ready, x1_turned = sem("a_r_var"), sem("a_r_rstd"), sem("a_x1_ready"), sem("a_x1_turned")
        x1_stored, own_v, own_a = sem("a_x1_stored"), sem("a_vector_steps"), sem("a_scalar_steps")
        K0 = lambda u: 2 * u
        X = lambda u: 4 + u
        Y = lambda u: 6 + u
        bank = M.bank
        block = ctx.enter_context(nc.Block())

        @block.sync
        def _(sp):
            xf_v = dram["x_fea"].rearrange("c (s t) -> s c t", t=TOK)
            xt_v = dram["x"].rearrange("s (j p) c -> s p j c", p=P)
            with sp.Fori(0, SEQ // 2) as i:
                for u in range(2):
                    n = i * 2 + u
                    sp.wait_ge(x1_ready, C + n - 1)
                    sp.dma_start(x_fea[u][:, :], xf_v[n, :, :]).then_inc(x_loaded[u], 16)
                    sp.dma_start(x_tok[u][:, :, :], xt_v[n, :, :, :]).then_inc(x_loaded[u], 16)

        @block.gpsimd
        def _(pool):
            pool.sem_inc(squares, C)
            with pool.Fori(0, SEQ // 2) as i:
                for u in range(2):
                    n = i * 2 + u
                    pool.wait_ge(halves, C + 2 * n + 2)
                    nc.gpsimd.tensor_tensor(k_sq[u][:, :, :], kv[u][:, :, 0:HALF], kv[u][:, :, 0:HALF], ALU.mult).then_inc(squares, 1)
                    nc.gpsimd.tensor_tensor(q_sq[u][:, :], q[u][:, :], q[u][:, :], ALU.mult).then_inc(squares, 1)

        @block.tensor
        def _(pe):
            for s in (kv_made, q_made, q_norm2, states, out_made, o_turned, f_made, x1_turned):
                pe.sem_inc(s, C)
            pe.wait_ge(M.ready_a, M.READY_A)
            mm = nc.tensor.matmul
            with pe.Fori(0, SEQ // 2) as i:
                for u in range(2):
                    n = i * 2 + u
                    pe.wait_ge(x_loaded[u], i * 32 + 32)
                    pe.wait_ge(x1_stored, C + n - 1)
                    mm(bank(X(u))[:, 0:TOK], M.a_wq[:, :], x_fea[u][:, :], start=True, stop=True).then_inc(q_made, 1)
                    for j in range(TILES):
                        last = mm(bank(K0(u) + j), x_fea[u][:, j * P:(j + 1) * P], M.a_wkv[:, :], start=True, stop=True)
                    last.then_inc(kv_made, 1)
                for u in range(2):
                    n = i * 2 + u
                    pe.wait_ge(squares, C + 2 * n + 2)
                    for j in range(TILES):
                        last = mm(bank(Y(u))[:, j * LA_H:(j + 1) * LA_H], q_sq[u][:, j * P:(j + 1) * P], M.head_sum[:, :],
                                  start=True, stop=True)
                    last.then_inc(q_norm2, 1)
                for u in range(2):
                    n = i * 2 + u
                    pe.wait_ge(k_scaled, C + n + 1)
                    for k in range(2):
                        for j in range(TILES):
                            last = mm(bank(X(u))[:, k * P:(k + 1) * P], kv[u][:, j, k * P:(k + 1) * P],
                                      kv[u][:, j, HALF + k * P:HALF + (k + 1) * P], start=(j == 0), stop=(j == TILES - 1))
                    last.then_inc(states, 1)
                for u in range(2):
                    n = i * 2 + u
                    pe.wait_ge(state_ready, C + n + 1)
                    for j in range(TILES):
                        last = mm(bank(K0(u))[:, j * P:(j + 1) * P], q[u][:, j * P:(j + 1) * P], state[u][:, :], start=True, stop=True)
                    last.then_inc(out_made, 1)
                for u in range(2):
                    n = i * 2 + u
                    pe.wait_ge(o_normed, C + n + 1)
                    for j in range(TILES):
                        last = nc.tensor.transpose(bank(Y(u))[:, j * P:(j + 1) * P], on[u][:, j, :], M.ident[:, :])
                    last.then_inc(o_turned, 1)
                for u in range(2):
                    n = i * 2 + u
                    pe.wait_ge(o_fea_ready, C + n + 1)
                    for j in range(TILES):
                        last = mm(bank(K0(u) + 1)[:, j * P:(j + 1) * P], o_fea[u][:, j * P:(j + 1) * P], M.a_wo[:, :], start=True, stop=True)
                    last.then_inc(f_made, 1)
                for u in range(2):
                    n = i * 2 + u
                    pe.wait_ge(x1_ready, C + n + 1)
                    for j in range(TILES):
                        last = nc.tensor.transpose(bank(X(u))[:, j * P:(j + 1) * P], r[u][:, j, :], M.ident[:, :])
                    last.then_inc(x1_turned, 1)

        @block.scalar
        def _(act):
            for s in (k_silu, q_silu, norms, o_rstd, r_rstd, x1_stored):
                act.sem_inc(s, C)
            a = nc.scalar.activation
            own = Steps(act, own_a, 8)
            nc.scalar.preload_act_table_set(SILU_SET)

            def root(var, out_sem, n, u, ready):
                act.wait_ge(ready, C + n + 1)
                own.link(a(lnv[u][:, :], mv[u][:, :, 1], ACT.Ln, bias=M.eps[:, :]))
                a(rstd[u][:, :], lnv[u][:, :], ACT.Exp, scale=-0.5).then_inc(out_sem, 1)

            with act.Fori(0, SEQ // 2) as i:
                own.at(i)
                for u in range(2):
                    n = i * 2 + u
                    act.wait_ge(q_made, C + n + 1)
                    a(q[u][:, :], bank(X(u))[:, 0:TOK], ACT.Silu, bias=M.a_bq[:, :]).then_inc(q_silu, 1)
                    act.wait_ge(kv_biased, C + n + 1)
                    a(kv[u][:, :, 0:HALF], kv[u][:, :, 0:HALF], ACT.Silu).then_inc(k_silu, 1)
                nc.scalar.preload_act_table_set(LN_EXP_SET)
                for u in range(2):
                    n = i * 2 + u
                    act.wait_ge(k_norm2, C + n + 1)
                    act.wait_ge(q_norm2, C + n + 1)
                    first = own.done(a(norm[u][:, :, 0:2 * LA_H], norm[u][:, :, 0:2 * LA_H], ACT.Ln))
                    second = own.done(a(norm[u][:, :, 2 * LA_H:], bank(Y(u))[:, 0:TILES * LA_H].rearrange("p (j h) -> p j h", j=TILES), ACT.Ln))
                    own.wait(second)
                    a(norm[u][:, :, :], norm[u][:, :, :], ACT.Exp, scale=0.5).then_inc(norms, 1)
                for u in range(2):
                    root(mv, o_rstd, i * 2 + u, u, o_var)
                for u in range(2):
                    root(mv, r_rstd, i * 2 + u, u, r_var)
                for u in range(2):
                    n = i * 2 + u
                    act.wait_ge(x1_turned, C + n + 1)
                    a(M.xb[:, 0, bass.ts(n, TOK)], bank(X(u))[:, 0:TOK], ACT.Copy).then_inc(x1_stored, 1)
                own.end()

        @block.vector
        def _(dve):
            for s in (kv_biased, halves, k_norm2, k_scaled, state_ready, o_var, o_normed, o_fea_ready, r_var, x1_ready):
                dve.sem_inc(s, C)
            v = nc.vector
            own = Steps(dve, own_v, 26)

            def stats(src, u, sig):
                for j in range(TILES):
                    place = own.done(v.bn_stats(st[u][:, j, :], src[:, j, :]))
                own.wait_alone(place)
                v.bn_aggr(mv[u][:, 0, :], st[u][:, 0, :])
                v.bn_aggr(mv[u][:, 1, :], st[u][:, 1, :]).then_inc(sig, 1)

            def normed(out, src, u, sig):
                for j in range(TILES):
                    last = v.tensor_scalar(out[:, j, :], src[:, j, :], mv[u][:, j, 0:1], rstd[u][:, j:j + 1], ALU.subtract, ALU.mult)
                last.then_inc(sig, 1)

            with dve.Fori(0, SEQ // 2) as i:
                own.at(i)
                for u in range(2):
                    n = i * 2 + u
                    dve.wait_ge(kv_made, C + n + 1)
                    dve.wait_ge(states, C + n - 1)
                    v.tensor_tensor(kv[u][:, :, :], M.psum[:, K0(u):K0(u) + 2, :],
                                    M.a_bkv[:, :].unsqueeze(1).broadcast_to([P, 2, 2 * HALF]), ALU.add).then_inc(kv_biased, 1)
                for u in range(2):
                    n = i * 2 + u
                    dve.wait_ge(q_silu, C + n + 1)
                    v.tensor_scalar(q[u][:, :], q[u][:, :], 0.5, None, ALU.add).then_inc(halves, 1)
                    dve.wait_ge(k_silu, C + n + 1)
                    v.tensor_scalar(kv[u][:, :, 0:HALF], kv[u][:, :, 0:HALF], 0.5, None, ALU.add).then_inc(halves, 1)
                for u in range(2):
                    n = i * 2 + u
                    dve.wait_ge(squares, C + 2 * n + 1)
                    for j in range(TILES):
                        last = v.tensor_reduce(norm[u][:, j, 0:2 * LA_H], k_sq[u][:, j, :].rearrange("p (h d) -> p h d", d=LA_D), AX, ALU.add)
                    last.then_inc(k_norm2, 1)
                for u in range(2):
                    n = i * 2 + u
                    dve.wait_ge(norms, C + n + 1)
                    own.link(v.tensor_scalar(norm[u][:, :, :], norm[u][:, :, :], 1e-6, None, ALU.add))
                    own.link(v.reciprocal(inv[u][:, :, :], norm[u][:, :, :]))
                    for j in range(TILES):
                        k_v = kv[u][:, j, 0:HALF].rearrange("p (h d) -> p h d", d=LA_D)
                        last = v.tensor_tensor(k_v, k_v, heads_wide(inv[u][:, j, 0:2 * LA_H], LA_D), ALU.mult)
                    last.then_inc(k_scaled, 1)
                for u in range(2):
                    n = i * 2 + u
                    dve.wait_ge(states, C + n + 1)
                    own.link(v.tensor_tensor(state0[u][:, :], bank(X(u))[:, 0:P], M.state_mask[:, :], ALU.mult))
                    v.tensor_tensor(state[u][:, :], bank(X(u))[:, P:2 * P], state0[u][:, :], ALU.mult).then_inc(state_ready, 1)
                for u in range(2):
                    n = i * 2 + u
                    dve.wait_ge(out_made, C + n + 1)
                    for j in range(TILES):
                        place = own.done(v.tensor_tensor(o[u][:, j, :].rearrange("p (h d) -> p h d", d=LA_D),
                                                         bank(K0(u))[:, j * P:(j + 1) * P].rearrange("p (h d) -> p h d", d=LA_D),
                                                         heads_wide(inv[u][:, j, 2 * LA_H:], LA_D), ALU.mult))
                    own.wait(place)
                    stats(o[u], u, o_var)
                for u in range(2):
                    n = i * 2 + u
                    dve.wait_ge(o_rstd, C + n + 1)
                    normed(on[u], o[u], u, o_normed)
                for u in range(2):
                    n = i * 2 + u
                    dve.wait_ge(o_turned, C + n + 1)
                    v.tensor_scalar(o_fea[u][:, :], bank(Y(u))[:, 0:TOK], M.a_lng[:, :], M.a_lnb[:, :], ALU.mult, ALU.add).then_inc(o_fea_ready, 1)
                for u in range(2):
                    n = i * 2 + u
                    dve.wait_ge(f_made, C + n + 1)
                    own.link(v.tensor_tensor(r[u][:, :, :], bank(K0(u) + 1)[:, 0:TOK].rearrange("p (j c) -> p j c", j=TILES), x_tok[u][:, :, :], ALU.add))
                    own.link(v.tensor_tensor(r[u][:, :, :], r[u][:, :, :], M.a_bo[:, :].unsqueeze(1).broadcast_to([P, TILES, DIM]), ALU.add))
                    stats(r[u], u, r_var)
                for u in range(2):
                    n = i * 2 + u
                    dve.wait_ge(r_rstd, C + n + 1)
                    normed(r[u], r[u], u, x1_ready)
                own.end()


class Channel:

    def __init__(self, eng, filled, read):
        self.eng, self.filled, self.read = eng, filled, read

    def at(self, uses):
        self.uses = uses

    def filling(self):
        self.eng.wait_ge(self.read, C + self.uses)
        self.uses = self.uses + 1

    def reading(self):
        self.uses = self.uses + 1
        self.eng.wait_ge(self.filled, C + self.uses)


def over_sequences(eng, heads, lag, pre, head, tail, layer=0):
    def body(s, u, first=False, last=False):
        for h in range(heads + lag):
            head(layer, s, u, h, first, last)
            if not first:
                tail(layer, s - 1, 1 - u, h)
            if not last:
                pre(layer, s + 1, 1 - u, h, first)
        if not last:
            pre(layer, s + 1, 1 - u, None, first)
    for h in list(range(heads + lag)) + [None]:
        pre(layer, 0, 0, h, None)
    body(0, 0, first=True)
    with eng.Fori(0, SEQ // 2 - 1) as i:
        body(2 * i + 1, 1)
        body(2 * i + 2, 0)
    body(SEQ - 1, 1, last=True)
    for h in range(heads + lag):
        tail(layer, SEQ - 1, 1, h)


def over_local(eng, early, pre, step, after, tail, drain, layer):
    def body(s, u, first=False, last=False):
        for h in range(LO_H):
            if not last:
                early(layer, s + 1, 1 - u, h, first)
            step(layer, s, u, h, first)
            after(layer, s, u, h, first)
            if not first:
                tail(layer, s - 1, 1 - u, h)
            if not last:
                pre(layer, s + 1, 1 - u, h, first)
    for h in range(LO_H):
        early(layer, 0, 0, h, None)
        pre(layer, 0, 0, h, None)
    body(0, 0, first=True)
    with eng.Fori(0, SEQ // 2 - 1) as i:
        body(2 * i + 1, 1)
        body(2 * i + 2, 0)
    body(SEQ - 1, 1, last=True)
    drain(layer, SEQ - 1, 1)
    for h in range(LO_H):
        tail(layer, SEQ - 1, 1, h)


def local_transformer(nc, M, dram):
    ctx = ExitStack()
    with ctx:
        sb = lambda name, shape, dt=F32: ctx.enter_context(nc.sbuf_tensor(name, shape, dt))
        sem = lambda name: ctx.enter_context(nc.semaphore(name))
        INNER = LO_H * LO_D
        CH = INNER // P
        S1 = P + WINDOW
        PW = P + TOK
        tables = sb("b_tables", [P, LAYERS, 4, TILES, LO_D])
        table_scale = sb("b_table_scale", [P, LAYERS, 4, LO_D])
        h_fea = [sb(f"b_h{u}", [P, TOK]) for u in range(2)]
        sq = sb("b_sq", [P, 2 * INNER])
        ss = sb("b_ss", [P, 2 * LO_H])
        ln_ss = sb("b_ln_ss", [P, 2 * LO_H])
        root = sb("b_root", [P, 2 * LO_H])
        q_scale = [sb(f"b_q_scale{u}", [P, TILES, LO_H]) for u in range(2)]
        k_scale = sb("b_k_scale", [P, LO_H])
        k_unit = sb("b_k_unit", [P, INNER])
        rot_q = [sb(f"b_rot_q{j}", [P, 2, INNER]) for j in range(TILES)]
        rot_k = [sb(f"b_rot_k{j}", [P, 2, INNER]) for j in range(TILES)]
        v_tok = [sb(f"b_v{u}", [P, TILES, INNER]) for u in range(2)]
        q_fea = [sb(f"b_q_fea{u}", [P, CH, TOK]) for u in range(2)]
        k_fea = [sb(f"b_k_fea{u}", [P, CH, TOK]) for u in range(2)]
        mx = [sb(f"b_mx{p}", [P, TILES]) for p in range(4)]
        neg = [sb(f"b_neg{p}", [P, TILES]) for p in range(4)]
        prob = [sb(f"b_prob{p}", [P, PW]) for p in range(4)]
        prob_t = [sb(f"b_prob_t{p}", [P, PW]) for p in range(2)]
        row_sum = [sb(f"b_row_sum{u}", [P, TILES, LO_H]) for u in range(2)]
        inv_sum = [sb(f"b_inv_sum{e}", [P, TILES, LO_H // 2]) for e in range(2)]
        o = sb("b_o", [P, TILES, INNER])
        o_fea = sb("b_o_fea", [P, CH, TOK])
        h_ffn = [sb(f"b_hf{u}", [P, BLK]) for u in range(2)]
        c_sq = [sb(f"b_csq{u}", [P, BLK]) for u in range(2)]
        lnv = [sb(f"b_lnv{u}", [P, BLK]) for u in range(2)]
        rstd = [sb(f"b_rstd{u}", [P, BLK]) for u in range(2)]
        hn = sb("b_hn", [P, SEQ * TOK])
        gelu = [sb(f"b_gelu{k}", [P, BLK]) for k in range(3)]
        hid = [sb(f"b_hid{k}", [P, BLK]) for k in range(3)]
        wo, w1, w2, cols = M.b_wo, M.b_w1, M.b_w2, M.b_cols

        tables_ready, table_loaded = sem("b_tables_ready"), sem("b_table_loaded")
        h_ready, qk_made, v_made = sem("b_h_ready"), sem("b_qk_made"), sem("b_v_made")
        squared, summed, rooted, v_copied = sem("b_squared"), sem("b_summed"), sem("b_rooted"), sem("b_v_copied")
        k_unit_ready, q_rotated, k_rotated = sem("b_k_unit_ready"), sem("b_q_rotated"), sem("b_k_rotated")
        five_filled, five_read = sem("b_five_filled"), sem("b_five_read")
        two_filled, two_read = sem("b_two_filled"), sem("b_two_read")
        scored, neg_ready, exped, pv_made, scaled = sem("b_scored"), sem("b_neg_ready"), sem("b_exped"), sem("b_pv_made"), sem("b_scaled")
        own_squares, own_scale, own_max, own_inv, own_ln = (sem("b_own_" + s) for s in ("squares", "scale", "max", "inv", "ln"))
        spare = sem("b_spare")
        wo_loaded, ffn_loaded = sem("b_wo_loaded"), sem("b_ffn_loaded")
        hf_ready, centered, csquared, var_made, rstd_ready, hn_ready, own_var, own_hn = (sem("b_" + s) for s in (
            "hf_ready", "centered", "csquared", "var_made", "rstd_ready", "hn_ready", "own_var", "own_hn"))
        ag_made, gelued, hid_ready, y_made, ffn_written = (sem("b_" + s) for s in ("ag_made", "gelued", "hid_ready", "y_made", "ffn_written"))
        bank = M.bank
        block = ctx.enter_context(nc.Block())
        tile = lambda l, s, j: (l * SEQ + s) * TILES + j
        swapped = lambda ap: ap.rearrange("p (h t d) -> p h t d", t=2, d=LO_D // 2)[:, :, ::-1, :]
        by_head = lambda ap: ap.rearrange("p (h d) -> p h d", d=LO_D)

        nothing = lambda *a: None

        def table(l, kind, j):
            return tables[:, l, kind, j, :].unsqueeze(1).broadcast_to([P, LO_H, LO_D])

        def table_half(l, kind, j, t):
            half = LO_D // 2
            return tables[:, l, kind, j, t * half:(t + 1) * half].unsqueeze(1).broadcast_to([P, LO_H, half])

        def half_heads(ap, t):
            return ap.rearrange("p (h t d) -> p t h d", t=2, d=LO_D // 2)[:, t, :, :]

        FIVE_USES, TWO_USES = SEQ * 7, SEQ * 8
        O_TURNED = 3
        SCORE_BANKS = (3, 4, 7)
        before = lambda h: (-1, 0, -2)[h] if h < 3 else h - 2

        def five_before(l, s, first):
            return l * FIVE_USES + (2 if first else s * 7)

        def two_before(l, s, first):
            return l * TWO_USES + (2 if first else s * 8 - 1)

        def five_at_end(l):
            return (l + 1) * FIVE_USES - 2

        def two_at_end(l):
            return (l + 1) * TWO_USES - 3

        @block.sync
        def _(sp):
            sp.dma_start(table_scale[:, :, :, :], dram["b_table_scale"].partition_broadcast(P)).then_inc(table_loaded, 16)
            with sp.Fori(0, LAYERS) as l:
                sp.wait_ge(two_read, C + l * TWO_USES)
                sp.dma_start(wo[:, :, :], dram["b_wo"][bass.ds(l, 1), :, :, :].rearrange("l p c n -> p (l c) n")).then_inc(wo_loaded, 16)
                sp.wait_ge(ffn_written, C + l * NBLK)
                sp.dma_start(w1[:, :], dram["b_w1"][bass.ds(l, 1), :, :].rearrange("l p n -> p (l n)")).then_inc(ffn_loaded, 16)
                sp.dma_start(w2[:, :, :], dram["b_w2"][bass.ds(l, 1), :, :, :].rearrange("l p c n -> p (l c) n")).then_inc(ffn_loaded, 16)
                sp.dma_start(cols[:, :], dram["b_cols"][bass.ds(l, 1), :, :].rearrange("l p n -> p (l n)")).then_inc(ffn_loaded, 16)

        @block.gpsimd
        def _(pool):
            for s in (h_ready, k_rotated, hf_ready):
                pool.sem_inc(s, C)
            for u in range(2):
                nc.gpsimd.memset(h_fea[u][:, :], 0.0).then_inc(tables_ready, 1)
                nc.gpsimd.memset(h_ffn[u][:, :], 0.0).then_inc(tables_ready, 1)
            pool.wait_ge(tables_ready, 5 + LAYERS)

            def pre(l, s, u, h, first):
                if h == 0:
                    pool.wait_ge(v_made, C + l * SEQ + s - 1)
                    pool.wait_ge(k_rotated, C + tile(l, s, 0))
                    gate(pool, spare)
                    nc.gpsimd.tensor_copy(h_fea[u][0:64, :], M.xb[0:64, l, bass.ts(s, TOK)]).then_inc(h_ready, 1)
                    pool.wait_ge(h_ready, C + 2 * (l * SEQ + s) + 1)
                    gate(pool, spare)
                    nc.gpsimd.tensor_copy(h_fea[u][64:P, 1:TOK], M.xb[64:P, l, bass.ds(s * TOK, TOK - 1)]).then_inc(h_ready, 1)
                if h in (3, 6):
                    j = h // 6
                    pool.wait_ge(k_unit_ready, C + tile(l, s, j) + 1)
                    if h == 3:
                        pool.wait_ge(h_ready, C + 2 * (l * SEQ + s) + 2)
                    if first is not None:
                        pool.wait_ge(two_filled, C + two_before(l, s - 1, first))
                    gate(pool, spare)
                    nc.gpsimd.tensor_tensor(by_head(rot_k[j][:, 0, :]), by_head(k_unit[:, :]), table(l, 2, j), ALU.mult)
                    for t in range(2):
                        last = nc.gpsimd.tensor_tensor(half_heads(rot_k[j][:, 1, :], t), half_heads(k_unit[:, :], 1 - t), table_half(l, 3, j, t), ALU.mult)
                    last.then_inc(k_rotated, 1)

            with pool.Fori(0, LAYERS) as l:
                pool.wait_ge(ffn_written, C + l * NBLK)
                pool.wait_ge(hf_ready, C + 2 * (l * NBLK))
                gate(pool, spare)
                over_local(pool, nothing, pre, nothing, nothing, nothing, nothing, l)
                pool.wait_ge(two_read, C + l * TWO_USES + TWO_USES)
                gate(pool, spare)
                with pool.Fori(0, NBLK // 2) as i:
                    for u in range(2):
                        b = i * 2 + u
                        pool.wait_ge(centered, C + l * NBLK + b - 1)
                        pool.wait_ge(hf_ready, C + 2 * (l * NBLK + b))
                        gate(pool, spare)
                        nc.gpsimd.tensor_copy(h_ffn[u][0:64, :], M.xb[0:64, 1, bass.ts(b, BLK)]).then_inc(hf_ready, 1)
                        pool.wait_ge(hf_ready, C + 2 * (l * NBLK + b) + 1)
                        gate(pool, spare)
                        nc.gpsimd.tensor_copy(h_ffn[u][64:P, :].rearrange("p (s t) -> p s t", t=TOK)[:, :, 1:TOK],
                                              M.xb[64:P, 1, bass.ts(b, BLK)].rearrange("p (s t) -> p s t", t=TOK)[:, :, 0:TOK - 1]).then_inc(hf_ready, 1)

        @block.tensor
        def _(pe):
            for s in (qk_made, v_made, five_filled, two_filled, scored, pv_made, centered, var_made, ag_made, y_made):
                pe.sem_inc(s, C)
            mm = nc.tensor.matmul
            five, two = Channel(pe, five_filled, five_read), Channel(pe, two_filled, two_read)
            pe.wait_ge(M.loaded_b, M.LOADED_B)
            turned, o_turned = [None, None], [None]

            def pre(l, s, u, h, first):
                if first is None and h == 0:
                    five.at(l * FIVE_USES)
                    two.at(l * TWO_USES)
                if h in (1, 4):
                    j = h // 4
                    if h == 1:
                        pe.wait_ge(h_ready, C + 2 * (l * SEQ + s) + 2)
                        pe.wait_ge(v_copied, C + l * SEQ + s)
                    pe.wait_ge(q_rotated, C + tile(l, s, j))
                    pe.wait_ge(k_unit_ready, C + tile(l, s, j))
                    for part in range(2):
                        last = mm(bank(part), h_fea[u][:, j * P:(j + 1) * P], M.b_wqkv[:, l, part * INNER:(part + 1) * INNER], start=True, stop=True)
                    last.then_inc(qk_made, 1)
                if h in (5, 7):
                    j = h // 7
                    for src, ch, b, sig, made in ((rot_q[j], five, 5, five_filled, q_rotated), (rot_k[j], two, 2, two_filled, k_rotated)):
                        pe.wait_ge(made, C + tile(l, s, j) + 1)
                        ch.filling()
                        for c in range(CH):
                            for w in range(2):
                                last = mm(bank(b)[:, c * P:(c + 1) * P], src[:, w, c * P:(c + 1) * P], M.ident[:, :], is_transpose=True,
                                          start=(w == 0), stop=(w == 1))
                        last.then_inc(sig, 1)
                if h == 7:
                    pe.wait_ge(q_rotated, C + tile(l, s, 1) + 1)
                    pe.wait_ge(k_unit_ready, C + tile(l, s, 1) + 1)
                    for j in range(TILES):
                        last = mm(bank(j), h_fea[u][:, j * P:(j + 1) * P], M.b_wqkv[:, l, 2 * INNER:3 * INNER], start=True, stop=True)
                    last.then_inc(v_made, 1)

            def turn(n, g):
                pe.wait_ge(exped, C + n * LO_H + g + 1)
                ch, b, sig = (five, 5, five_filled) if g % 2 == 0 else (two, 2, two_filled)
                ch.filling()
                for t in range(3):
                    last = nc.tensor.transpose(bank(b)[:, t * P:(t + 1) * P], prob[g % 4][:, t * P:(t + 1) * P], M.ident[:, :])
                last.then_inc(sig, 1)
                turned[g % 2] = ch.uses

            def weigh(n, u, g):
                pe.wait_ge(five_read if g % 2 == 0 else two_read, C + turned[g % 2])
                if g == 0:
                    pe.wait_ge(v_copied, C + n + 1)
                if g % 4 == 0:
                    pe.wait_ge(scaled, C + 2 * n + g // 4)
                at, vc = (g % 4) * LO_D, slice(g * LO_D, (g + 1) * LO_D)
                mm(bank(6)[:, at:at + LO_D], prob_t[g % 2][:, 0:P], v_tok[u][:, 0, vc], start=True, stop=True)
                at = at + BANK // 2
                mm(bank(6)[:, at:at + LO_D], prob_t[g % 2][:, P:2 * P], v_tok[u][:, 0, vc], start=True, stop=False)
                mm(bank(6)[:, at:at + LO_D], prob_t[g % 2][:, 2 * P:3 * P], v_tok[u][:, 1, vc], start=False, stop=True).then_inc(pv_made, 1)

            def step(l, s, u, h, first):
                n = l * SEQ + s
                if h == 0:
                    five.at(five_before(l, s, first))
                    two.at(two_before(l, s, first))
                    pe.wait_ge(five_read, C + five_before(l, s, first))
                    pe.wait_ge(two_read, C + two_before(l, s, first))
                    turned[1] = two_before(l, s, first)
                c, rows, b = h // 2, slice((h % 2) * LO_D, (h % 2 + 1) * LO_D), SCORE_BANKS[h % 3]
                pe.wait_ge(exped, C + n * LO_H + before(h))
                mm(bank(b)[:, 0:P], q_fea[u][rows, c, 0:P], k_fea[u][rows, c, 0:P], start=True, stop=False)
                mm(bank(b)[:, 0:P], M.identb[:, :], M.mask_lo0[:, :], start=False, stop=True)
                mm(bank(b)[:, P:P + S1], q_fea[u][rows, c, P:TOK], k_fea[u][rows, c, TOK - S1:TOK], start=True, stop=False)
                mm(bank(b)[:, P:P + S1], M.identb[:, :], M.mask_lo1[:, :], start=False, stop=True).then_inc(scored, 1)

            def after(l, s, u, h, first):
                n = l * SEQ + s
                if h > 1:
                    turn(n, h - 2)
                elif not first:
                    turn(n - 1, h - 2 + LO_H)
                if h > 2:
                    weigh(n, u, h - 3)
                elif not first:
                    weigh(n - 1, 1 - u, h - 3 + LO_H)

            def drain(l, s, u):
                n = l * SEQ + s
                turned[1] = two_at_end(l)
                five.at(five_at_end(l))
                two.at(two_at_end(l))
                turn(n, LO_H - 2)
                weigh(n, u, LO_H - 3)
                turn(n, LO_H - 1)
                weigh(n, u, LO_H - 2)
                weigh(n, u, LO_H - 1)

            def tail(l, s, u, h):
                n = l * SEQ + s
                if h == 3:
                    pe.wait_ge(scaled, C + 2 * n + 2)
                    for j, (ch, b, sig) in enumerate(((five, 5, five_filled), (two, 2, two_filled))):
                        ch.filling()
                        for c in range(CH):
                            last = nc.tensor.transpose(bank(b)[:, c * P:(c + 1) * P], o[:, j, c * P:(c + 1) * P], M.ident[:, :])
                        last.then_inc(sig, 1)
                    o_turned[0] = five.uses
                if h == 6:
                    pe.wait_ge(wo_loaded, l * 16 + 16)
                    pe.wait_ge(five_read, C + o_turned[0])
                    two.filling()
                    for c in range(CH):
                        last = mm(bank(2)[:, 0:TOK], wo[:, c, :], o_fea[:, c, :], start=(c == 0), stop=(c == CH - 1))
                    last.then_inc(two_filled, 1)

            with pe.Fori(0, LAYERS) as l:
                over_local(pe, nothing, pre, step, after, tail, drain, l)
                pe.wait_ge(two_read, C + l * TWO_USES + TWO_USES)
                gate(pe, spare)
                f0 = l * NBLK
                with pe.Fori(0, NBLK // 2) as i:
                    for u in range(2):
                        b = i * 2 + u
                        pe.wait_ge(hf_ready, C + 2 * (f0 + b) + 2)
                        pe.wait_ge(hn_ready, C + f0 + b - 1)
                        mm(bank(u), M.center[:, :], h_ffn[u][:, :], start=True, stop=True).then_inc(centered, 1)
                    for u in range(2):
                        b = i * 2 + u
                        pe.wait_ge(csquared, C + f0 + b + 1)
                        mm(bank(2 + u), M.mean[:, :], c_sq[u][:, :], start=True, stop=True).then_inc(var_made, 1)
                pe.wait_ge(hn_ready, C + f0 + NBLK)
                pe.wait_ge(ffn_loaded, l * 48 + 48)
                gate(pe, spare)
                with pe.Fori(0, NBLK) as b:
                    for k, (off, w) in enumerate(HID_CUT):
                        pe.wait_ge(hid_ready, C + 3 * (f0 + b) + k - 2)
                        mm(bank(2 * k)[0:w, :], w1[:, HID + off:HID + off + w], hn[:, bass.ts(b, BLK)], start=True, stop=True)
                        mm(bank(2 * k + 1)[0:w, :], w1[:, off:off + w], hn[:, bass.ts(b, BLK)], start=True, stop=True).then_inc(ag_made, 1)
                    pe.wait_ge(ffn_written, C + f0 + b)
                    for k, (off, w) in enumerate(HID_CUT):
                        pe.wait_ge(hid_ready, C + 3 * (f0 + b) + k + 1)
                        last = mm(bank(6), w2[0:w, k, :], hid[k][0:w, :], start=(k == 0), stop=(k == 2))
                    last.then_inc(y_made, 1)
                pe.wait_ge(ffn_written, C + f0 + NBLK)
                gate(pe, spare)

        @block.scalar
        def _(act):
            for s in (squared, rooted, v_copied, five_read, exped, csquared, rstd_ready, gelued):
                act.sem_inc(s, C)
            a = nc.scalar.activation
            five = Channel(act, five_filled, five_read)
            own, own_l = Steps(act, own_ln, 1), Steps(act, own_var, 1)
            act.wait_ge(tables_ready, 5 + LAYERS)

            def early(l, s, u, h, first):
                if first is None and h == 0:
                    five.at(l * FIVE_USES)
                if h in (2, 5):
                    j = h // 5
                    act.wait_ge(qk_made, C + tile(l, s, j) + 1)
                    act.wait_ge(summed, C + tile(l, s, j))
                    a(sq[:, :].rearrange("p (b n) -> p b n", b=2), M.psum[:, 0:2, :], ACT.Square).then_inc(squared, 1)
                if h in (3, 6):
                    j = h // 6
                    own.at(tile(l, s, j))
                    act.wait_ge(summed, C + tile(l, s, j) + 1)
                    own.link(a(ln_ss[:, :], ss[:, :], ACT.Ln, scale=65536.0))
                    a(root[:, :], ln_ss[:, :], ACT.Exp, scale=-0.5).then_inc(rooted, 1)

            def pre(l, s, u, h, first):
                if h in (5, 7):
                    j = h // 7
                    if h == 5 and first is not None:
                        act.wait_ge(scored, C + (l * SEQ + s - 1) * LO_H)
                    five.reading()
                    a(q_fea[u][:, :, j * P:(j + 1) * P], bank(5).rearrange("p (c n) -> p c n", c=CH), ACT.Copy).then_inc(five_read, 1)
                if h == 7:
                    n = l * SEQ + s
                    act.wait_ge(v_made, C + n + 1)
                    if first is not None:
                        act.wait_ge(pv_made, C + (n - 1) * LO_H)
                    a(v_tok[u][:, :, :], M.psum[:, 0:2, :], ACT.Copy).then_inc(v_copied, 1)

            def take_turned(n, g):
                five.reading()
                act.wait_ge(pv_made, C + n * LO_H + g - 1)
                a(prob_t[0][:, :], bank(5)[:, 0:PW], ACT.Copy).then_inc(five_read, 1)

            def step(l, s, u, h, first):
                n = l * SEQ + s
                if h == 0:
                    five.at(five_before(l, s, first))
                    act.wait_ge(scaled, C + 2 * n - 2)
                p, b = h % 4, SCORE_BANKS[h % 3]
                act.wait_ge(neg_ready, C + n * LO_H + h + 1)
                act.wait_ge(pv_made, C + n * LO_H + h - 4)
                a(prob[p][:, 0:P], bank(b)[:, 0:P], ACT.Exp, bias=neg[p][:, 0:1], scale=q_scale[u][:, 0, h:h + 1],
                  accum_out=row_sum[u][:, 0, h:h + 1])
                a(prob[p][:, PW - S1:PW], bank(b)[:, P:P + S1], ACT.Exp, bias=neg[p][:, 1:2], scale=q_scale[u][:, 1, h:h + 1],
                  accum_out=row_sum[u][:, 1, h:h + 1]).then_inc(exped, 1)

            def after(l, s, u, h, first):
                n = l * SEQ + s
                if h % 2 == 0 and h > 1:
                    take_turned(n, h - 2)
                if h == 0 and not first:
                    take_turned(n - 1, LO_H - 2)

            def drain(l, s, u):
                five.at(five_at_end(l))
                take_turned(l * SEQ + s, LO_H - 2)

            def tail(l, s, u, h):
                if h == 3:
                    five.reading()
                    act.wait_ge(two_filled, C + two_before(l, s + 1, False))
                    a(o_fea[:, :, 0:P], bank(5).rearrange("p (c n) -> p c n", c=CH), ACT.Copy).then_inc(five_read, 1)

            with act.Fori(0, LAYERS) as l:
                nc.scalar.preload_act_table_set(LN_EXP_SET)
                over_local(act, early, pre, step, after, tail, drain, l)
                f0 = l * NBLK
                with act.Fori(0, NBLK // 2) as i:
                    for u in range(2):
                        b = i * 2 + u
                        act.wait_ge(centered, C + f0 + b + 1)
                        act.wait_ge(var_made, C + f0 + b - 1)
                        a(c_sq[u][:, :], bank(u), ACT.Square).then_inc(csquared, 1)
                    for u in range(2):
                        b = i * 2 + u
                        own_l.at(f0 + b)
                        act.wait_ge(var_made, C + f0 + b + 1)
                        act.wait_ge(hn_ready, C + f0 + b - 1)
                        own_l.link(a(lnv[u][:, :], bank(2 + u), ACT.Ln, bias=M.eps[:, :]))
                        a(rstd[u][:, :], lnv[u][:, :], ACT.Exp, scale=-0.5).then_inc(rstd_ready, 1)
                nc.scalar.preload_act_table_set(GELU_SET)
                act.wait_ge(ffn_loaded, l * 48 + 48)
                gate(act, spare)
                with act.Fori(0, NBLK) as b:
                    for k, (off, w) in enumerate(HID_CUT):
                        act.wait_ge(ag_made, C + 3 * (f0 + b) + k + 1)
                        act.wait_ge(hid_ready, C + 3 * (f0 + b) + k - 2)
                        a(gelu[k][0:w, :], bank(2 * k)[0:w, :], ACT.Gelu, bias=cols[0:w, 3 + k:4 + k]).then_inc(gelued, 1)

        @block.vector
        def _(dve):
            for s in (summed, k_unit_ready, q_rotated, two_read, neg_ready, scaled, hn_ready, hid_ready, ffn_written):
                dve.sem_inc(s, C)
            v = nc.vector
            for p in range(4):
                last = v.memset(prob[p][:, P:2 * P], 0.0)
            last.then_inc(tables_ready, 1)
            dve.wait_ge(table_loaded, 16)
            dve.wait_ge(M.loaded_b, M.LOADED_B)
            for l in range(LAYERS):
                v.tensor_tensor(tables[:, l, :, :, :], M.rotary[:, :, :, :], table_scale[:, l, :, :].unsqueeze(2).broadcast_to([P, 4, TILES, LO_D]),
                                ALU.mult).then_inc(tables_ready, 1)
            dve.wait_ge(tables_ready, 5 + LAYERS)
            two = Channel(dve, two_filled, two_read)
            own_s, own_k, own_m, own_i, own_h = (Steps(dve, s, 1) for s in (own_squares, own_scale, own_max, own_inv, own_hn))

            def pre(l, s, u, h, first):
                if first is None and h == 0:
                    two.at(l * TWO_USES)
                if h in (2, 5):
                    j = h // 5
                    own_s.at(tile(l, s, j))
                    dve.wait_ge(squared, C + tile(l, s, j) + 1)
                    own_s.link(v.tensor_reduce(ss[:, :], by_head(sq[:, :]), AX, ALU.add))
                    v.tensor_scalar(ss[:, :], ss[:, :], 1e-24, None, ALU.max).then_inc(summed, 1)
                if h in (3, 6):
                    j = h // 6
                    own_k.at(tile(l, s, j))
                    dve.wait_ge(rooted, C + tile(l, s, j) + 1)
                    v.tensor_scalar(q_scale[u][:, j, :], root[:, 0:LO_H], 256.0 * 8.0, None, ALU.mult)
                    own_k.link(v.tensor_scalar(k_scale[:, :], root[:, LO_H:], 256.0, None, ALU.mult))
                    dve.wait_ge(k_rotated, C + tile(l, s, j))
                    v.tensor_tensor(by_head(k_unit[:, :]), by_head(bank(1)), heads_wide(k_scale[:, :], LO_D), ALU.mult).then_inc(k_unit_ready, 1)
                    if first is not None:
                        dve.wait_ge(five_filled, C + five_before(l, s - 1, first))
                    v.tensor_tensor(by_head(rot_q[j][:, 0, :]), by_head(bank(0)), table(l, 0, j), ALU.mult)
                    for t in range(2):
                        last = v.tensor_tensor(half_heads(rot_q[j][:, 1, :], t), half_heads(bank(0), 1 - t), table_half(l, 1, j, t), ALU.mult)
                    last.then_inc(q_rotated, 1)
                if h in (5, 7):
                    j = h // 7
                    if h == 5 and first is not None:
                        dve.wait_ge(scored, C + (l * SEQ + s - 1) * LO_H)
                    two.reading()
                    v.tensor_copy(k_fea[u][:, :, j * P:(j + 1) * P], bank(2).rearrange("p (c n) -> p c n", c=CH)).then_inc(two_read, 1)

            def take_turned(n, g):
                two.reading()
                dve.wait_ge(pv_made, C + n * LO_H + g - 1)
                v.tensor_copy(prob_t[1][:, :], bank(2)[:, 0:PW]).then_inc(two_read, 1)

            def scale(n, u, e):
                dve.wait_ge(exped, C + n * LO_H + 4 * e + 4)
                own_i.at(2 * n + e)
                own_i.link(v.reciprocal(inv_sum[e][:, :, :], row_sum[u][:, :, 4 * e:4 * e + 4]))
                dve.wait_ge(pv_made, C + n * LO_H + 4 * e + 4)
                for j in range(TILES):
                    last = v.tensor_tensor(o[:, j, e * BANK // 2:(e + 1) * BANK // 2].rearrange("p (h d) -> p h d", d=LO_D),
                                           bank(6)[:, j * BANK // 2:(j + 1) * BANK // 2].rearrange("p (h d) -> p h d", d=LO_D),
                                           heads_wide(inv_sum[e][:, j, :], LO_D), ALU.mult)
                last.then_inc(scaled, 1)

            def step(l, s, u, h, first):
                n = l * SEQ + s
                if h == 0:
                    two.at(two_before(l, s, first))
                p, b = h % 4, SCORE_BANKS[h % 3]
                own_m.at(n * LO_H + h)
                dve.wait_ge(scored, C + n * LO_H + h + 1)
                dve.wait_ge(exped, C + n * LO_H + h - 3)
                v.tensor_reduce(mx[p][:, 0:1], bank(b)[:, 0:P], AX, ALU.max)
                own_m.link(v.tensor_reduce(mx[p][:, 1:2], bank(b)[:, P:P + S1], AX, ALU.max))
                v.scalar_tensor_tensor(neg[p][:, :], mx[p][:, :], -1.0, q_scale[u][:, :, h], ALU.mult, ALU.mult).then_inc(neg_ready, 1)

            def after(l, s, u, h, first):
                n = l * SEQ + s
                if h == 1 and not first:
                    take_turned(n - 1, LO_H - 1)
                if h % 2 == 1 and h > 1:
                    take_turned(n, h - 2)
                if h == 2 and not first:
                    scale(n - 1, 1 - u, 1)
                if h == 6:
                    if not first:
                        dve.wait_ge(five_filled, C + five_before(l, s, first) + O_TURNED)
                        dve.wait_ge(two_filled, C + two_before(l, s, first) + O_TURNED)
                    scale(n, u, 0)

            def drain(l, s, u):
                n = l * SEQ + s
                two.at(two_at_end(l))
                take_turned(n, LO_H - 1)
                scale(n, u, 1)

            def tail(l, s, u, h):
                if h == 4:
                    two.reading()
                    v.tensor_copy(o_fea[:, :, P:TOK], bank(2).rearrange("p (c n) -> p c n", c=CH)).then_inc(two_read, 1)
                if h == 6:
                    two.reading()
                    v.tensor_tensor(M.xb[:, 1, bass.ts(s, TOK)], bank(2)[:, 0:TOK], M.xb[:, l, bass.ts(s, TOK)], ALU.add).then_inc(two_read, 1)

            with dve.Fori(0, LAYERS) as l:
                over_local(dve, nothing, pre, step, after, tail, drain, l)
                f0 = l * NBLK
                dve.wait_ge(ffn_loaded, l * 48 + 48)
                gate(dve, spare)
                with dve.Fori(0, NBLK // 2) as i:
                    for u in range(2):
                        b = i * 2 + u
                        own_h.at(f0 + b)
                        dve.wait_ge(rstd_ready, C + f0 + b + 1)
                        own_h.link(v.scalar_tensor_tensor(hn[:, bass.ts(b, BLK)], bank(u), cols[:, 0:1], rstd[u][:, :], ALU.mult, ALU.mult))
                        v.tensor_scalar(hn[:, bass.ts(b, BLK)], hn[:, bass.ts(b, BLK)], cols[:, 1:2], None, ALU.add).then_inc(hn_ready, 1)
                with dve.Fori(0, NBLK) as b:
                    dve.wait_ge(y_made, C + f0 + b)
                    for k, (off, w) in enumerate(HID_CUT):
                        dve.wait_ge(gelued, C + 3 * (f0 + b) + k + 1)
                        v.scalar_tensor_tensor(hid[k][0:w, :], bank(2 * k + 1)[0:w, :], cols[0:w, 6 + k:7 + k], gelu[k][0:w, :],
                                               ALU.add, ALU.mult).then_inc(hid_ready, 1)
                    dve.wait_ge(y_made, C + f0 + b + 1)
                    v.scalar_tensor_tensor(M.xb[:, 1, bass.ts(b, BLK)], bank(6), cols[:, 2:3], M.xb[:, 1, bass.ts(b, BLK)],
                                           ALU.add, ALU.add).then_inc(ffn_written, 1)


def causal_attention(nc, M, dram):
    ctx = ExitStack()
    with ctx:
        sb = lambda name, shape, dt=F32: ctx.enter_context(nc.sbuf_tensor(name, shape, dt))
        sem = lambda name: ctx.enter_context(nc.semaphore(name))
        HC = CA_H // 2
        LAG = 2
        V_BANKS = (7, 2, 7, 3)
        HALF = 8 * CA_D
        PW = P + TOK
        z = sb("c_z", [P, TOK])
        x2 = [sb(f"c_x2{u}", [P, TILES, DIM]) for u in range(2)]
        x2_fea = [sb(f"c_x2_fea{u}", [P, TOK]) for u in range(2)]
        v_tok = [sb(f"c_v{u}", [P, TILES, CA_H * CA_D]) for u in range(2)]
        qk = [sb(f"c_qk{p}", [P, 2, TOK]) for p in range(2)]
        neg = [sb(f"c_neg{p}", [P, TILES]) for p in range(2)]
        prob = [sb(f"c_prob{p}", [P, PW]) for p in range(2)]
        prob_t = [sb(f"c_prob_t{p}", [P, PW]) for p in range(2)]
        row_sum = [sb(f"c_row_sum{u}", [P, TILES, CA_H]) for u in range(2)]
        inv_sum = [sb(f"c_inv_sum{e}", [P, TILES, 8]) for e in range(2)]
        o = sb("c_o", [P, TILES, CA_H * CA_D])
        o_fea = sb("c_o_fea", [P, HC, TOK])
        r = sb("c_r", [P, TILES, DIM])
        x3 = sb("c_x3", [P, TILES, DIM])
        x3_fea = sb("c_x3_fea", [P, TOK])
        st, mv = [sb(f"c_st{k}", [P, TILES, 6]) for k in range(2)], [sb(f"c_mv{k}", [P, TILES, 2]) for k in range(2)]
        lnv, rstd = [sb(f"c_lnv{k}", [P, TILES]) for k in range(2)], [sb(f"c_rstd{k}", [P, TILES]) for k in range(2)]

        names = ("wq_scaled w1_high qk_made qk_read scored neg_ready exped even_made even_read odd_made odd_read pv_made scaled "
                 "z_ready z_turned z_var z_rstd x2_ready x2_turned x2_fea_ready v_made v_copied "
                 "o_turned o_read y_made r_var r_rstd x3_ready x3_turned x3_fea_ready routed logits_read stored "
                 "own_inv own_r own_st own_st2 own_ln own_ln2 spare").split()
        S = {}
        for name in names:
            S[name] = sem("c_" + name)
        bank = M.bank
        block = ctx.enter_context(nc.Block())

        def before_start(eng, names):
            for name in names.split():
                eng.sem_inc(S[name], C)

        @block.sync
        def _(sp):
            for dst, src in M.d_loads:
                sp.dma_start(dst, src).then_inc(M.loaded_d, 16)

        @block.gpsimd
        def _(pool):
            before_start(pool, "z_ready stored")

            def pre(l, s, u, h, first):
                if h == 10 and first:
                    pool.wait_ge(M.loaded_d, M.LOADED_D)
                    nc.gpsimd.tensor_copy(M.d_w1_hi[:, :, :], M.d_w1[:, :, :]).then_inc(S["w1_high"], 1)
                    pool.wait_ge(S["w1_high"], 1)
                    nc.gpsimd.tensor_tensor(M.d_w1_lo[:, :, :], M.d_w1[:, :, :], M.d_w1_hi[:, :, :].bitcast(F32), ALU.subtract)
                if h == 9:
                    pool.wait_ge(S["z_turned"], C + s)
                    gate(pool, S["spare"])
                    nc.gpsimd.tensor_tensor(z[:, :], M.xb[:, 0, bass.ts(s, TOK)], M.xb[:, 1, bass.ts(s, TOK)], ALU.add).then_inc(S["z_ready"], 1)

            def tail(l, s, u, h):
                if h == 8:
                    pool.wait_ge(S["x3_ready"], C + s + 1)
                    pool.wait_ge(S["x3_fea_ready"], C + s + 1)
                    gate(pool, S["spare"])
                    nc.gpsimd.tensor_copy(M.xb[:, 1, bass.ts(s, TOK)], x3[:, :, :].rearrange("p j c -> p (j c)")).then_inc(S["stored"], 1)
                    nc.gpsimd.tensor_copy(M.xb[:, 0, bass.ts(s, TOK)], x3_fea[:, :]).then_inc(S["stored"], 1)

            over_sequences(pool, CA_H, LAG, pre, lambda *a: None, tail, 0)

        @block.tensor
        def _(pe):
            before_start(pe, "qk_made scored even_made odd_made pv_made z_turned x2_turned v_made o_turned y_made x3_turned routed")
            mm = nc.tensor.matmul
            pe.wait_ge(M.loaded_c, M.LOADED_C)
            pe.wait_ge(S["wq_scaled"], 1)

            def project(n, c, u):
                pe.wait_ge(S["qk_read"], C + n * HC + c)
                for part in range(2):
                    last = mm(bank(2)[:, part * TOK:(part + 1) * TOK], M.c_w[:, part, c * P:(c + 1) * P], x2_fea[u][:, :], start=True, stop=True)
                last.then_inc(S["qk_made"], 1)

            def pre(l, s, u, h, first):
                if h == 10:
                    pe.wait_ge(S["z_ready"], C + s + 1)
                    if first is not None:
                        pe.wait_ge(S["logits_read"], C + s - 1)
                        pe.wait_ge(S["v_copied"], C + 4 * s)
                    for j in range(TILES):
                        last = nc.tensor.transpose(bank(7)[:, j * P:(j + 1) * P], z[:, j * P:(j + 1) * P], M.ident[:, :])
                    last.then_inc(S["z_turned"], 1)
                if h == 14:
                    pe.wait_ge(S["x2_ready"], C + s + 1)
                    for j in range(TILES):
                        last = nc.tensor.transpose(bank(7)[:, j * P:(j + 1) * P], x2[u][:, j, :], M.ident[:, :])
                    last.then_inc(S["x2_turned"], 1)
                if h is None or h >= 15:
                    k = 3 if h is None else h - 15
                    if k == 0:
                        pe.wait_ge(S["x2_fea_ready"], C + s + 1)
                    j, e = k // 2, k % 2
                    if k == 1:
                        pe.wait_ge(S["qk_read"], C + s * HC)
                    elif k == 2:
                        pe.wait_ge(S["v_copied"], C + 4 * s + 1)
                    elif k == 3:
                        pe.wait_ge(S["even_read"], C + s * HC)
                    mm(bank(V_BANKS[k]), x2_fea[u][:, j * P:(j + 1) * P], M.c_w[:, 2, e * HALF:(e + 1) * HALF], start=True, stop=True).then_inc(S["v_made"], 1)
                if h is None:
                    pe.wait_ge(S["v_copied"], C + 4 * s + 2)
                    project(s, 0, u)

            def head(l, n, u, h, first, last_seq):
                if h < CA_H:
                    c, rows, b = h // 2, slice((h % 2) * CA_D, (h % 2 + 1) * CA_D), h % 2
                    q_f, k_f = qk[c % 2][rows, 0, :], qk[c % 2][rows, 1, :]
                    pe.wait_ge(S["exped"], C + n * CA_H + h - 1)
                    pe.wait_ge(S["qk_read"], C + n * HC + c + 1)
                    mm(bank(b)[:, 0:P], q_f[:, 0:P], k_f[:, 0:P], start=True, stop=False)
                    mm(bank(b)[:, 0:P], M.identb[:, :], M.mask_causal[:, :], start=False, stop=True)
                    mm(bank(b)[:, P:PW], q_f[:, P:TOK], k_f[:, :], start=True, stop=False, skip_group_check=True)
                    mm(bank(b)[:, 2 * P:PW], M.identb[:, :], M.mask_causal[:, :], start=False, stop=True, skip_group_check=True).then_inc(S["scored"], 1)
                    if h % 2 == 0 and c + 1 < HC:
                        project(n, c + 1, u)
                    if h == 0:
                        pe.wait_ge(S["v_copied"], C + 4 * n + 3)
                g = h - 1
                if 0 <= g < CA_H:
                    b, sig, read = (3, S["even_made"], S["even_read"]) if g % 2 == 0 else (4, S["odd_made"], S["odd_read"])
                    pe.wait_ge(S["exped"], C + n * CA_H + g + 1)
                    pe.wait_ge(read, C + n * HC + g // 2)
                    if g == 0:
                        pe.wait_ge(S["v_copied"], C + 4 * n + 4)
                    for t in range(3):
                        last = nc.tensor.transpose(bank(b)[:, t * P:(t + 1) * P], prob[g % 2][:, t * P:(t + 1) * P], M.ident[:, :])
                    last.then_inc(sig, 1)
                g = h - 2
                if 0 <= g < CA_H:
                    pe.wait_ge(S["even_read"] if g % 2 == 0 else S["odd_read"], C + n * HC + g // 2 + 1)
                    if g % 8 == 0:
                        pe.wait_ge(S["scaled"], C + 2 * n + g // 8)
                    cut, vc = slice((g % 8) * CA_D, (g % 8 + 1) * CA_D), slice(g * CA_D, (g + 1) * CA_D)
                    mm(bank(5)[:, cut], prob_t[g % 2][:, 0:P], v_tok[u][:, 0, vc], start=True, stop=True)
                    mm(bank(6)[:, cut], prob_t[g % 2][:, P:2 * P], v_tok[u][:, 0, vc], start=True, stop=False)
                    mm(bank(6)[:, cut], prob_t[g % 2][:, 2 * P:3 * P], v_tok[u][:, 1, vc], start=False, stop=True).then_inc(S["pv_made"], 1)

            def tail(l, s, u, h):
                if h < 4:
                    j, e = h // 2, h % 2
                    pe.wait_ge(S["scaled"], C + 2 * s + 2)
                    pe.wait_ge(S["o_read"], C + 4 * s + h)
                    if h == 0:
                        pe.wait_ge(S["logits_read"], C + s)
                    for c in range(4):
                        last = nc.tensor.transpose(bank(7)[:, c * P:(c + 1) * P], o[:, j, (4 * e + c) * P:(4 * e + c + 1) * P], M.ident[:, :])
                    last.then_inc(S["o_turned"], 1)
                if h == 4:
                    pe.wait_ge(S["o_read"], C + 4 * s + 4)
                    for j in range(TILES):
                        for c in range(HC):
                            last = mm(bank(7)[:, j * P:(j + 1) * P], o_fea[:, c, j * P:(j + 1) * P], M.c_wo[:, c, :], start=(c == 0), stop=(c == HC - 1))
                    last.then_inc(S["y_made"], 1)
                if h == 8:
                    pe.wait_ge(S["x3_ready"], C + s + 1)
                    for j in range(TILES):
                        last = nc.tensor.transpose(bank(7)[:, j * P:(j + 1) * P], x3[:, j, :], M.ident[:, :])
                    last.then_inc(S["x3_turned"], 1)
                if h == 9:
                    pe.wait_ge(S["x3_fea_ready"], C + s + 1)
                    for j in range(TILES):
                        last = mm(bank(7)[:, j * EXPERTS:(j + 1) * EXPERTS], x3_fea[:, j * P:(j + 1) * P], M.d_wr[:, :], start=True, stop=True)
                    last.then_inc(S["routed"], 1)

            over_sequences(pe, CA_H, LAG, pre, head, tail, 0)

        @block.scalar
        def _(act):
            before_start(act, "exped even_read z_rstd x2_fea_ready v_copied o_read r_rstd x3_fea_ready")
            a = nc.scalar.activation
            nc.scalar.preload_act_table_set(LN_EXP_SET)
            own = [Steps(act, S["own_ln"], 1), Steps(act, S["own_ln2"], 1)]

            def rsqrt(k, s, ready, sig):
                own[k].at(s)
                act.wait_ge(ready, C + s + 1)
                own[k].link(a(lnv[k][:, :], mv[k][:, :, 1], ACT.Ln, bias=M.eps[:, :]))
                a(rstd[k][:, :], lnv[k][:, :], ACT.Exp, scale=-0.5).then_inc(sig, 1)

            def pre(l, s, u, h, first):
                if h == 12:
                    rsqrt(0, s, S["z_var"], S["z_rstd"])
                if h == 14:
                    act.wait_ge(S["x2_turned"], C + s + 1)
                    a(x2_fea[u][:, :], bank(7)[:, 0:TOK], ACT.Copy).then_inc(S["x2_fea_ready"], 1)
                if h is None or h >= 15:
                    k = 3 if h is None else h - 15
                    j, e = k // 2, k % 2
                    act.wait_ge(S["v_made"], C + 4 * s + k + 1)
                    a(v_tok[u][:, j, e * HALF:(e + 1) * HALF], bank(V_BANKS[k]), ACT.Copy).then_inc(S["v_copied"], 1)

            def head(l, n, u, h, first, last_seq):
                if h < CA_H:
                    b = h % 2
                    act.wait_ge(S["neg_ready"], C + n * CA_H + h + 1)
                    act.wait_ge(S["pv_made"], C + n * CA_H + h - 2)
                    if h == 0:
                        act.wait_ge(S["scaled"], C + 2 * n - 2)
                    a(prob[b][:, 0:P], bank(b)[:, 0:P], ACT.Exp, bias=neg[b][:, 0:1], accum_out=row_sum[u][:, 0, h:h + 1])
                    a(prob[b][:, P:PW], bank(b)[:, P:PW], ACT.Exp, bias=neg[b][:, 1:2], accum_out=row_sum[u][:, 1, h:h + 1]).then_inc(S["exped"], 1)
                g = h - 1
                if 0 <= g < CA_H and g % 2 == 0:
                    act.wait_ge(S["even_made"], C + n * HC + g // 2 + 1)
                    act.wait_ge(S["pv_made"], C + n * CA_H + g - 1)
                    a(prob_t[0][:, :], bank(3)[:, 0:PW], ACT.Copy).then_inc(S["even_read"], 1)

            def tail(l, s, u, h):
                if h < 4:
                    j, e = h // 2, h % 2
                    act.wait_ge(S["o_turned"], C + 4 * s + h + 1)
                    if h == 0:
                        act.wait_ge(S["y_made"], C + s)
                    a(o_fea[:, 4 * e:4 * e + 4, j * P:(j + 1) * P], bank(7).rearrange("p (c n) -> p c n", c=4), ACT.Copy).then_inc(S["o_read"], 1)
                if h == 6:
                    rsqrt(1, s, S["r_var"], S["r_rstd"])
                if h == 8:
                    act.wait_ge(S["x3_turned"], C + s + 1)
                    act.wait_ge(S["stored"], C + 2 * s)
                    a(x3_fea[:, :], bank(7)[:, 0:TOK], ACT.Copy).then_inc(S["x3_fea_ready"], 1)

            over_sequences(act, CA_H, LAG, pre, head, tail, 0)

        @block.vector
        def _(dve):
            before_start(dve, "qk_read neg_ready odd_read scaled z_var x2_ready r_var x3_ready logits_read")
            v = nc.vector
            dve.wait_ge(M.loaded_c, M.LOADED_C)
            v.tensor_scalar(M.c_w[:, 0, :], M.c_w[:, 0, :], CA_D ** -0.5, None, ALU.mult).then_inc(S["wq_scaled"], 1)
            own_i, own_r = Steps(dve, S["own_inv"], 2), Steps(dve, S["own_r"], 1)
            own_s = [Steps(dve, S["own_st"], 3), Steps(dve, S["own_st2"], 3)]

            def stats(k, s, src, sig):
                own_s[k].at(s)
                for j in range(TILES):
                    place = own_s[k].done(v.bn_stats(st[k][:, j, :], src[:, j * P:(j + 1) * P]))
                own_s[k].wait_alone(place)
                v.bn_aggr(mv[k][:, 0, :], st[k][:, 0, :])
                v.bn_aggr(mv[k][:, 1, :], st[k][:, 1, :]).then_inc(sig, 1)

            def normed(k, out, src, sig):
                for j in range(TILES):
                    last = v.tensor_scalar(out[:, j, :], src[:, j * P:(j + 1) * P], mv[k][:, j, 0:1], rstd[k][:, j:j + 1], ALU.subtract, ALU.mult)
                last.then_inc(sig, 1)

            def take(n, c):
                dve.wait_ge(S["qk_made"], C + n * HC + c + 1)
                dve.wait_ge(S["scored"], C + n * CA_H + 2 * c - 2)
                v.tensor_copy(qk[c % 2][:, :, :], bank(2).rearrange("p (w t) -> p w t", w=2)).then_inc(S["qk_read"], 1)

            def pre(l, s, u, h, first):
                if h == 11:
                    dve.wait_ge(S["z_turned"], C + s + 1)
                    stats(0, s, bank(7), S["z_var"])
                if h == 13:
                    dve.wait_ge(S["z_rstd"], C + s + 1)
                    normed(0, x2[u], bank(7), S["x2_ready"])
                if h is None:
                    take(s, 0)

            def head(l, n, u, h, first, last_seq):
                if h in (10, CA_H + LAG - 1):
                    e = 0 if h == 10 else 1
                    own_i.at(n)
                    own_i.k = e
                    dve.wait_ge(S["exped"], C + n * CA_H + 8 * e + 8)
                    own_i.link(v.reciprocal(inv_sum[e][:, :, :], row_sum[u][:, :, 8 * e:8 * e + 8]))
                    dve.wait_ge(S["pv_made"], C + n * CA_H + 8 * e + 8)
                    dve.wait_ge(S["o_turned"], C + 4 * n)
                    for j in range(TILES):
                        last = v.tensor_tensor(o[:, j, e * HALF:(e + 1) * HALF].rearrange("p (h d) -> p h d", d=CA_D),
                                               bank(5 + j).rearrange("p (h d) -> p h d", d=CA_D), heads_wide(inv_sum[e][:, j, :], CA_D), ALU.mult)
                    last.then_inc(S["scaled"], 1)
                if h < CA_H:
                    b = h % 2
                    dve.wait_ge(S["scored"], C + n * CA_H + h + 1)
                    dve.wait_ge(S["exped"], C + n * CA_H + h - 1)
                    v.tensor_reduce(neg[b][:, 0:1], bank(b)[:, 0:P], AX, ALU.max, negate=True)
                    v.tensor_reduce(neg[b][:, 1:2], bank(b)[:, P:PW], AX, ALU.max, negate=True).then_inc(S["neg_ready"], 1)
                    if h % 2 == 0 and h // 2 + 1 < HC:
                        take(n, h // 2 + 1)
                g = h - 1
                if 0 <= g < CA_H and g % 2 == 1:
                    dve.wait_ge(S["odd_made"], C + n * HC + g // 2 + 1)
                    dve.wait_ge(S["pv_made"], C + n * CA_H + g - 1)
                    v.tensor_copy(prob_t[1][:, :], bank(4)[:, 0:PW]).then_inc(S["odd_read"], 1)

            def tail(l, s, u, h):
                if h == 5:
                    own_r.at(s)
                    dve.wait_ge(S["y_made"], C + s + 1)
                    own_r.link(v.tensor_tensor(r[:, :, :], bank(7)[:, 0:TOK].rearrange("p (j c) -> p j c", j=TILES), x2[u][:, :, :], ALU.add))
                    stats(1, s, r[:, :, :].rearrange("p j c -> p (j c)"), S["r_var"])
                if h == 7:
                    dve.wait_ge(S["r_rstd"], C + s + 1)
                    dve.wait_ge(S["stored"], C + 2 * s)
                    normed(1, x3, r[:, :, :].rearrange("p j c -> p (j c)"), S["x3_ready"])
                if h == 10:
                    dve.wait_ge(S["routed"], C + s + 1)
                    v.tensor_copy(M.logits[:, bass.ts(s, TILES), :], bank(7)[:, 0:TILES * EXPERTS].rearrange("p (j e) -> p j e", j=TILES)).then_inc(S["logits_read"], 1)

            over_sequences(dve, CA_H, LAG, pre, head, tail, 0)


def experts(nc, M, dram):
    ctx = ExitStack()
    with ctx:
        sb = lambda name, shape, dt=F32: ctx.enter_context(nc.sbuf_tensor(name, shape, dt))
        sem = lambda name: ctx.enter_context(nc.semaphore(name))
        KF = FFN // P
        TB = BLK // P
        TOP_BIT = 29
        EARLY = 2
        STEPS = 2
        SEARCH = STEPS * EARLY * EXPERTS
        wide = [P, NT, EXPERTS]
        row = lambda ap: ap.unsqueeze(2).broadcast_to(wide)
        col = lambda ap: ap.unsqueeze(1).broadcast_to(wide)
        by_expert = lambda ap: ap.rearrange("p t e -> p e t")
        t1 = [sb(f"d_row{k}", [P, NT]) for k in range(6)]
        prob, w_a, w_b = sb("d_prob", wide), sb("d_wa", wide), sb("d_wb", wide)
        first, second, gate_w = sb("d_first", wide), sb("d_second", wide), sb("d_gate", wide)
        order = sb("d_order", [P, EXPERTS])
        thr, cand, bit, take = (sb(f"d_{s}", [P, EXPERTS], I32) for s in ("thr", "cand", "bit", "take"))
        bit_f, count = sb("d_bit_f", [P, EXPERTS]), sb("d_count", [P, EXPERTS])
        room = sb("d_room", [P, EXPERTS])
        equal_b = sb("d_equal_b", wide, BF16)
        ones_b, before_b = sb("d_ones_b", [P, P], BF16), sb("d_before_b", [P, P], BF16)
        y_early = [M.d_w1[:, :, :].rearrange("p e (t c) -> p e t c", c=DIM),
                   sb("d_y_early", [P, EXPERTS, TB, DIM])]
        room_c = M.c_w[:, :, :].rearrange("p w c -> p (w c)")
        sum_early = [[room_c[:, (2 * b + p) * BLK:(2 * b + p + 1) * BLK].rearrange("p (t c) -> p t c", c=DIM) for p in range(2)]
                     for b in range(EARLY)]
        x_hi, x_lo = ([sb(f"d_x_{part}{p}", [P, BLK], F32R) for p in range(2)] for part in ("hi", "lo"))
        hid = [sb(f"d_hid{p}", [P, KF, BLK]) for p in range(2)]
        gates = sb("d_gates", wide)
        g_blk = [sb(f"d_g_blk{p}", [P, TB, EXPERTS]) for p in range(2)]
        acc = [sb(f"d_acc{p}", [P, TB, DIM]) for p in range(2)]
        total = [sb(f"d_total{p}", [P, TB, DIM]) for p in range(2)]
        res = [sb(f"d_res{p}", [P, TB, DIM]) for p in range(2)]
        st, mv = [sb(f"d_st{p}", [P, TB, 6]) for p in range(2)], [sb(f"d_mv{p}", [P, TB, 2]) for p in range(2)]
        lnv, rstd = [sb(f"d_lnv{p}", [P, TB]) for p in range(2)], [sb(f"d_rstd{p}", [P, TB]) for p in range(2)]

        MAIN = NBLK - EARLY
        STORE0 = 32
        names = ("shifted exped counted summed equal_ready ranked own h_made h_even h_odd y_made combined var rstd res_ready "
                 "x_high x_split early_h early_y early_gated gates_ready early_sum own_ln own_st own_fin loop spare").split()
        S = {}
        for name in names:
            S[name] = sem("d_" + name)
        stored = [sem(f"d_stored{u}") for u in range(2)]
        H0, Y0 = EARLY * EXPERTS * KF, EARLY * EXPERTS
        bank = M.bank
        block = ctx.enter_context(nc.Block())

        @block.sync
        def _(sp):
            out_v = dram["out"].rearrange("(b s) (j p) c -> b p (s j) c", s=BLK // TOK, p=P)
            with sp.Fori(0, MAIN // 2) as i:
                for u in range(2):
                    sp.wait_ge(S["res_ready"], C + i * 2 + u + 1)
                    sp.dma_start(out_v[bass.ds(i * 2 + u + EARLY, 1), :, :, :].rearrange("b p t c -> p (b t) c"), res[u][:, :, :]).then_inc(stored[u], 16)
            for b in range(EARLY):
                sp.wait_ge(S["res_ready"], C + MAIN + b + 1)
                sp.dma_start(out_v[b, :, :, :], res[b][:, :, :]).then_inc(stored[b], 16)
            for u in range(2):
                sp.wait_ge(stored[u], STORE0 + NBLK // 2 * 16)

        @block.tensor
        def _(pe):
            mm = nc.tensor.matmul
            pe.sem_inc(S["summed"], C)
            pe.wait_ge(M.loaded_d, M.LOADED_D)
            def hidden(out, e, k, u):
                w_hi, w_lo = (w[:, e, k * P:(k + 1) * P] for w in (M.d_w1_hi, M.d_w1_lo))
                mm(out, w_hi, x_lo[u][:, :], start=True, stop=False)
                mm(out, w_hi, x_hi[u][:, :], start=False, stop=False)
                return mm(out, w_lo, x_hi[u][:, :], start=False, stop=True)

            def up_early(b, e, chunks):
                for k in chunks:
                    if b or e:
                        pe.wait_ge(S["early_h"], KF * (b * EXPERTS + e - 1) + k + 1)
                    if k == 0 and e == 0:
                        pe.wait_ge(S["x_split"], C + b + 1)
                    hidden(bank(k), e, k, b % 2).then_inc(S["h_made"], 1)

            def down_early(b, e, tiles, done):
                g = b * EXPERTS + e
                if tiles[0] == 0:
                    pe.wait_ge(S["early_h"], KF * g + KF)
                    if g > 1:
                        pe.wait_ge(S["early_y"], g - 1)
                for t in tiles:
                    for k in range(KF):
                        last = mm(bank(4 + e % 2)[:, t * P:(t + 1) * P], hid[e % 2][:, k, t * P:(t + 1) * P], M.d_w2[:, e, k, :],
                                  start=(k == 0), stop=(k == KF - 1))
                if done:
                    last.then_inc(S["y_made"], 1)

            def count_step(k):
                pe.wait_ge(S["counted"], C + k + 1)
                mm(bank(6)[:, 0:EXPERTS], M.ones[:, :], count[:, :], start=True, stop=True).then_inc(S["summed"], 1)

            up_early(0, 0, range(KF))
            for b in range(EARLY):
                for e in range(EXPERTS):
                    for q in range(4):
                        if q < 2 and (b, e) != (EARLY - 1, EXPERTS - 1):
                            up_early(b + (e + 1) // EXPERTS, (e + 1) % EXPERTS, (2 * q, 2 * q + 1))
                        if q >= 2:
                            down_early(b, e, (2 * q - 4, 2 * q - 3), q == 3)
                        if q % 2 == 1:
                            count_step(STEPS * (b * EXPERTS + e) + q // 2)
            pe.wait_ge(S["equal_ready"], 1)
            mm(bank(6)[:, 0:EXPERTS], M.ones[:, :], count[:, :], start=True, stop=True)
            flat = lambda ap: ap.rearrange("p t e -> p (t e)")
            mm(bank(7)[:, 0:NT * EXPERTS], before_b[:, :], flat(equal_b[:, :, :]), start=True, stop=False)
            for t in range(NT - 1):
                last = mm(bank(7)[:, (t + 1) * EXPERTS:NT * EXPERTS], ones_b[:, :],
                          equal_b[:, t, :].unsqueeze(1).broadcast_to([P, NT - 1 - t, EXPERTS]), start=False, stop=(t == NT - 2))
            last.then_inc(S["ranked"], 1)
            pe.wait_ge(S["early_h"], EARLY * EXPERTS * KF)
            pe.wait_ge(S["early_y"], EARLY * EXPERTS)

            gate(pe, S["spare"])
            def main_block(b, u):
                def up(e):
                    g = b * EXPERTS + e
                    if e == 0:
                        pe.wait_ge(S["x_split"], C + EARLY + b + 1)
                    for k in range(KF):
                        pe.wait_ge(S["h_even"] if k % 2 == 0 else S["h_odd"], C + 2 * (g - 1) + k // 2 + 1)
                        hidden(bank(k), e, k, u).then_inc(S["h_made"], 1)

                def down(e):
                    g = b * EXPERTS + e
                    pe.wait_ge(S["h_even"], C + 2 * g + 2)
                    pe.wait_ge(S["h_odd"], C + 2 * g + 2)
                    pe.wait_ge(S["combined"], C + g - 1)
                    for t in range(TB):
                        for k in range(KF):
                            last = mm(bank(4 + e % 2)[:, t * P:(t + 1) * P], hid[e % 2][:, k, t * P:(t + 1) * P], M.d_w2[:, e, k, :],
                                      start=(k == 0), stop=(k == KF - 1))
                    last.then_inc(S["y_made"], 1)

                up(0)
                for e in range(1, EXPERTS):
                    up(e)
                    down(e - 1)
                down(EXPERTS - 1)

            with pe.Fori(0, MAIN // 2) as i:
                for u in range(2):
                    main_block(i * 2 + u, u)

        @block.scalar
        def _(act):
            a = nc.scalar.activation
            nc.scalar.preload_act_table_set(LN_EXP_SET)
            act.sem_inc(S["h_even"], C)
            act.sem_inc(S["rstd"], C)
            act.wait_ge(S["shifted"], 1)
            a(w_b[:, :, :], w_a[:, :, :], ACT.Exp).then_inc(S["exped"], 1)
            for g in range(EARLY * EXPERTS + 1):
                if g < EARLY * EXPERTS:
                    if g > 1:
                        act.wait_ge(S["y_made"], g - 1)
                    for k in range(KF):
                        act.wait_ge(S["h_made"], KF * g + k + 1)
                        a(hid[g % 2][:, k, :], bank(k), ACT.Relu).then_inc(S["early_h"], 1)
                if g > 0:
                    act.wait_ge(S["y_made"], g)
                    a(y_early[(g - 1) // EXPERTS][:, (g - 1) % EXPERTS, :, :].rearrange("p t c -> p (t c)"), bank(4 + (g - 1) % 2), ACT.Copy).then_inc(S["early_y"], 1)
            own = Steps(act, S["own_ln"], 1)
            def inverse_root(n, u):
                own.at(n)
                act.wait_ge(S["var"], C + n + 1)
                own.link(a(lnv[u][:, :], mv[u][:, :, 1], ACT.Ln, bias=M.eps[:, :]))
                a(rstd[u][:, :], lnv[u][:, :], ACT.Exp, scale=-0.5).then_inc(S["rstd"], 1)

            with act.Fori(0, MAIN // 2) as i:
                for u in range(2):
                    b = i * 2 + u
                    for e in range(EXPERTS):
                        g = b * EXPERTS + e
                        act.wait_ge(S["y_made"], Y0 + g - 1)
                        for k in (0, 2):
                            act.wait_ge(S["h_made"], H0 + KF * g + k + 1)
                            a(hid[e % 2][:, k, :], bank(k), ACT.Relu).then_inc(S["h_even"], 1)
                        if u == 1 and e == 3:
                            inverse_root(b - 1, 0)
                    if u == 1:
                        inverse_root(b, 1)
            for b in range(EARLY):
                inverse_root(MAIN + b, b)

        @block.vector
        def _(dve):
            v = nc.vector
            for s in (S["counted"], S["h_odd"], S["combined"], S["var"], S["res_ready"]):
                dve.sem_inc(s, C)
            for u in range(2):
                dve.sem_inc(stored[u], STORE0)
            own = Steps(dve, S["own"], 1000)
            own.at(0)
            own.link(v.tensor_reduce(t1[0][:, :], M.logits[:, :, :], AX, ALU.max))
            v.tensor_tensor(w_a[:, :, :], M.logits[:, :, :], row(t1[0][:, :]), ALU.subtract).then_inc(S["shifted"], 1)
            for e in range(EXPERTS):
                own.done(v.memset(order[:, e:e + 1], float(EXPERTS - e)))
            own.done(v.memset(thr[:, :], 0))
            own.done(v.memset(bit[:, :], 1 << TOP_BIT))
            own.done(v.memset(bit_f[:, :], float(1 << TOP_BIT)))
            dve.wait_ge(M.loaded_d, M.LOADED_D)
            own.done(v.tensor_copy(ones_b[:, :], M.ones[:, :]))
            own.done(v.tensor_copy(before_b[:, :], M.before[:, :]))
            dve.wait_ge(S["exped"], 1)
            own.link(v.tensor_reduce(t1[1][:, :], w_b[:, :, :], AX, ALU.add))
            own.link(v.reciprocal(t1[2][:, :], t1[1][:, :]))
            own.link(v.tensor_tensor(prob[:, :, :], w_b[:, :, :], row(t1[2][:, :]), ALU.mult))

            def pick(out, src, k):
                own.link(v.tensor_reduce(t1[k][:, :], src, AX, ALU.max))
                own.link(v.tensor_tensor(w_a[:, :, :], src, row(t1[k][:, :]), ALU.is_equal))
                own.link(v.tensor_tensor(w_a[:, :, :], w_a[:, :, :], col(order[:, :]), ALU.mult))
                own.link(v.tensor_reduce(t1[k + 1][:, :], w_a[:, :, :], AX, ALU.max))
                own.link(v.tensor_tensor(out, w_a[:, :, :], row(t1[k + 1][:, :]), ALU.is_equal))

            pick(first[:, :, :], prob[:, :, :], 2)
            own.link(v.scalar_tensor_tensor(w_b[:, :, :], first[:, :, :], -2.0, prob[:, :, :], ALU.mult, ALU.add))
            pick(second[:, :, :], w_b[:, :, :], 4)
            own.link(v.tensor_tensor(first[:, :, :], first[:, :, :], second[:, :, :], ALU.add))
            own.link(v.tensor_tensor(gate_w[:, :, :], prob[:, :, :], first[:, :, :], ALU.mult))

            loop = Steps(dve, S["loop"], 4)
            with dve.Fori(0, SEARCH // 4) as i:
                for q in range(4):
                    k = i * 4 + q
                    loop.at(k)
                    loop.link(v.tensor_tensor(cand[:, :], thr[:, :], bit[:, :], ALU.bitwise_or))
                    loop.link(v.tensor_tensor(w_a[:, :, :], gate_w[:, :, :], col(cand[:, :].bitcast(F32)), ALU.is_ge))
                    v.tensor_reduce(count[:, :], by_expert(w_a[:, :, :]), AX, ALU.add).then_inc(S["counted"], 1)
                    dve.wait_ge(S["summed"], C + k + 1)
                    v.tensor_single_scalar(bit[:, :], bit[:, :], 1, ALU.logical_shift_right)
                    loop.link(v.scalar_tensor_tensor(take[:, :], bank(6)[:, 0:EXPERTS], float(CAP), bit_f[:, :], ALU.is_ge, ALU.mult))
                    v.tensor_scalar(bit_f[:, :], bit_f[:, :], 0.5, None, ALU.mult)
                    loop.link(v.tensor_tensor(thr[:, :], thr[:, :], take[:, :], ALU.bitwise_or))
            thr_f = col(thr[:, :].bitcast(F32))
            own.link(v.tensor_tensor(w_a[:, :, :], gate_w[:, :, :], thr_f, ALU.is_gt))
            own.link(v.tensor_reduce(count[:, :], by_expert(w_a[:, :, :]), AX, ALU.add))
            v.tensor_tensor(equal_b[:, :, :], gate_w[:, :, :], thr_f, ALU.is_equal).then_inc(S["equal_ready"], 1)
            dve.wait_ge(S["ranked"], 1)
            own.link(v.tensor_scalar(room[:, :], bank(6)[:, 0:EXPERTS], -1.0, float(CAP), ALU.mult, ALU.add))
            own.link(v.tensor_tensor(w_b[:, :, :], bank(7)[:, 0:NT * EXPERTS].rearrange("p (t e) -> p t e", e=EXPERTS), col(room[:, :]), ALU.is_lt))
            own.link(v.tensor_tensor(w_b[:, :, :], w_b[:, :, :], equal_b[:, :, :], ALU.mult))
            own.link(v.tensor_tensor(w_b[:, :, :], w_b[:, :, :], w_a[:, :, :], ALU.add))
            v.tensor_tensor(gates[:, :, :], gate_w[:, :, :], w_b[:, :, :], ALU.mult).then_inc(S["gates_ready"], 1)
            dve.wait_ge(S["gates_ready"], 1)

            def statistics(n, fin, u):
                own_f.at(n)
                for t in range(TB):
                    place = own_f.done(v.bn_stats(st[u][:, t, :], fin[:, t, :]))
                own_f.wait_alone(place)
                for t in range(TB):
                    last = v.bn_aggr(mv[u][:, t, :], st[u][:, t, :])
                last.then_inc(S["var"], 1)

            def normalise(n, fin, u):
                dve.wait_ge(S["rstd"], C + n + 1)
                for t in range(TB):
                    last = v.tensor_scalar(res[u][:, t, :], fin[:, t, :], mv[u][:, t, 0:1], rstd[u][:, t:t + 1], ALU.subtract, ALU.mult)
                last.then_inc(S["res_ready"], 1)


            own_s, own_f = Steps(dve, S["own_st"], 1), Steps(dve, S["own_fin"], TB + 1)
            with dve.Fori(0, MAIN // 2) as i:
                for u in range(2):
                    b = i * 2 + u
                    own_s.at(b)
                    place = own_s.done(v.tensor_copy(g_blk[u][:, :, :], gates[:, bass.ds((b + EARLY) * TB, TB), :]))

                    def combine(e, place):
                        g = b * EXPERTS + e
                        dve.wait_ge(S["y_made"], Y0 + g + 1)
                        dve.wait_ge(S["combined"], C + g)
                        if e == 0:
                            own_s.wait(place)
                        out = acc[e % 2] if e < EXPERTS - 1 else total[u]
                        for t in range(TB):
                            before = M.xb[:, 1, bass.ds((b + EARLY) * BLK + t * P, P)] if e == 0 else acc[(e + 1) % 2][:, t, :]
                            last = v.scalar_tensor_tensor(out[:, t, :], bank(4 + e % 2)[:, t * P:(t + 1) * P], g_blk[u][:, t, e:e + 1],
                                                          before, ALU.mult, ALU.add)
                        last.then_inc(S["combined"], 1)

                    for e in range(EXPERTS):
                        g = b * EXPERTS + e
                        dve.wait_ge(S["y_made"], Y0 + g - 1)
                        for k in (1, 3):
                            dve.wait_ge(S["h_made"], H0 + KF * g + k + 1)
                            v.tensor_scalar(hid[e % 2][:, k, :], bank(k), 0.0, None, ALU.max).then_inc(S["h_odd"], 1)
                        if e:
                            combine(e - 1, place)
                        if u == 1 and e == 2:
                            statistics(b - 1, total[0], 0)
                        if u == 1 and e == 4:
                            dve.wait_ge(stored[0], STORE0 + 16 * i)
                            normalise(b - 1, total[0], 0)
                    combine(EXPERTS - 1, place)
                    dve.wait_ge(S["combined"], C + b * EXPERTS + EXPERTS)
                    if u == 1:
                        dve.wait_ge(stored[1], STORE0 + 16 * i)
                        statistics(b, total[1], 1)
                        normalise(b, total[1], 1)
            for b in range(EARLY):
                dve.wait_ge(S["early_sum"], (b + 1) * EXPERTS)
                dve.wait_ge(stored[b], STORE0 + 16 * (MAIN // 2))
                statistics(MAIN + b, sum_early[b][(EXPERTS - 1) % 2], b)
            for b in range(EARLY):
                normalise(MAIN + b, sum_early[b][(EXPERTS - 1) % 2], b)

        @block.gpsimd
        def _(pool):
            pool.sem_inc(S["x_high"], C)
            pool.sem_inc(S["x_split"], C)

            def split(n, x, u):
                gate(pool, S["spare"])
                nc.gpsimd.tensor_copy(x_hi[u][:, :], x).then_inc(S["x_high"], 1)
                pool.wait_ge(S["x_high"], C + n + 1)
                gate(pool, S["spare"])
                nc.gpsimd.tensor_tensor(x_lo[u][:, :], x, x_hi[u][:, :].bitcast(F32), ALU.subtract).then_inc(S["x_split"], 1)

            for b in range(EARLY):
                split(b, M.xb[:, 0, b * BLK:(b + 1) * BLK], b)
            with pool.Fori(0, MAIN // 2) as i:
                for u in range(2):
                    pool.wait_ge(S["h_made"], (i * 2 + u + 1) * EXPERTS * KF)
                    split(i * 2 + u + EARLY, M.xb[:, 0, bass.ds((i * 2 + u + EARLY) * BLK, BLK)], u)
            pool.wait_ge(S["gates_ready"], 1)
            pool.wait_ge(S["early_y"], EARLY * EXPERTS)
            for b in range(EARLY):
                for e in range(EXPERTS):
                    g = b * EXPERTS + e
                    y = y_early[b][:, e, :, :]
                    nc.gpsimd.tensor_tensor(y, y, gates[:, b * TB:(b + 1) * TB, e:e + 1].broadcast_to([P, TB, DIM]), ALU.mult).then_inc(S["early_gated"], 1)
                    pool.wait_ge(S["early_gated"], g + 1)
                    if g:
                        pool.wait_ge(S["early_sum"], g)
                    prior = M.xb[:, 1, b * BLK:(b + 1) * BLK].rearrange("p (t c) -> p t c", c=DIM) if e == 0 else sum_early[b][(e + 1) % 2][:, :, :]
                    nc.gpsimd.tensor_tensor(sum_early[b][e % 2][:, :, :], y, prior, ALU.add).then_inc(S["early_sum"], 1)


class Memory:
    pass


def program(nc, dram):
    ctx = ExitStack()
    with ctx:
        sb = lambda name, shape, dt=F32: ctx.enter_context(nc.sbuf_tensor(name, shape, dt))
        sem = lambda name: ctx.enter_context(nc.semaphore(name))
        M = Memory()
        M.psum = ctx.enter_context(nc.psum_tensor("banks", [P, 8, BANK], F32))
        M.bank = lambda b: M.psum[:, b, :]
        M.xb = sb("xb", [P, 2, SEQ * TOK])
        M.ident = sb("ident", [P, P])
        M.head_sum = sb("head_sum", [P, LA_H])
        M.state_mask = sb("state_mask", [P, P])
        M.eps = sb("eps", [P, 1])
        M.a_wkv = sb("a_wkv", [P, 4 * DIM])
        M.a_wq = sb("a_wq", [P, DIM])
        M.a_wo = sb("a_wo", [P, DIM])
        M.a_bkv = sb("a_bkv", [P, 4 * DIM])
        M.a_bo = sb("a_bo", [P, DIM])
        M.a_cols = sb("a_cols", [P, 3])
        M.a_bq, M.a_lng, M.a_lnb = (M.a_cols[:, k:k + 1] for k in range(3))
        M.masks = sb("masks", [P, 4 * P + WINDOW], BF16)
        masks = sb("masks32", [P, 4 * P + WINDOW])
        cuts = [0, P, 2 * P + WINDOW, 3 * P + WINDOW, 4 * P + WINDOW]
        M.mask_lo0, M.mask_lo1, M.mask_causal, M.identb = (M.masks[:, a:b] for a, b in zip(cuts, cuts[1:]))
        M.center, M.mean = sb("center", [P, P]), sb("mean", [P, P])
        M.rotary = sb("rotary", [P, 4, TILES, LO_D])
        M.b_wqkv = sb("b_wqkv", [P, LAYERS, 3 * LO_H * LO_D])
        M.b_wo = sb("b_wo", [P, LO_H * LO_D // P, DIM])
        M.b_w1 = sb("b_w1", [P, 2 * HID])
        M.b_w2 = sb("b_w2", [P, 3, DIM])
        M.b_cols = sb("b_cols", [P, 9])
        M.loaded_b, M.LOADED_B = sem("loaded_b"), 4 * 16
        M.c_w = sb("c_w", [P, 3, CA_H * CA_D])
        M.c_wo = sb("c_wo", [P, CA_H * CA_D // P, DIM])
        M.d_wr = sb("d_wr", [P, EXPERTS])
        M.ones = sb("ones", [P, P])
        M.before = sb("before", [P, P])
        M.logits = sb("logits", [P, NT, EXPERTS])
        M.loaded_c, M.LOADED_C = sem("loaded_c"), 4 * 16
        loaded_a, M.ready_a = sem("loaded_a"), sem("ready_a")
        M.READY_A = 4
        block = nc.Block()
        with block:
            @block.sync
            def _(sp):
                for dst, src in ((M.a_wkv[:, :], dram["a_wkv"]), (M.a_wq[:, :], dram["a_wq"]), (M.ident[:, :], dram["ident"]),
                                 (M.a_wo[:, :], dram["a_wo"]), (M.head_sum[:, :], dram["head_sum"]),
                                 (M.state_mask[:, :], dram["state_mask"]), (M.a_cols[:, :], dram["a_cols"]),
                                 (masks[:, :], dram["masks"]), (M.a_bkv[:, :], dram["a_bkv"].partition_broadcast(P)), (M.a_bo[:, :], dram["a_bo"].partition_broadcast(P))):
                    sp.dma_start(dst, src).then_inc(loaded_a, 16)
                for dst, src in ((M.b_wqkv[:, :, :], dram["b_wqkv"]), (M.rotary[:, :, :, :], dram["rotary"]),
                                 (M.center[:, :], dram["center"]), (M.mean[:, :], dram["mean"])):
                    sp.dma_start(dst, src).then_inc(M.loaded_b, 16)
                for dst, src in ((M.c_w[:, :, :], dram["c_w"]), (M.c_wo[:, :, :], dram["c_wo"]), (M.d_wr[:, :], dram["d_wr"]), (M.before[:, :], dram["before"])):
                    sp.dma_start(dst, src).then_inc(M.loaded_c, 16)

            @block.vector
            def _(dve):
                nc.vector.memset(M.eps[:, :], EPS).then_inc(M.ready_a, 1)
                dve.wait_ge(loaded_a, 10 * 16)
                nc.vector.tensor_tensor(M.a_wkv[:, :].rearrange("p (k c) -> p k c", k=4), M.a_wkv[:, :].rearrange("p (k c) -> p k c", k=4),
                                        M.ident[:, :].unsqueeze(1).broadcast_to([P, 4, DIM]), ALU.add).then_inc(M.ready_a, 1)
                nc.vector.tensor_copy(M.masks[:, :], masks[:, :]).then_inc(M.ready_a, 1)
                nc.vector.tensor_tensor(M.a_wq[:, :], M.a_wq[:, :], M.ident[:, :], ALU.add).then_inc(M.ready_a, 1)
        linear_attention(nc, M, dram)
        local_transformer(nc, M, dram)
        M.d_w1, M.d_w2 = sb("d_w1", [P, EXPERTS, FFN]), sb("d_w2", [P, EXPERTS, FFN // P, DIM])
        M.d_w1_hi, M.d_w1_lo = (sb(f"d_w1_{part}", [P, EXPERTS, FFN], F32R) for part in ("hi", "lo"))
        M.loaded_d, M.LOADED_D = sem("loaded_d"), 3 * 16
        M.d_loads = ((M.ones[:, 0:P], dram["ones"]), (M.d_w1[:, :, :], dram["d_w1"]), (M.d_w2[:, :, :, :], dram["d_w2"]))
        causal_attention(nc, M, dram)
        experts(nc, M, dram)

def later_arrays(g, T):
    import numpy as np
    swap = lambda a: np.roll(a, LO_D // 2, -1)
    def by_cut(a, rows):
        out = np.zeros((len(a), P, 3) + a.shape[2:], a.dtype)
        for k, (off, w) in enumerate(HID_CUT):
            out[:, :w, k] = a[:, off:off + w]
        return out
    b1 = g["L0_ffn_b1"]
    cols = np.concatenate([g["L0_ffn_ln_g"][:, :, None], g["L0_ffn_ln_b"][:, :, None], g["L0_ffn_b2"][:, :, None],
                           by_cut(b1[:, HID:], 0), by_cut(b1[:, :HID], 0)], 2)
    qs, ks = g["L0_ffn_q_scale"], g["L0_ffn_k_scale"]
    chunked = lambda a: a.reshape(a.shape[:-2] + (-1, P, a.shape[-1])).swapaxes(-3, -2)
    return {
        "b_wqkv": g["L0_ffn_wqkv"].transpose(1, 0, 2),
        "b_table_scale": np.stack([qs, swap(qs), ks, swap(ks)], 1),
        "b_wo": chunked(g["L0_ffn_wo"]),
        "b_w1": g["L0_ffn_w1"],
        "b_w2": by_cut(g["L0_ffn_w2"], 0),
        "b_cols": cols,
        "c_w": np.stack([g[k].reshape(-1, DIM).T for k in ("L1_attn_w_q", "L1_attn_w_k", "L1_attn_w_v")], 1),
        "c_wo": chunked(g["L1_attn_w_o"]),
        "d_wr": g["L1_ffn_Wr"],
        "d_w1": g["L1_ffn_W1"].transpose(1, 0, 2),
        "d_w2": g["L1_ffn_W2"].reshape(EXPERTS, FFN // P, P, DIM).transpose(2, 0, 1, 3),
    }


def constants():
    import numpy as np
    d = np.arange(P)
    tri = lambda keep: np.where(keep, 0.0, -1e30).astype(np.float32)
    half = np.arange(0, LO_D, 2, dtype=np.float64)
    freq = np.arange(TOK)[:, None] * (1.0 / 10000.0 ** (half / LO_D))[None, :]
    base = (half + 0.4 * LO_D) / (1.4 * LO_D)
    scale = base[None, :] ** ((np.arange(TOK) - TOK // 2) / float(WINDOW // 2))[:, None]
    two = lambda a: np.concatenate([a, a], 1)
    sin = np.concatenate([-np.sin(freq), np.sin(freq)], 1)
    rotary = np.stack([two(np.cos(freq) * scale), sin * two(scale), two(np.cos(freq) / scale), sin / two(scale)], 1)
    rotary = rotary.reshape(TILES, P, 4, LO_D).transpose(1, 2, 0, 3)
    q_at, k_at = d[:, None], d[None, :]
    k_wide = np.arange(P + WINDOW)[None, :]
    return {
        "ident": np.eye(P, dtype=np.float32),
        "head_sum": (d[:, None] // LA_D == np.arange(LA_H)[None, :]).astype(np.float32),
        "state_mask": (d[:, None] // LA_D == d[None, :] // LA_D).astype(np.float32) / TOK ** 2,
        "rotary": rotary.astype(np.float32),
        "center": (np.eye(P) - 1.0 / P).astype(np.float32),
        "mean": np.full((P, P), 1.0 / P, np.float32),
        "ones": np.ones((P, P), np.float32),
        "before": (d[:, None] < d[None, :]).astype(np.float32),
        "masks": np.concatenate([tri((k_at <= q_at) & (k_at >= q_at - WINDOW)), tri((k_wide >= q_at) & (k_wide <= q_at + WINDOW)),
                                 tri(k_at <= q_at), np.eye(P, dtype=np.float32)], 1),
    }


def kernel(**inputs):
    import numpy as np
    import concourse.bacc as bacc
    from concourse.bass_utils import run_bass_kernel_spmd as run

    g = {k: np.asarray(v) for k, v in inputs.items()}
    x = g["L0_attn_x"]
    T = lambda a: np.ascontiguousarray(np.swapaxes(a, -1, -2))
    arrays = {
        "x": x,
        "x_fea": T(x.reshape(SEQ * TOK, DIM)),
        "a_wkv": np.concatenate([T(g["L0_attn_Wk"][0]), T(g["L0_attn_Wk"][1]), T(g["L0_attn_Wv"][0]), T(g["L0_attn_Wv"][1])], 1),
        "a_wq": T(g["L0_attn_Wq"]),
        "a_wo": T(g["L0_attn_Wo"]),
        "a_cols": np.stack([g["L0_attn_bq"], g["L0_attn_ln_g"], g["L0_attn_ln_b"]], 1),
        "a_bkv": np.concatenate([g["L0_attn_bk"].reshape(-1), g["L0_attn_bv"].reshape(-1)]),
        "a_bo": g["L0_attn_bo"],
    }
    arrays.update(constants())
    arrays.update(later_arrays(g, T))
    arrays = {k: np.ascontiguousarray(v) for k, v in arrays.items()}
    nc = bacc.Bacc("TRN2", target_bir_lowering=False, num_devices=1)
    dram = {}
    for name, a in arrays.items():
        dram[name] = nc.dram_tensor("in_" + name, a.shape, mybir.dt.from_np(a.dtype), kind="ExternalInput").ap()
    dram["out"] = nc.dram_tensor("out_x", x.shape, F32, kind="ExternalOutput").ap()
    program(nc, dram)
    return run(nc, [{"in_" + k: a for k, a in arrays.items()}], core_ids=[0]).results[0]["out_x"]
```

```python
from contextlib import ExitStack

import concourse.bass as bass
from concourse import mybir

F32 = mybir.dt.float32
F32R = mybir.dt.float32r
BF16 = mybir.dt.bfloat16
I32 = mybir.dt.int32
ACT = mybir.ActivationFunctionType
ALU = mybir.AluOpType
AX = mybir.AxisListType.X

P = 128
BANK = 512
C = 6
SEQ, TOK, DIM = 16, 256, 128
TILES = TOK // P
EPS = 1e-5
SILU_SET, LN_EXP_SET, GELU_SET = "silu_and_others", "natural_log_exp_and_others", "gelu_and_others"

LA_H, LA_D = 16, 8
LO_H, LO_D, LAYERS = 8, 64, 2
WINDOW = 64
HID = DIM * 4 * 2 // 3
HID_CUT = [(0, 128), (128, 128), (256, HID - 256)]
CA_H, CA_D = 16, 64
EXPERTS, FFN, CAP = 8, 512, 1280
BLK = 512
NBLK = SEQ * TOK // BLK
NT = SEQ * TILES


class Steps:

    def __init__(self, eng, sem, per_round):
        self.eng, self.sem, self.per, self.k = eng, sem, per_round, 0

    def at(self, rounds):
        self.before, self.k = rounds * self.per, 0

    def done(self, ins):
        ins.then_inc(self.sem, 1)
        self.k += 1
        assert self.k <= self.per, "more steps in a round than per_round says"
        return self.k

    def wait(self, place):
        self.eng.wait_ge(self.sem, self.before + place)

    def wait_alone(self, place):
        self.eng.wait_ge(self.sem, self.before + place)
        self.eng.sem_inc(self.sem, 1)
        self.k += 1

    def link(self, ins):
        self.wait(self.done(ins))


def gate(eng, spare):
    eng.sem_inc(spare, 1)


def heads_wide(ap, width):
    return ap.unsqueeze(len(ap.shape)).broadcast_to(list(ap.shape) + [width])


def over_pairs(eng, stages):
    PAIRS = SEQ // 2

    def both(i, first_ones, last_ones):
        for is_last, stage in stages:
            if is_last and last_ones:
                for u in range(2):
                    stage(i - 1, 2 * (i - 1) + u, u)
            if not is_last and first_ones:
                for u in range(2):
                    stage(i, 2 * i + u, u)
    both(0, True, False)
    with eng.Fori(0, PAIRS - 1) as k:
        both(k + 1, True, True)
    both(PAIRS, False, True)


def linear_attention(nc, M, dram):
    ctx = ExitStack()
    with ctx:
        sb = lambda name, shape, dt=F32: ctx.enter_context(nc.sbuf_tensor(name, shape, dt))
        sem = lambda name: ctx.enter_context(nc.semaphore(name))
        HALF = LA_H * 2 * LA_D
        x_tok = [sb(f"x_tok{u}", [P, TILES, DIM]) for u in range(2)]
        x_fea = [sb(f"x_fea{u}", [P, TOK]) for u in range(2)]
        kv = [sb(f"kv{u}", [P, TILES, 2 * HALF]) for u in range(2)]
        q = [sb(f"q{u}", [P, TOK]) for u in range(2)]
        k_sq = [sb(f"k_sq{u}", [P, TILES, HALF]) for u in range(2)]
        q_sq = [sb(f"q_sq{u}", [P, TOK]) for u in range(2)]
        norm = [sb(f"norm{u}", [P, TILES, 3 * LA_H]) for u in range(2)]
        inv = [sb(f"inv{u}", [P, TILES, 3 * LA_H]) for u in range(2)]
        state0 = [sb(f"state0{u}", [P, P]) for u in range(2)]
        state = [sb(f"state{u}", [P, P]) for u in range(2)]
        o = [sb(f"o{u}", [P, TILES, DIM]) for u in range(2)]
        on = [sb(f"on{u}", [P, TILES, DIM]) for u in range(2)]
        o_fea = [sb(f"o_fea{u}", [P, TOK]) for u in range(2)]
        r = [sb(f"r{u}", [P, TILES, DIM]) for u in range(2)]
        st = [sb(f"stats{u}", [P, TILES, 6]) for u in range(2)]
        mv = [sb(f"mv{u}", [P, TILES, 2]) for u in range(2)]
        lnv = [sb(f"lnv{u}", [P, TILES]) for u in range(2)]
        rstd = [sb(f"rstd{u}", [P, TILES]) for u in range(2)]

        x_fea_loaded, x_tok_loaded = ([sem(f"a_x_{k}_loaded{u}") for u in range(2)] for k in ("fea", "tok"))
        kv_made, q_made, kv_biased = sem("a_kv_made"), sem("a_q_made"), sem("a_kv_biased")
        k_silu, q_silu, halves = sem("a_k_silu"), sem("a_q_silu"), sem("a_halves_added")
        squares, q_norm2, k_norm2 = sem("a_squares"), sem("a_q_norm2"), sem("a_k_norm2")
        norms, k_scaled, states, state_ready = sem("a_norms"), sem("a_k_scaled"), sem("a_states"), sem("a_state_ready")
        out_made, o_var, o_rstd, o_normed = sem("a_out_made"), sem("a_o_var"), sem("a_o_rstd"), sem("a_o_normed")
        o_turned, o_fea_ready, f_made = sem("a_o_turned"), sem("a_o_fea_ready"), sem("a_f_made")
        r_var, r_rstd, x1_ready, x1_turned = sem("a_r_var"), sem("a_r_rstd"), sem("a_x1_ready"), sem("a_x1_turned")
        x1_stored = sem("a_x1_stored")
        biased, spare = sem("a_biased"), sem("a_spare")
        own_v = [sem(f"a_vector_steps{k}") for k in range(4)]
        own_a = [sem(f"a_scalar_steps{k}") for k in range(3)]
        K0 = lambda u: 2 * u
        X = lambda u: 4 + u
        Y = lambda u: 6 + u
        bank = M.bank
        block = ctx.enter_context(nc.Block())

        @block.sync
        def _(sp):
            xf_v = dram["x_fea"].rearrange("c (s t) -> s c t", t=TOK)
            xt_v = dram["x"].rearrange("s (j p) c -> s p j c", p=P)
            with sp.Fori(0, SEQ // 2) as i:
                for u in range(2):
                    n = i * 2 + u
                    sp.wait_ge(kv_made, C + n - 1)
                    sp.dma_start(x_fea[u][:, :], xf_v[n, :, :]).then_inc(x_fea_loaded[u], 16)
                for u in range(2):
                    n = i * 2 + u
                    sp.wait_ge(x1_ready, C + n - 1)
                    sp.dma_start(x_tok[u][:, :, :], xt_v[n, :, :, :]).then_inc(x_tok_loaded[u], 16)

        @block.gpsimd
        def _(pool):
            pool.sem_inc(biased, C)
            pool.wait_ge(M.ready_a, M.READY_A)
            gate(pool, spare)
            with pool.Fori(0, SEQ // 2) as i:
                for u in range(2):
                    pool.wait_ge(x_tok_loaded[u], i * 16 + 16)
                    gate(pool, spare)
                    nc.gpsimd.tensor_tensor(x_tok[u][:, :, :], x_tok[u][:, :, :], M.a_bo[:, :].unsqueeze(1).broadcast_to([P, TILES, DIM]), ALU.add).then_inc(biased, 1)

        @block.tensor
        def _(pe):
            for s in (kv_made, q_made, q_norm2, states, out_made, o_turned, f_made, x1_turned):
                pe.sem_inc(s, C)
            pe.wait_ge(M.ready_a, M.READY_A)
            mm = nc.tensor.matmul

            def project(i, n, u):
                pe.wait_ge(x_fea_loaded[u], i * 16 + 16)
                mm(bank(X(u))[:, 0:TOK], M.a_wq[:, :], x_fea[u][:, :], start=True, stop=True).then_inc(q_made, 1)
                pe.wait_ge(norms, C + n - 1)
                for j in range(TILES):
                    last = mm(bank(K0(u) + j), x_fea[u][:, j * P:(j + 1) * P], M.a_wkv[:, :], start=True, stop=True)
                last.then_inc(kv_made, 1)

            def turn_o(i, n, u):
                pe.wait_ge(o_normed, C + n + 1)
                for j in range(TILES):
                    last = nc.tensor.transpose(bank(Y(u))[:, j * P:(j + 1) * P], on[u][:, j, :], M.ident[:, :])
                last.then_inc(o_turned, 1)

            def query_norms(i, n, u):
                pe.wait_ge(squares, C + 2 * n + 2)
                for j in range(TILES):
                    last = mm(bank(K0(u))[:, j * LA_H:(j + 1) * LA_H], q_sq[u][:, j * P:(j + 1) * P], M.head_sum[:, :],
                              start=True, stop=True)
                last.then_inc(q_norm2, 1)

            def project_o(i, n, u):
                pe.wait_ge(o_fea_ready, C + n + 1)
                for j in range(TILES):
                    last = mm(bank(Y(u))[:, j * P:(j + 1) * P], o_fea[u][:, j * P:(j + 1) * P], M.a_wo[:, :], start=True, stop=True)
                last.then_inc(f_made, 1)

            def make_states(i, n, u):
                pe.wait_ge(k_scaled, C + n + 1)
                for k in range(2):
                    for j in range(TILES):
                        last = mm(bank(X(u))[:, k * P:(k + 1) * P], kv[u][:, j, k * P:(k + 1) * P],
                                  kv[u][:, j, HALF + k * P:HALF + (k + 1) * P], start=(j == 0), stop=(j == TILES - 1))
                last.then_inc(states, 1)

            def turn_x1(i, n, u):
                pe.wait_ge(x1_ready, C + n + 1)
                for j in range(TILES):
                    last = nc.tensor.transpose(bank(Y(u))[:, j * P:(j + 1) * P], r[u][:, j, :], M.ident[:, :])
                last.then_inc(x1_turned, 1)

            def read_states(i, n, u):
                pe.wait_ge(state_ready, C + n + 1)
                pe.wait_ge(x1_stored, C + n - 1)
                for j in range(TILES):
                    last = mm(bank(Y(u))[:, j * P:(j + 1) * P], q[u][:, j * P:(j + 1) * P], state[u][:, :], start=True, stop=True)
                last.then_inc(out_made, 1)

            over_pairs(pe, ((False, project), (True, turn_o), (False, query_norms), (True, project_o), (False, make_states),
                            (True, turn_x1), (False, read_states)))

        @block.scalar
        def _(act):
            for s in (k_silu, q_silu, squares, norms, o_rstd, r_rstd, x1_stored):
                act.sem_inc(s, C)
            a = nc.scalar.activation
            own, own_o, own_r = (Steps(act, x, k) for x, k in zip(own_a, (2, 1, 1)))
            nc.scalar.preload_act_table_set(SILU_SET)

            def root(steps, out_sem, n, u, ready):
                steps.at(n)
                act.wait_ge(ready, C + n + 1)
                steps.link(a(lnv[u][:, :], mv[u][:, :, 1], ACT.Ln, bias=M.eps[:, :]))
                a(rstd[u][:, :], lnv[u][:, :], ACT.Exp, scale=-0.5).then_inc(out_sem, 1)

            def silus(i, n, u):
                if u == 0:
                    nc.scalar.preload_act_table_set(SILU_SET)
                act.wait_ge(q_made, C + n + 1)
                act.wait_ge(out_made, C + n - 1)
                a(q[u][:, :], bank(X(u))[:, 0:TOK], ACT.Silu, bias=M.a_bq[:, :]).then_inc(q_silu, 1)
                act.wait_ge(kv_biased, C + n + 1)
                a(kv[u][:, :, 0:HALF], kv[u][:, :, 0:HALF], ACT.Silu).then_inc(k_silu, 1)
                if u == 1:
                    nc.scalar.preload_act_table_set(LN_EXP_SET)

            def make_squares(i, n, u):
                act.wait_ge(halves, C + 2 * n + 2)
                act.wait_ge(k_norm2, C + n - 1)
                act.wait_ge(q_norm2, C + n - 1)
                a(k_sq[u][:, :, :], kv[u][:, :, 0:HALF], ACT.Square).then_inc(squares, 1)
                a(q_sq[u][:, :], q[u][:, :], ACT.Square).then_inc(squares, 1)

            def roots_of_norms(i, n, u):
                act.wait_ge(k_norm2, C + n + 1)
                act.wait_ge(q_norm2, C + n + 1)
                own.at(n)
                own.done(a(norm[u][:, :, 0:2 * LA_H], norm[u][:, :, 0:2 * LA_H], ACT.Ln))
                second = own.done(a(norm[u][:, :, 2 * LA_H:], bank(K0(u))[:, 0:TILES * LA_H].rearrange("p (j h) -> p j h", j=TILES), ACT.Ln))
                own.wait(second)
                a(norm[u][:, :, :], norm[u][:, :, :], ACT.Exp, scale=0.5).then_inc(norms, 1)

            def store_x1(i, n, u):
                act.wait_ge(x1_turned, C + n + 1)
                a(M.xb[:, 0, bass.ts(n, TOK)], bank(Y(u))[:, 0:TOK], ACT.Copy).then_inc(x1_stored, 1)

            over_pairs(act, ((False, silus), (False, make_squares), (False, roots_of_norms), (True, lambda i, n, u: root(own_r, r_rstd, n, u, r_var)),
                             (True, store_x1), (False, lambda i, n, u: root(own_o, o_rstd, n, u, o_var))))

        @block.vector
        def _(dve):
            for s in (kv_biased, halves, k_norm2, k_scaled, state_ready, o_var, o_normed, o_fea_ready, r_var, x1_ready):
                dve.sem_inc(s, C)
            v = nc.vector
            own, own_s, own_o, own_r = (Steps(dve, x, k) for x, k in zip(own_v, (2, 1, 5, 4)))

            def stats(steps, src, u, sig):
                for j in range(TILES):
                    place = steps.done(v.bn_stats(st[u][:, j, :], src[:, j, :]))
                steps.wait_alone(place)
                v.bn_aggr(mv[u][:, 0, :], st[u][:, 0, :])
                v.bn_aggr(mv[u][:, 1, :], st[u][:, 1, :]).then_inc(sig, 1)

            def normed(out, src, u, sig):
                for j in range(TILES):
                    last = v.tensor_scalar(out[:, j, :], src[:, j, :], mv[u][:, j, 0:1], rstd[u][:, j:j + 1], ALU.subtract, ALU.mult)
                last.then_inc(sig, 1)

            def add_bias(i, n, u):
                dve.wait_ge(kv_made, C + n + 1)
                dve.wait_ge(states, C + n - 1)
                v.tensor_tensor(kv[u][:, :, :], M.psum[:, K0(u):K0(u) + 2, :],
                                M.a_bkv[:, :].unsqueeze(1).broadcast_to([P, 2, 2 * HALF]), ALU.add).then_inc(kv_biased, 1)

            def normalise_o(i, n, u):
                dve.wait_ge(o_rstd, C + n + 1)
                normed(on[u], o[u], u, o_normed)

            def add_halves(i, n, u):
                dve.wait_ge(q_silu, C + n + 1)
                v.tensor_scalar(q[u][:, :], q[u][:, :], 0.5, None, ALU.add).then_inc(halves, 1)
                dve.wait_ge(k_silu, C + n + 1)
                v.tensor_scalar(kv[u][:, :, 0:HALF], kv[u][:, :, 0:HALF], 0.5, None, ALU.add).then_inc(halves, 1)

            def gain_and_bias(i, n, u):
                dve.wait_ge(o_turned, C + n + 1)
                v.tensor_scalar(o_fea[u][:, :], bank(Y(u))[:, 0:TOK], M.a_lng[:, :], M.a_lnb[:, :], ALU.mult, ALU.add).then_inc(o_fea_ready, 1)

            def key_norms(i, n, u):
                dve.wait_ge(squares, C + 2 * n + 1)
                for j in range(TILES):
                    last = v.tensor_reduce(norm[u][:, j, 0:2 * LA_H], k_sq[u][:, j, :].rearrange("p (h d) -> p h d", d=LA_D), AX, ALU.add)
                last.then_inc(k_norm2, 1)

            def residual(i, n, u):
                own_r.at(n)
                dve.wait_ge(f_made, C + n + 1)
                dve.wait_ge(biased, C + n + 1)
                own_r.link(v.tensor_tensor(r[u][:, :, :], bank(Y(u))[:, 0:TOK].rearrange("p (j c) -> p j c", j=TILES), x_tok[u][:, :, :], ALU.add))
                stats(own_r, r[u], u, r_var)

            def scale_keys(i, n, u):
                own.at(n)
                dve.wait_ge(norms, C + n + 1)
                own.link(v.tensor_scalar(norm[u][:, :, :], norm[u][:, :, :], 1e-6, None, ALU.add))
                own.link(v.reciprocal(inv[u][:, :, :], norm[u][:, :, :]))
                for j in range(TILES):
                    k_v = kv[u][:, j, 0:HALF].rearrange("p (h d) -> p h d", d=LA_D)
                    last = v.tensor_tensor(k_v, k_v, heads_wide(inv[u][:, j, 0:2 * LA_H], LA_D), ALU.mult)
                last.then_inc(k_scaled, 1)

            def normalise_r(i, n, u):
                dve.wait_ge(r_rstd, C + n + 1)
                normed(r[u], r[u], u, x1_ready)

            def multiply_states(i, n, u):
                own_s.at(n)
                dve.wait_ge(states, C + n + 1)
                own_s.link(v.tensor_tensor(state0[u][:, :], bank(X(u))[:, 0:P], M.state_mask[:, :], ALU.mult))
                v.tensor_tensor(state[u][:, :], bank(X(u))[:, P:2 * P], state0[u][:, :], ALU.mult).then_inc(state_ready, 1)

            def scale_output(i, n, u):
                own_o.at(n)
                dve.wait_ge(out_made, C + n + 1)
                for j in range(TILES):
                    place = own_o.done(v.tensor_tensor(o[u][:, j, :].rearrange("p (h d) -> p h d", d=LA_D),
                                                       bank(Y(u))[:, j * P:(j + 1) * P].rearrange("p (h d) -> p h d", d=LA_D),
                                                       heads_wide(inv[u][:, j, 2 * LA_H:], LA_D), ALU.mult))
                own_o.wait(place)
                stats(own_o, o[u], u, o_var)

            over_pairs(dve, ((False, add_bias), (True, normalise_o), (False, add_halves), (True, gain_and_bias), (False, key_norms),
                             (True, residual), (False, scale_keys), (True, normalise_r), (False, multiply_states), (False, scale_output)))


class Channel:

    def __init__(self, eng, filled, read):
        self.eng, self.filled, self.read = eng, filled, read

    def at(self, uses):
        self.uses = uses

    def filling(self):
        self.eng.wait_ge(self.read, C + self.uses)
        self.uses = self.uses + 1

    def reading(self):
        self.uses = self.uses + 1
        self.eng.wait_ge(self.filled, C + self.uses)


def over_sequences(eng, heads, lag, pre, head, tail, layer=0):
    def body(s, u, first=False, last=False):
        for h in range(heads + lag):
            head(layer, s, u, h, first, last)
            if not first:
                tail(layer, s - 1, 1 - u, h)
            if not last:
                pre(layer, s + 1, 1 - u, h, first)
        if not last:
            pre(layer, s + 1, 1 - u, None, first)
    for h in list(range(heads + lag)) + [None]:
        pre(layer, 0, 0, h, None)
    body(0, 0, first=True)
    with eng.Fori(0, SEQ // 2 - 1) as i:
        body(2 * i + 1, 1)
        body(2 * i + 2, 0)
    body(SEQ - 1, 1, last=True)
    for h in range(heads + lag):
        tail(layer, SEQ - 1, 1, h)


def over_local(eng, early, pre, step, after, tail, drain, layer):
    def body(s, u, first=False, last=False):
        for h in range(LO_H):
            if not last:
                early(layer, s + 1, 1 - u, h, first)
            step(layer, s, u, h, first)
            after(layer, s, u, h, first)
            if not first:
                tail(layer, s - 1, 1 - u, h)
            if not last:
                pre(layer, s + 1, 1 - u, h, first)
    for h in range(LO_H):
        early(layer, 0, 0, h, None)
        pre(layer, 0, 0, h, None)
    body(0, 0, first=True)
    with eng.Fori(0, SEQ // 2 - 1) as i:
        body(2 * i + 1, 1)
        body(2 * i + 2, 0)
    body(SEQ - 1, 1, last=True)
    drain(layer, SEQ - 1, 1)
    for h in range(LO_H):
        tail(layer, SEQ - 1, 1, h)


def local_transformer(nc, M, dram):
    ctx = ExitStack()
    with ctx:
        sb = lambda name, shape, dt=F32: ctx.enter_context(nc.sbuf_tensor(name, shape, dt))
        sem = lambda name: ctx.enter_context(nc.semaphore(name))
        INNER = LO_H * LO_D
        CH = INNER // P
        S1 = P + WINDOW
        PW = P + TOK
        tables = sb("b_tables", [P, LAYERS, 4, TILES, LO_D])
        table_scale = sb("b_table_scale", [P, LAYERS, 4, LO_D])
        h_fea = [sb(f"b_h{u}", [P, TOK]) for u in range(2)]
        sq = sb("b_sq", [P, 2 * INNER])
        ss = sb("b_ss", [P, 2 * LO_H])
        ln_ss = sb("b_ln_ss", [P, 2 * LO_H])
        root = sb("b_root", [P, 2 * LO_H])
        q_scale = [sb(f"b_q_scale{u}", [P, TILES, LO_H]) for u in range(2)]
        k_scale = sb("b_k_scale", [P, LO_H])
        k_unit = sb("b_k_unit", [P, INNER])
        rot = sb("b_rot", [P, 4 * TILES, INNER])
        rot_q, rot_k = ([rot[:, (2 * w + j) * 2:(2 * w + j) * 2 + 2, :] for j in range(TILES)] for w in range(2))
        v_tok = [sb(f"b_v{u}", [P, TILES, INNER]) for u in range(2)]
        q_fea = [sb(f"b_q_fea{u}", [P, CH, TOK]) for u in range(2)]
        k_fea = [sb(f"b_k_fea{u}", [P, CH, TOK]) for u in range(2)]
        mx = [sb(f"b_mx{p}", [P, TILES]) for p in range(4)]
        neg = [sb(f"b_neg{p}", [P, TILES]) for p in range(4)]
        prob = [sb(f"b_prob{p}", [P, PW]) for p in range(4)]
        prob_t = [sb(f"b_prob_t{p}", [P, PW]) for p in range(2)]
        row_sum = [sb(f"b_row_sum{u}", [P, TILES, LO_H]) for u in range(2)]
        inv_sum = [sb(f"b_inv_sum{e}", [P, TILES, LO_H // 2]) for e in range(2)]
        o = sb("b_o", [P, TILES, INNER])
        o_fea = sb("b_o_fea", [P, CH, TOK])
        c_sq = [sb(f"b_csq{u}", [P, BLK]) for u in range(2)]
        lnv = [sb(f"b_lnv{k}", [P, BLK]) for k in range(4)]
        hid = [sb(f"b_hid{k}", [P, BLK]) for k in range(3)]
        gelu, rstd = lnv[:3], hid + [sb("b_rstd", [P, BLK])]
        hn = rot[:, :, :].rearrange("p w n -> p (w n)")
        wo, w1, w2, cols = M.b_wo, M.b_w1, M.b_w2, M.b_cols

        tables_ready, table_loaded = sem("b_tables_ready"), sem("b_table_loaded")
        h_ready, qk_made, v_made = sem("b_h_ready"), sem("b_qk_made"), sem("b_v_made")
        squared, summed, rooted, v_copied = sem("b_squared"), sem("b_summed"), sem("b_rooted"), sem("b_v_copied")
        k_unit_ready, q_rotated, k_rotated = sem("b_k_unit_ready"), sem("b_q_rotated"), sem("b_k_rotated")
        five_filled, five_read = sem("b_five_filled"), sem("b_five_read")
        two_filled, two_read = sem("b_two_filled"), sem("b_two_read")
        scored, neg_ready, exped, pv_made, scaled = sem("b_scored"), sem("b_neg_ready"), sem("b_exped"), sem("b_pv_made"), sem("b_scaled")
        own_squares, own_scale, own_max, own_inv, own_ln = (sem("b_own_" + s) for s in ("squares", "scale", "max", "inv", "ln"))
        spare = sem("b_spare")
        c_w_steps = sem("b_c_w_steps")
        wo_loaded, ffn_loaded = sem("b_wo_loaded"), sem("b_ffn_loaded")
        centered, csquared, var_made, rstd_ready, hn_ready, own_var, own_hn = (sem("b_" + s) for s in (
            "centered", "csquared", "var_made", "rstd_ready", "hn_ready", "own_var", "own_hn"))
        ag_made, gelued, hid_ready, y_made, ffn_written = (sem("b_" + s) for s in ("ag_made", "gelued", "hid_ready", "y_made", "ffn_written"))
        bank = M.bank
        block = ctx.enter_context(nc.Block())
        tile = lambda l, s, j: (l * SEQ + s) * TILES + j
        by_head = lambda ap: ap.rearrange("p (h d) -> p h d", d=LO_D)

        nothing = lambda *a: None

        def table(l, kind, j):
            return tables[:, l, kind, j, :].unsqueeze(1).broadcast_to([P, LO_H, LO_D])

        def table_half(l, kind, j, t):
            half = LO_D // 2
            return tables[:, l, kind, j, t * half:(t + 1) * half].unsqueeze(1).broadcast_to([P, LO_H, half])

        def half_heads(ap, t):
            return ap.rearrange("p (h t d) -> p t h d", t=2, d=LO_D // 2)[:, t, :, :]

        FIVE_USES, TWO_USES = SEQ * 7, SEQ * 8
        O_TURNED = 3
        SCORE_BANKS = (3, 4, 7)
        before = lambda h: (-1, 0, -2)[h] if h < 3 else h - 2

        def five_before(l, s, first):
            return l * FIVE_USES + (2 if first else s * 7)

        def two_before(l, s, first):
            return l * TWO_USES + (2 if first else s * 8 - 1)

        def five_at_end(l):
            return (l + 1) * FIVE_USES - 2

        def two_at_end(l):
            return (l + 1) * TWO_USES - 3

        @block.sync
        def _(sp):
            sp.dma_start(table_scale[:, :, :, :], dram["b_table_scale"].partition_broadcast(P)).then_inc(table_loaded, 16)
            with sp.Fori(0, LAYERS) as l:
                sp.wait_ge(two_read, C + l * TWO_USES)
                sp.dma_start(wo[:, :, :], dram["b_wo"][bass.ds(l, 1), :, :, :].rearrange("l p c n -> p (l c) n")).then_inc(wo_loaded, 16)
                sp.wait_ge(ffn_written, C + l * NBLK)
                sp.dma_start(w1[:, :], dram["b_w1"][bass.ds(l, 1), :, :].rearrange("l p n -> p (l n)")).then_inc(ffn_loaded, 16)
                sp.dma_start(w2[:, :, :], dram["b_w2"][bass.ds(l, 1), :, :, :].rearrange("l p c n -> p (l c) n")).then_inc(ffn_loaded, 16)
                sp.dma_start(cols[:, :], dram["b_cols"][bass.ds(l, 1), :, :].rearrange("l p n -> p (l n)")).then_inc(ffn_loaded, 16)

        @block.gpsimd
        def _(pool):
            for s in (h_ready, k_rotated):
                pool.sem_inc(s, C)
            for u in range(2):
                nc.gpsimd.memset(h_fea[u][:, :], 0.0).then_inc(tables_ready, 1)
            pool.wait_ge(tables_ready, 3 + LAYERS)

            def pre(l, s, u, h, first):
                if h == 0:
                    pool.wait_ge(v_made, C + l * SEQ + s - 1)
                    pool.wait_ge(k_rotated, C + tile(l, s, 0))
                    gate(pool, spare)
                    nc.gpsimd.tensor_copy(h_fea[u][0:64, :], M.xb[0:64, l, bass.ts(s, TOK)]).then_inc(h_ready, 1)
                    pool.wait_ge(h_ready, C + 2 * (l * SEQ + s) + 1)
                    gate(pool, spare)
                    nc.gpsimd.tensor_copy(h_fea[u][64:P, 1:TOK], M.xb[64:P, l, bass.ds(s * TOK, TOK - 1)]).then_inc(h_ready, 1)
                if h in (3, 6):
                    j = h // 6
                    pool.wait_ge(k_unit_ready, C + tile(l, s, j) + 1)
                    if h == 3:
                        pool.wait_ge(h_ready, C + 2 * (l * SEQ + s) + 2)
                    if first is not None:
                        pool.wait_ge(two_filled, C + two_before(l, s - 1, first))
                    gate(pool, spare)
                    nc.gpsimd.tensor_tensor(by_head(rot_k[j][:, 0, :]), by_head(k_unit[:, :]), table(l, 2, j), ALU.mult)
                    for t in range(2):
                        last = nc.gpsimd.tensor_tensor(half_heads(rot_k[j][:, 1, :], t), half_heads(k_unit[:, :], 1 - t), table_half(l, 3, j, t), ALU.mult)
                    last.then_inc(k_rotated, 1)

            with pool.Fori(0, LAYERS) as l:
                pool.wait_ge(ffn_written, C + l * NBLK)
                gate(pool, spare)
                over_local(pool, nothing, pre, nothing, nothing, nothing, nothing, l)
            pool.wait_ge(M.loaded_c, M.LOADED_C)
            pool.wait_ge(k_rotated, C + LAYERS * SEQ * TILES)
            nc.gpsimd.tensor_scalar(M.c_w[:, 0, :], M.c_w[:, 0, :], CA_D ** -0.5, None, ALU.mult).then_inc(c_w_steps, 1)
            pool.wait_ge(c_w_steps, 1)
            nc.gpsimd.tensor_copy(M.c_w_hi[:, :, :], M.c_w[:, :, :]).then_inc(c_w_steps, 1)
            pool.wait_ge(c_w_steps, 2)
            nc.gpsimd.tensor_tensor(M.c_w_lo[:, :, :], M.c_w[:, :, :], M.c_w_hi[:, :, :].bitcast(F32), ALU.subtract)

        @block.tensor
        def _(pe):
            for s in (qk_made, v_made, five_filled, two_filled, scored, pv_made, centered, var_made, ag_made, y_made):
                pe.sem_inc(s, C)
            mm = nc.tensor.matmul
            five, two = Channel(pe, five_filled, five_read), Channel(pe, two_filled, two_read)
            pe.wait_ge(M.loaded_b, M.LOADED_B)
            turned, o_turned = [None, None], [None]

            def pre(l, s, u, h, first):
                if first is None and h == 0:
                    five.at(l * FIVE_USES)
                    two.at(l * TWO_USES)
                if h in (1, 4):
                    j = h // 4
                    if h == 1:
                        pe.wait_ge(h_ready, C + 2 * (l * SEQ + s) + 2)
                        pe.wait_ge(v_copied, C + l * SEQ + s)
                    pe.wait_ge(q_rotated, C + tile(l, s, j))
                    pe.wait_ge(k_unit_ready, C + tile(l, s, j))
                    for part in range(2):
                        last = mm(bank(part), h_fea[u][:, j * P:(j + 1) * P], M.b_wqkv[:, l, part * INNER:(part + 1) * INNER], start=True, stop=True)
                    last.then_inc(qk_made, 1)
                if h in (5, 7):
                    j = h // 7
                    if h == 7:
                        pe.wait_ge(k_unit_ready, C + tile(l, s, 1) + 1)
                        mm(bank(1), h_fea[u][:, P:TOK], M.b_wqkv[:, l, 2 * INNER:3 * INNER], start=True, stop=True)
                    for src, ch, b, sig, made in ((rot_q[j], five, 5, five_filled, q_rotated), (rot_k[j], two, 2, two_filled, k_rotated)):
                        pe.wait_ge(made, C + tile(l, s, j) + 1)
                        ch.filling()
                        for c in range(CH):
                            for w in range(2):
                                last = mm(bank(b)[:, c * P:(c + 1) * P], src[:, w, c * P:(c + 1) * P], M.ident[:, :], is_transpose=True,
                                          start=(w == 0), stop=(w == 1))
                        last.then_inc(sig, 1)
                        if h == 7 and ch is five:
                            mm(bank(0), h_fea[u][:, 0:P], M.b_wqkv[:, l, 2 * INNER:3 * INNER], start=True, stop=True).then_inc(v_made, 1)

            def turn(n, g):
                pe.wait_ge(exped, C + n * LO_H + g + 1)
                ch, b, sig = (five, 5, five_filled) if g % 2 == 0 else (two, 2, two_filled)
                ch.filling()
                for t in range(3):
                    last = nc.tensor.transpose(bank(b)[:, t * P:(t + 1) * P], prob[g % 4][:, t * P:(t + 1) * P], M.ident[:, :])
                last.then_inc(sig, 1)
                turned[g % 2] = ch.uses

            def weigh(n, u, g):
                pe.wait_ge(five_read if g % 2 == 0 else two_read, C + turned[g % 2])
                if g == 0:
                    pe.wait_ge(v_copied, C + n + 1)
                if g % 4 == 0:
                    pe.wait_ge(scaled, C + 2 * n + g // 4)
                at, vc = (g % 4) * LO_D, slice(g * LO_D, (g + 1) * LO_D)
                mm(bank(6)[:, at:at + LO_D], prob_t[g % 2][:, 0:P], v_tok[u][:, 0, vc], start=True, stop=True)
                at = at + BANK // 2
                mm(bank(6)[:, at:at + LO_D], prob_t[g % 2][:, P:2 * P], v_tok[u][:, 0, vc], start=True, stop=False)
                mm(bank(6)[:, at:at + LO_D], prob_t[g % 2][:, 2 * P:3 * P], v_tok[u][:, 1, vc], start=False, stop=True).then_inc(pv_made, 1)

            def step(l, s, u, h, first):
                n = l * SEQ + s
                if h == 0:
                    five.at(five_before(l, s, first))
                    two.at(two_before(l, s, first))
                    pe.wait_ge(five_read, C + five_before(l, s, first))
                    pe.wait_ge(two_read, C + two_before(l, s, first))
                    turned[1] = two_before(l, s, first)
                c, rows, b = h // 2, slice((h % 2) * LO_D, (h % 2 + 1) * LO_D), SCORE_BANKS[h % 3]
                pe.wait_ge(exped, C + n * LO_H + before(h))
                mm(bank(b)[:, 0:P], q_fea[u][rows, c, 0:P], k_fea[u][rows, c, 0:P], start=True, stop=False)
                mm(bank(b)[:, 0:P], M.identb[:, :], M.mask_lo0[:, :], start=False, stop=True)
                mm(bank(b)[:, P:P + S1], q_fea[u][rows, c, P:TOK], k_fea[u][rows, c, TOK - S1:TOK], start=True, stop=False)
                mm(bank(b)[:, P:P + S1], M.identb[:, :], M.mask_lo1[:, :], start=False, stop=True).then_inc(scored, 1)

            def after(l, s, u, h, first):
                n = l * SEQ + s
                if h > 1:
                    turn(n, h - 2)
                elif not first:
                    turn(n - 1, h - 2 + LO_H)
                if h > 2:
                    weigh(n, u, h - 3)
                elif not first:
                    weigh(n - 1, 1 - u, h - 3 + LO_H)

            def drain(l, s, u):
                n = l * SEQ + s
                turned[1] = two_at_end(l)
                five.at(five_at_end(l))
                two.at(two_at_end(l))
                turn(n, LO_H - 2)
                weigh(n, u, LO_H - 3)
                turn(n, LO_H - 1)
                weigh(n, u, LO_H - 2)
                weigh(n, u, LO_H - 1)

            def tail(l, s, u, h):
                n = l * SEQ + s
                if h == 3:
                    pe.wait_ge(scaled, C + 2 * n + 2)
                    for j, (ch, b, sig) in enumerate(((five, 5, five_filled), (two, 2, two_filled))):
                        ch.filling()
                        for c in range(CH):
                            last = nc.tensor.transpose(bank(b)[:, c * P:(c + 1) * P], o[:, j, c * P:(c + 1) * P], M.ident[:, :])
                        last.then_inc(sig, 1)
                    o_turned[0] = five.uses
                if h == 6:
                    pe.wait_ge(wo_loaded, l * 16 + 16)
                    pe.wait_ge(five_read, C + o_turned[0])
                    two.filling()
                    for c in range(CH):
                        last = mm(bank(2)[:, 0:TOK], wo[:, c, :], o_fea[:, c, :], start=(c == 0), stop=(c == CH - 1))
                    last.then_inc(two_filled, 1)

            with pe.Fori(0, LAYERS) as l:
                over_local(pe, nothing, pre, step, after, tail, drain, l)
                pe.wait_ge(two_read, C + l * TWO_USES + TWO_USES)
                gate(pe, spare)
                f0 = l * NBLK
                with pe.Fori(0, NBLK // 4) as i:
                    for k0 in (0, 2):
                        for k in (k0, k0 + 1):
                            b = i * 4 + k
                            pe.wait_ge(hn_ready, C + f0 + b - 3)
                            mm(bank(k), M.center[:, 0, :], M.xb[:, 1, bass.ts(b, BLK)], start=True, stop=True)
                            mm(bank(k).rearrange("p (s t) -> p s t", t=TOK)[:, :, 1:TOK], M.center[:, 1, :],
                               M.xb[:, 1, bass.ts(b, BLK)].rearrange("p (s t) -> p s t", t=TOK)[:, :, 0:TOK - 1], start=False, stop=True,
                               skip_group_check=True).then_inc(centered, 1)
                        for k in (k0, k0 + 1):
                            b = i * 4 + k
                            pe.wait_ge(csquared, C + f0 + b + 1)
                            mm(bank(4 + k), M.mean[:, :], c_sq[k % 2][:, :], start=True, stop=True).then_inc(var_made, 1)
                pe.wait_ge(hn_ready, C + f0 + NBLK)
                pe.wait_ge(ffn_loaded, l * 48 + 48)
                gate(pe, spare)
                with pe.Fori(0, NBLK) as b:
                    for k, (off, w) in enumerate(HID_CUT):
                        pe.wait_ge(hid_ready, C + 3 * (f0 + b) + k - 2)
                        mm(bank(2 * k)[0:w, :], w1[:, HID + off:HID + off + w], hn[:, bass.ts(b, BLK)], start=True, stop=True)
                        mm(bank(2 * k + 1)[0:w, :], w1[:, off:off + w], hn[:, bass.ts(b, BLK)], start=True, stop=True).then_inc(ag_made, 1)
                    pe.wait_ge(ffn_written, C + f0 + b)
                    for k, (off, w) in enumerate(HID_CUT):
                        pe.wait_ge(hid_ready, C + 3 * (f0 + b) + k + 1)
                        last = mm(bank(6), w2[0:w, k, :], hid[k][0:w, :], start=(k == 0), stop=(k == 2))
                    last.then_inc(y_made, 1)
                pe.wait_ge(ffn_written, C + f0 + NBLK)
                gate(pe, spare)

        @block.scalar
        def _(act):
            for s in (squared, rooted, v_copied, five_read, exped, csquared, rstd_ready, gelued):
                act.sem_inc(s, C)
            a = nc.scalar.activation
            five = Channel(act, five_filled, five_read)
            own, own_l = Steps(act, own_ln, 1), Steps(act, own_var, 1)
            act.wait_ge(tables_ready, 3 + LAYERS)

            def early(l, s, u, h, first):
                if first is None and h == 0:
                    five.at(l * FIVE_USES)
                if h in (2, 5):
                    j = h // 5
                    act.wait_ge(qk_made, C + tile(l, s, j) + 1)
                    act.wait_ge(summed, C + tile(l, s, j))
                    a(sq[:, :].rearrange("p (b n) -> p b n", b=2), M.psum[:, 0:2, :], ACT.Square).then_inc(squared, 1)
                if h in (3, 6):
                    j = h // 6
                    own.at(tile(l, s, j))
                    act.wait_ge(summed, C + tile(l, s, j) + 1)
                    own.link(a(ln_ss[:, :], ss[:, :], ACT.Ln, scale=65536.0))
                    a(root[:, :], ln_ss[:, :], ACT.Exp, scale=-0.5).then_inc(rooted, 1)

            def pre(l, s, u, h, first):
                if h in (5, 7):
                    j = h // 7
                    if h == 5 and first is not None:
                        act.wait_ge(scored, C + (l * SEQ + s - 1) * LO_H)
                    five.reading()
                    a(q_fea[u][:, :, j * P:(j + 1) * P], bank(5).rearrange("p (c n) -> p c n", c=CH), ACT.Copy).then_inc(five_read, 1)
                if h == 7:
                    n = l * SEQ + s
                    act.wait_ge(v_made, C + n + 1)
                    if first is not None:
                        act.wait_ge(pv_made, C + (n - 1) * LO_H)
                    a(v_tok[u][:, :, :], M.psum[:, 0:2, :], ACT.Copy).then_inc(v_copied, 1)

            def take_turned(n, g):
                five.reading()
                act.wait_ge(pv_made, C + n * LO_H + g - 1)
                a(prob_t[0][:, :], bank(5)[:, 0:PW], ACT.Copy).then_inc(five_read, 1)

            def step(l, s, u, h, first):
                n = l * SEQ + s
                if h == 0:
                    five.at(five_before(l, s, first))
                    act.wait_ge(scaled, C + 2 * n - 2)
                p, b = h % 4, SCORE_BANKS[h % 3]
                act.wait_ge(neg_ready, C + n * LO_H + h + 1)
                act.wait_ge(pv_made, C + n * LO_H + h - 4)
                a(prob[p][:, 0:P], bank(b)[:, 0:P], ACT.Exp, bias=neg[p][:, 0:1], scale=q_scale[u][:, 0, h:h + 1],
                  accum_out=row_sum[u][:, 0, h:h + 1])
                a(prob[p][:, PW - S1:PW], bank(b)[:, P:P + S1], ACT.Exp, bias=neg[p][:, 1:2], scale=q_scale[u][:, 1, h:h + 1],
                  accum_out=row_sum[u][:, 1, h:h + 1]).then_inc(exped, 1)

            def after(l, s, u, h, first):
                n = l * SEQ + s
                if h % 2 == 0 and h > 1:
                    take_turned(n, h - 2)
                if h == 0 and not first:
                    take_turned(n - 1, LO_H - 2)

            def drain(l, s, u):
                five.at(five_at_end(l))
                take_turned(l * SEQ + s, LO_H - 2)

            def tail(l, s, u, h):
                if h == 3:
                    five.reading()
                    act.wait_ge(two_filled, C + two_before(l, s + 1, False))
                    a(o_fea[:, :, 0:P], bank(5).rearrange("p (c n) -> p c n", c=CH), ACT.Copy).then_inc(five_read, 1)

            with act.Fori(0, LAYERS) as l:
                nc.scalar.preload_act_table_set(LN_EXP_SET)
                over_local(act, early, pre, step, after, tail, drain, l)
                f0 = l * NBLK
                with act.Fori(0, NBLK // 4) as i:
                    for k0 in (0, 2):
                        for k in (k0, k0 + 1):
                            b = i * 4 + k
                            act.wait_ge(centered, C + f0 + b + 1)
                            act.wait_ge(var_made, C + f0 + b - 1)
                            a(c_sq[k % 2][:, :], bank(k), ACT.Square).then_inc(csquared, 1)
                        for k in (k0, k0 + 1):
                            b = i * 4 + k
                            own_l.at(f0 + b)
                            act.wait_ge(var_made, C + f0 + b + 1)
                            act.wait_ge(hn_ready, C + f0 + b - 3)
                            own_l.link(a(lnv[k][:, :], bank(4 + k), ACT.Ln, bias=M.eps[:, :]))
                            a(rstd[k][:, :], lnv[k][:, :], ACT.Exp, scale=-0.5).then_inc(rstd_ready, 1)
                nc.scalar.preload_act_table_set(GELU_SET)
                act.wait_ge(ffn_loaded, l * 48 + 48)
                gate(act, spare)
                with act.Fori(0, NBLK) as b:
                    for k, (off, w) in enumerate(HID_CUT):
                        act.wait_ge(ag_made, C + 3 * (f0 + b) + k + 1)
                        act.wait_ge(hid_ready, C + 3 * (f0 + b) + k - 2)
                        a(gelu[k][0:w, :], bank(2 * k)[0:w, :], ACT.Gelu, bias=cols[0:w, 3 + k:4 + k]).then_inc(gelued, 1)

        @block.vector
        def _(dve):
            for s in (summed, k_unit_ready, q_rotated, two_read, neg_ready, scaled, hn_ready, hid_ready, ffn_written):
                dve.sem_inc(s, C)
            v = nc.vector
            for p in range(4):
                last = v.memset(prob[p][:, P:2 * P], 0.0)
            last.then_inc(tables_ready, 1)
            dve.wait_ge(table_loaded, 16)
            dve.wait_ge(M.loaded_b, M.LOADED_B)
            for l in range(LAYERS):
                v.tensor_tensor(tables[:, l, :, :, :], M.rotary[:, :, :, :], table_scale[:, l, :, :].unsqueeze(2).broadcast_to([P, 4, TILES, LO_D]),
                                ALU.mult).then_inc(tables_ready, 1)
            dve.wait_ge(tables_ready, 3 + LAYERS)
            two = Channel(dve, two_filled, two_read)
            own_s, own_k, own_m, own_i, own_h = (Steps(dve, s, 1) for s in (own_squares, own_scale, own_max, own_inv, own_hn))

            def pre(l, s, u, h, first):
                if first is None and h == 0:
                    two.at(l * TWO_USES)
                if h in (2, 5):
                    j = h // 5
                    own_s.at(tile(l, s, j))
                    dve.wait_ge(squared, C + tile(l, s, j) + 1)
                    own_s.link(v.tensor_reduce(ss[:, :], by_head(sq[:, :]), AX, ALU.add))
                    v.tensor_scalar(ss[:, :], ss[:, :], 1e-24, None, ALU.max).then_inc(summed, 1)
                if h in (3, 6):
                    j = h // 6
                    own_k.at(tile(l, s, j))
                    dve.wait_ge(rooted, C + tile(l, s, j) + 1)
                    v.tensor_scalar(q_scale[u][:, j, :], root[:, 0:LO_H], 256.0 * 8.0, None, ALU.mult)
                    own_k.link(v.tensor_scalar(k_scale[:, :], root[:, LO_H:], 256.0, None, ALU.mult))
                    dve.wait_ge(k_rotated, C + tile(l, s, j))
                    v.tensor_tensor(by_head(k_unit[:, :]), by_head(bank(1)), heads_wide(k_scale[:, :], LO_D), ALU.mult).then_inc(k_unit_ready, 1)
                    if first is not None:
                        dve.wait_ge(five_filled, C + five_before(l, s - 1, first))
                    v.tensor_tensor(by_head(rot_q[j][:, 0, :]), by_head(bank(0)), table(l, 0, j), ALU.mult)
                    for t in range(2):
                        last = v.tensor_tensor(half_heads(rot_q[j][:, 1, :], t), half_heads(bank(0), 1 - t), table_half(l, 1, j, t), ALU.mult)
                    last.then_inc(q_rotated, 1)
                if h in (5, 7):
                    j = h // 7
                    if h == 5 and first is not None:
                        dve.wait_ge(scored, C + (l * SEQ + s - 1) * LO_H)
                    two.reading()
                    v.tensor_copy(k_fea[u][:, :, j * P:(j + 1) * P], bank(2).rearrange("p (c n) -> p c n", c=CH)).then_inc(two_read, 1)

            def take_turned(n, g):
                two.reading()
                dve.wait_ge(pv_made, C + n * LO_H + g - 1)
                v.tensor_copy(prob_t[1][:, :], bank(2)[:, 0:PW]).then_inc(two_read, 1)

            def scale(n, u, e):
                dve.wait_ge(exped, C + n * LO_H + 4 * e + 4)
                own_i.at(2 * n + e)
                own_i.link(v.reciprocal(inv_sum[e][:, :, :], row_sum[u][:, :, 4 * e:4 * e + 4]))
                dve.wait_ge(pv_made, C + n * LO_H + 4 * e + 4)
                for j in range(TILES):
                    last = v.tensor_tensor(o[:, j, e * BANK // 2:(e + 1) * BANK // 2].rearrange("p (h d) -> p h d", d=LO_D),
                                           bank(6)[:, j * BANK // 2:(j + 1) * BANK // 2].rearrange("p (h d) -> p h d", d=LO_D),
                                           heads_wide(inv_sum[e][:, j, :], LO_D), ALU.mult)
                last.then_inc(scaled, 1)

            def step(l, s, u, h, first):
                n = l * SEQ + s
                if h == 0:
                    two.at(two_before(l, s, first))
                p, b = h % 4, SCORE_BANKS[h % 3]
                own_m.at(n * LO_H + h)
                dve.wait_ge(scored, C + n * LO_H + h + 1)
                dve.wait_ge(exped, C + n * LO_H + h - 3)
                v.tensor_reduce(mx[p][:, 0:1], bank(b)[:, 0:P], AX, ALU.max)
                own_m.link(v.tensor_reduce(mx[p][:, 1:2], bank(b)[:, P:P + S1], AX, ALU.max))
                v.scalar_tensor_tensor(neg[p][:, :], mx[p][:, :], -1.0, q_scale[u][:, :, h], ALU.mult, ALU.mult).then_inc(neg_ready, 1)

            def after(l, s, u, h, first):
                n = l * SEQ + s
                if h == 1 and not first:
                    take_turned(n - 1, LO_H - 1)
                if h % 2 == 1 and h > 1:
                    take_turned(n, h - 2)
                if h == 2 and not first:
                    scale(n - 1, 1 - u, 1)
                if h == 6:
                    if not first:
                        dve.wait_ge(five_filled, C + five_before(l, s, first) + O_TURNED)
                        dve.wait_ge(two_filled, C + two_before(l, s, first) + O_TURNED)
                    scale(n, u, 0)

            def drain(l, s, u):
                n = l * SEQ + s
                two.at(two_at_end(l))
                take_turned(n, LO_H - 1)
                scale(n, u, 1)

            def tail(l, s, u, h):
                if h == 4:
                    two.reading()
                    v.tensor_copy(o_fea[:, :, P:TOK], bank(2).rearrange("p (c n) -> p c n", c=CH)).then_inc(two_read, 1)
                if h == 6:
                    two.reading()
                    v.tensor_tensor(M.xb[:, 1, bass.ts(s, TOK)], bank(2)[:, 0:TOK], M.xb[:, l, bass.ts(s, TOK)], ALU.add).then_inc(two_read, 1)

            with dve.Fori(0, LAYERS) as l:
                over_local(dve, nothing, pre, step, after, tail, drain, l)
                f0 = l * NBLK
                dve.wait_ge(ffn_loaded, l * 48 + 48)
                gate(dve, spare)
                with dve.Fori(0, NBLK // 4) as i:
                    for k in range(4):
                        b = i * 4 + k
                        own_h.at(f0 + b)
                        dve.wait_ge(rstd_ready, C + f0 + b + 1)
                        own_h.link(v.scalar_tensor_tensor(hn[:, bass.ts(b, BLK)], bank(k), cols[:, 0:1], rstd[k][:, :], ALU.mult, ALU.mult))
                        v.tensor_scalar(hn[:, bass.ts(b, BLK)], hn[:, bass.ts(b, BLK)], cols[:, 1:2], None, ALU.add).then_inc(hn_ready, 1)
                with dve.Fori(0, NBLK) as b:
                    dve.wait_ge(y_made, C + f0 + b)
                    for k, (off, w) in enumerate(HID_CUT):
                        dve.wait_ge(gelued, C + 3 * (f0 + b) + k + 1)
                        v.scalar_tensor_tensor(hid[k][0:w, :], bank(2 * k + 1)[0:w, :], cols[0:w, 6 + k:7 + k], gelu[k][0:w, :],
                                               ALU.add, ALU.mult).then_inc(hid_ready, 1)
                    dve.wait_ge(y_made, C + f0 + b + 1)
                    v.scalar_tensor_tensor(M.xb[:, 1, bass.ts(b, BLK)], bank(6), cols[:, 2:3], M.xb[:, 1, bass.ts(b, BLK)],
                                           ALU.add, ALU.add).then_inc(ffn_written, 1)


def causal_attention(nc, M, dram):
    ctx = ExitStack()
    with ctx:
        sb = lambda name, shape, dt=F32: ctx.enter_context(nc.sbuf_tensor(name, shape, dt))
        sem = lambda name: ctx.enter_context(nc.semaphore(name))
        HC = CA_H // 2
        LAG = 2
        V_BANKS = (7, 2, 7, 3)
        HALF = 8 * CA_D
        PW = P + TOK
        z = sb("c_z", [P, TOK])
        x2 = [sb(f"c_x2{u}", [P, TILES, DIM]) for u in range(2)]
        x2_hi, x2_lo = ([sb(f"c_x2_{part}{u}", [P, TOK], F32R) for u in range(2)] for part in ("hi", "lo"))
        v_tok = [sb(f"c_v{u}", [P, TILES, CA_H * CA_D]) for u in range(2)]
        qk = [sb(f"c_qk{p}", [P, 2, TOK]) for p in range(2)]
        neg = [sb(f"c_neg{p}", [P, TILES]) for p in range(2)]
        prob = [sb(f"c_prob{p}", [P, PW]) for p in range(2)]
        prob_t = [sb(f"c_prob_t{p}", [P, PW]) for p in range(2)]
        row_sum = [sb(f"c_row_sum{u}", [P, TILES, CA_H]) for u in range(2)]
        inv_sum = [sb(f"c_inv_sum{e}", [P, TILES, 8]) for e in range(2)]
        o = sb("c_o", [P, TILES, CA_H * CA_D])
        o_fea = M.b_wqkv[:, :, :].rearrange("p l c -> p (l c)")[:, 0:HC * TOK].rearrange("p (c t) -> p c t", c=HC)
        r = sb("c_r", [P, TILES, DIM])
        x3 = sb("c_x3", [P, TILES, DIM])
        x3_fea = sb("c_x3_fea", [P, TOK])
        st, mv = [sb(f"c_st{k}", [P, TILES, 6]) for k in range(2)], [sb(f"c_mv{k}", [P, TILES, 2]) for k in range(2)]
        lnv, rstd = [sb(f"c_lnv{k}", [P, TILES]) for k in range(2)], [sb(f"c_rstd{k}", [P, TILES]) for k in range(2)]

        names = ("w1_high qk_made qk_read scored neg_ready exped even_made even_read odd_made odd_read pv_made scaled "
                 "z_ready z_turned z_var z_rstd x2_ready x2_turned x2_high x2_fea_ready v_made v_copied "
                 "o_turned o_read y_made r_var r_rstd x3_ready x3_turned x3_fea_ready routed logits_read stored "
                 "own_inv own_r own_st own_st2 own_ln own_ln2 spare").split()
        S = {}
        for name in names:
            S[name] = sem("c_" + name)
        bank = M.bank
        block = ctx.enter_context(nc.Block())

        def before_start(eng, names):
            for name in names.split():
                eng.sem_inc(S[name], C)

        @block.sync
        def _(sp):
            for dst, src in M.d_loads:
                sp.dma_start(dst, src).then_inc(M.loaded_d, 16)

        @block.gpsimd
        def _(pool):
            before_start(pool, "z_ready stored")

            def pre(l, s, u, h, first):
                if h == 10 and first:
                    pool.wait_ge(M.loaded_d, M.LOADED_D)
                    nc.gpsimd.tensor_copy(M.d_w1_hi[:, :, :], M.d_w1[:, :, :]).then_inc(S["w1_high"], 1)
                    pool.wait_ge(S["w1_high"], 1)
                    nc.gpsimd.tensor_tensor(M.d_w1_lo[:, :, :], M.d_w1[:, :, :], M.d_w1_hi[:, :, :].bitcast(F32), ALU.subtract)
                if h == 9:
                    pool.wait_ge(S["z_turned"], C + s)
                    gate(pool, S["spare"])
                    nc.gpsimd.tensor_tensor(z[:, :], M.xb[:, 0, bass.ts(s, TOK)], M.xb[:, 1, bass.ts(s, TOK)], ALU.add).then_inc(S["z_ready"], 1)

            def tail(l, s, u, h):
                if h == 8:
                    pool.wait_ge(S["x3_ready"], C + s + 1)
                    pool.wait_ge(S["x3_fea_ready"], C + s + 1)
                    gate(pool, S["spare"])
                    nc.gpsimd.tensor_copy(M.xb[:, 1, bass.ts(s, TOK)], x3[:, :, :].rearrange("p j c -> p (j c)")).then_inc(S["stored"], 1)
                    nc.gpsimd.tensor_copy(M.xb[:, 0, bass.ts(s, TOK)], x3_fea[:, :]).then_inc(S["stored"], 1)

            over_sequences(pool, CA_H, LAG, pre, lambda *a: None, tail, 0)

        @block.tensor
        def _(pe):
            before_start(pe, "qk_made scored even_made odd_made pv_made z_turned x2_turned v_made o_turned y_made x3_turned routed")
            mm = nc.tensor.matmul
            pe.wait_ge(M.loaded_c, M.LOADED_C)

            def in_three(out, a, b):
                mm(out, a[0], b[1], start=True, stop=False)
                mm(out, a[0], b[0], start=False, stop=False)
                return mm(out, a[1], b[0], start=False, stop=True)

            def project(n, c, u):
                pe.wait_ge(S["qk_read"], C + n * HC + c)
                for part in range(2):
                    last = in_three(bank(2)[:, part * TOK:(part + 1) * TOK], [w[:, part, c * P:(c + 1) * P] for w in (M.c_w_hi, M.c_w_lo)],
                                    [x[u][:, :] for x in (x2_hi, x2_lo)])
                last.then_inc(S["qk_made"], 1)

            def pre(l, s, u, h, first):
                if h == 10:
                    pe.wait_ge(S["z_ready"], C + s + 1)
                    if first is not None:
                        pe.wait_ge(S["logits_read"], C + s - 1)
                        pe.wait_ge(S["v_copied"], C + 4 * s)
                    for j in range(TILES):
                        last = nc.tensor.transpose(bank(7)[:, j * P:(j + 1) * P], z[:, j * P:(j + 1) * P], M.ident[:, :])
                    last.then_inc(S["z_turned"], 1)
                if h == 14:
                    pe.wait_ge(S["x2_ready"], C + s + 1)
                    for j in range(TILES):
                        last = nc.tensor.transpose(bank(7)[:, j * P:(j + 1) * P], x2[u][:, j, :], M.ident[:, :])
                    last.then_inc(S["x2_turned"], 1)
                if h is None or h >= 15:
                    k = 3 if h is None else h - 15
                    if k == 0:
                        pe.wait_ge(S["x2_fea_ready"], C + s + 1)
                    j, e = k // 2, k % 2
                    if k == 1:
                        pe.wait_ge(S["qk_read"], C + s * HC)
                    elif k == 2:
                        pe.wait_ge(S["v_copied"], C + 4 * s + 1)
                    elif k == 3:
                        pe.wait_ge(S["even_read"], C + s * HC)
                    in_three(bank(V_BANKS[k]), [x[u][:, j * P:(j + 1) * P] for x in (x2_hi, x2_lo)],
                             [w[:, 2, e * HALF:(e + 1) * HALF] for w in (M.c_w_hi, M.c_w_lo)]).then_inc(S["v_made"], 1)
                if h is None:
                    pe.wait_ge(S["v_copied"], C + 4 * s + 2)
                    project(s, 0, u)

            def head(l, n, u, h, first, last_seq):
                if h < CA_H:
                    c, rows, b = h // 2, slice((h % 2) * CA_D, (h % 2 + 1) * CA_D), h % 2
                    q_f, k_f = qk[c % 2][rows, 0, :], qk[c % 2][rows, 1, :]
                    pe.wait_ge(S["exped"], C + n * CA_H + h - 1)
                    pe.wait_ge(S["qk_read"], C + n * HC + c + 1)
                    mm(bank(b)[:, 0:P], q_f[:, 0:P], k_f[:, 0:P], start=True, stop=False)
                    mm(bank(b)[:, 0:P], M.identb[:, :], M.mask_causal[:, :], start=False, stop=True)
                    mm(bank(b)[:, P:PW], q_f[:, P:TOK], k_f[:, :], start=True, stop=False, skip_group_check=True)
                    mm(bank(b)[:, 2 * P:PW], M.identb[:, :], M.mask_causal[:, :], start=False, stop=True, skip_group_check=True).then_inc(S["scored"], 1)
                    if h % 2 == 0 and c + 1 < HC:
                        project(n, c + 1, u)
                    if h == 0:
                        pe.wait_ge(S["v_copied"], C + 4 * n + 3)
                g = h - 1
                if 0 <= g < CA_H:
                    b, sig, read = (3, S["even_made"], S["even_read"]) if g % 2 == 0 else (4, S["odd_made"], S["odd_read"])
                    pe.wait_ge(S["exped"], C + n * CA_H + g + 1)
                    pe.wait_ge(read, C + n * HC + g // 2)
                    if g == 0:
                        pe.wait_ge(S["v_copied"], C + 4 * n + 4)
                    for t in range(3):
                        last = nc.tensor.transpose(bank(b)[:, t * P:(t + 1) * P], prob[g % 2][:, t * P:(t + 1) * P], M.ident[:, :])
                    last.then_inc(sig, 1)
                g = h - 2
                if 0 <= g < CA_H:
                    pe.wait_ge(S["even_read"] if g % 2 == 0 else S["odd_read"], C + n * HC + g // 2 + 1)
                    if g % 8 == 0:
                        pe.wait_ge(S["scaled"], C + 2 * n + g // 8)
                    cut, vc = slice((g % 8) * CA_D, (g % 8 + 1) * CA_D), slice(g * CA_D, (g + 1) * CA_D)
                    mm(bank(5)[:, cut], prob_t[g % 2][:, 0:P], v_tok[u][:, 0, vc], start=True, stop=True)
                    mm(bank(6)[:, cut], prob_t[g % 2][:, P:2 * P], v_tok[u][:, 0, vc], start=True, stop=False)
                    mm(bank(6)[:, cut], prob_t[g % 2][:, 2 * P:3 * P], v_tok[u][:, 1, vc], start=False, stop=True).then_inc(S["pv_made"], 1)

            def tail(l, s, u, h):
                if h < 4:
                    j, e = h // 2, h % 2
                    pe.wait_ge(S["scaled"], C + 2 * s + 2)
                    pe.wait_ge(S["o_read"], C + 4 * s + h)
                    if h == 0:
                        pe.wait_ge(S["logits_read"], C + s)
                    for c in range(4):
                        last = nc.tensor.transpose(bank(7)[:, c * P:(c + 1) * P], o[:, j, (4 * e + c) * P:(4 * e + c + 1) * P], M.ident[:, :])
                    last.then_inc(S["o_turned"], 1)
                if h == 4:
                    pe.wait_ge(S["o_read"], C + 4 * s + 4)
                    for j in range(TILES):
                        for c in range(HC):
                            last = mm(bank(7)[:, j * P:(j + 1) * P], o_fea[:, c, j * P:(j + 1) * P], M.c_wo[:, c, :], start=(c == 0), stop=(c == HC - 1))
                    last.then_inc(S["y_made"], 1)
                if h == 8:
                    pe.wait_ge(S["x3_ready"], C + s + 1)
                    for j in range(TILES):
                        last = nc.tensor.transpose(bank(7)[:, j * P:(j + 1) * P], x3[:, j, :], M.ident[:, :])
                    last.then_inc(S["x3_turned"], 1)
                if h == 9:
                    pe.wait_ge(S["x3_fea_ready"], C + s + 1)
                    for j in range(TILES):
                        last = mm(bank(7)[:, j * EXPERTS:(j + 1) * EXPERTS], x3_fea[:, j * P:(j + 1) * P], M.d_wr[:, :], start=True, stop=True)
                    last.then_inc(S["routed"], 1)

            over_sequences(pe, CA_H, LAG, pre, head, tail, 0)

        @block.scalar
        def _(act):
            before_start(act, "exped even_read z_rstd x2_high v_copied o_read r_rstd x3_fea_ready")
            a = nc.scalar.activation
            nc.scalar.preload_act_table_set(LN_EXP_SET)
            own = [Steps(act, S["own_ln"], 1), Steps(act, S["own_ln2"], 1)]

            def rsqrt(k, s, ready, sig):
                own[k].at(s)
                act.wait_ge(ready, C + s + 1)
                own[k].link(a(lnv[k][:, :], mv[k][:, :, 1], ACT.Ln, bias=M.eps[:, :]))
                a(rstd[k][:, :], lnv[k][:, :], ACT.Exp, scale=-0.5).then_inc(sig, 1)

            def pre(l, s, u, h, first):
                if h == 12:
                    rsqrt(0, s, S["z_var"], S["z_rstd"])
                if h == 14:
                    act.wait_ge(S["x2_turned"], C + s + 1)
                    a(x2_hi[u][:, :], bank(7)[:, 0:TOK], ACT.Copy).then_inc(S["x2_high"], 1)
                if h is None or h >= 15:
                    k = 3 if h is None else h - 15
                    j, e = k // 2, k % 2
                    act.wait_ge(S["v_made"], C + 4 * s + k + 1)
                    a(v_tok[u][:, j, e * HALF:(e + 1) * HALF], bank(V_BANKS[k]), ACT.Copy).then_inc(S["v_copied"], 1)

            def head(l, n, u, h, first, last_seq):
                if h < CA_H:
                    b = h % 2
                    act.wait_ge(S["neg_ready"], C + n * CA_H + h + 1)
                    act.wait_ge(S["pv_made"], C + n * CA_H + h - 2)
                    if h == 0:
                        act.wait_ge(S["scaled"], C + 2 * n - 2)
                    a(prob[b][:, 0:P], bank(b)[:, 0:P], ACT.Exp, bias=neg[b][:, 0:1], accum_out=row_sum[u][:, 0, h:h + 1])
                    a(prob[b][:, P:PW], bank(b)[:, P:PW], ACT.Exp, bias=neg[b][:, 1:2], accum_out=row_sum[u][:, 1, h:h + 1]).then_inc(S["exped"], 1)
                g = h - 1
                if 0 <= g < CA_H and g % 2 == 0:
                    act.wait_ge(S["even_made"], C + n * HC + g // 2 + 1)
                    act.wait_ge(S["pv_made"], C + n * CA_H + g - 1)
                    a(prob_t[0][:, :], bank(3)[:, 0:PW], ACT.Copy).then_inc(S["even_read"], 1)

            def tail(l, s, u, h):
                if h < 4:
                    j, e = h // 2, h % 2
                    act.wait_ge(S["o_turned"], C + 4 * s + h + 1)
                    if h == 0:
                        act.wait_ge(S["y_made"], C + s)
                    a(o_fea[:, 4 * e:4 * e + 4, j * P:(j + 1) * P], bank(7).rearrange("p (c n) -> p c n", c=4), ACT.Copy).then_inc(S["o_read"], 1)
                if h == 6:
                    rsqrt(1, s, S["r_var"], S["r_rstd"])
                if h == 8:
                    act.wait_ge(S["x3_turned"], C + s + 1)
                    act.wait_ge(S["stored"], C + 2 * s)
                    a(x3_fea[:, :], bank(7)[:, 0:TOK], ACT.Copy).then_inc(S["x3_fea_ready"], 1)

            over_sequences(act, CA_H, LAG, pre, head, tail, 0)

        @block.vector
        def _(dve):
            before_start(dve, "x2_fea_ready qk_read neg_ready odd_read scaled z_var x2_ready r_var x3_ready logits_read")
            v = nc.vector
            dve.wait_ge(M.loaded_c, M.LOADED_C)
            own_i, own_r = Steps(dve, S["own_inv"], 2), Steps(dve, S["own_r"], 1)
            own_s = [Steps(dve, S["own_st"], 3), Steps(dve, S["own_st2"], 3)]

            def stats(k, s, src, sig):
                own_s[k].at(s)
                for j in range(TILES):
                    place = own_s[k].done(v.bn_stats(st[k][:, j, :], src[:, j * P:(j + 1) * P]))
                own_s[k].wait_alone(place)
                v.bn_aggr(mv[k][:, 0, :], st[k][:, 0, :])
                v.bn_aggr(mv[k][:, 1, :], st[k][:, 1, :]).then_inc(sig, 1)

            def normed(k, out, src, sig):
                for j in range(TILES):
                    last = v.tensor_scalar(out[:, j, :], src[:, j * P:(j + 1) * P], mv[k][:, j, 0:1], rstd[k][:, j:j + 1], ALU.subtract, ALU.mult)
                last.then_inc(sig, 1)

            def take(n, c):
                dve.wait_ge(S["qk_made"], C + n * HC + c + 1)
                dve.wait_ge(S["scored"], C + n * CA_H + 2 * c - 2)
                v.tensor_copy(qk[c % 2][:, :, :], bank(2).rearrange("p (w t) -> p w t", w=2)).then_inc(S["qk_read"], 1)

            def pre(l, s, u, h, first):
                if h == 11:
                    dve.wait_ge(S["z_turned"], C + s + 1)
                    stats(0, s, bank(7), S["z_var"])
                if h == 13:
                    dve.wait_ge(S["z_rstd"], C + s + 1)
                    normed(0, x2[u], bank(7), S["x2_ready"])
                if h == 14:
                    dve.wait_ge(S["x2_high"], C + s + 1)
                    v.tensor_tensor(x2_lo[u][:, :], bank(7)[:, 0:TOK], x2_hi[u][:, :].bitcast(F32), ALU.subtract).then_inc(S["x2_fea_ready"], 1)
                if h is None:
                    take(s, 0)

            def head(l, n, u, h, first, last_seq):
                if h in (10, CA_H + LAG - 1):
                    e = 0 if h == 10 else 1
                    own_i.at(n)
                    own_i.k = e
                    dve.wait_ge(S["exped"], C + n * CA_H + 8 * e + 8)
                    own_i.link(v.reciprocal(inv_sum[e][:, :, :], row_sum[u][:, :, 8 * e:8 * e + 8]))
                    dve.wait_ge(S["pv_made"], C + n * CA_H + 8 * e + 8)
                    dve.wait_ge(S["o_turned"], C + 4 * n)
                    for j in range(TILES):
                        last = v.tensor_tensor(o[:, j, e * HALF:(e + 1) * HALF].rearrange("p (h d) -> p h d", d=CA_D),
                                               bank(5 + j).rearrange("p (h d) -> p h d", d=CA_D), heads_wide(inv_sum[e][:, j, :], CA_D), ALU.mult)
                    last.then_inc(S["scaled"], 1)
                if h < CA_H:
                    b = h % 2
                    dve.wait_ge(S["scored"], C + n * CA_H + h + 1)
                    dve.wait_ge(S["exped"], C + n * CA_H + h - 1)
                    v.tensor_reduce(neg[b][:, 0:1], bank(b)[:, 0:P], AX, ALU.max, negate=True)
                    v.tensor_reduce(neg[b][:, 1:2], bank(b)[:, P:PW], AX, ALU.max, negate=True).then_inc(S["neg_ready"], 1)
                    if h % 2 == 0 and h // 2 + 1 < HC:
                        take(n, h // 2 + 1)
                g = h - 1
                if 0 <= g < CA_H and g % 2 == 1:
                    dve.wait_ge(S["odd_made"], C + n * HC + g // 2 + 1)
                    dve.wait_ge(S["pv_made"], C + n * CA_H + g - 1)
                    v.tensor_copy(prob_t[1][:, :], bank(4)[:, 0:PW]).then_inc(S["odd_read"], 1)

            def tail(l, s, u, h):
                if h == 5:
                    own_r.at(s)
                    dve.wait_ge(S["y_made"], C + s + 1)
                    own_r.link(v.tensor_tensor(r[:, :, :], bank(7)[:, 0:TOK].rearrange("p (j c) -> p j c", j=TILES), x2[u][:, :, :], ALU.add))
                    stats(1, s, r[:, :, :].rearrange("p j c -> p (j c)"), S["r_var"])
                if h == 7:
                    dve.wait_ge(S["r_rstd"], C + s + 1)
                    dve.wait_ge(S["stored"], C + 2 * s)
                    normed(1, x3, r[:, :, :].rearrange("p j c -> p (j c)"), S["x3_ready"])
                if h == 10:
                    dve.wait_ge(S["routed"], C + s + 1)
                    v.tensor_copy(M.logits[:, bass.ts(s, TILES), :], bank(7)[:, 0:TILES * EXPERTS].rearrange("p (j e) -> p j e", j=TILES)).then_inc(S["logits_read"], 1)

            over_sequences(dve, CA_H, LAG, pre, head, tail, 0)


def experts(nc, M, dram):
    ctx = ExitStack()
    with ctx:
        sb = lambda name, shape, dt=F32: ctx.enter_context(nc.sbuf_tensor(name, shape, dt))
        sem = lambda name: ctx.enter_context(nc.semaphore(name))
        KF = FFN // P
        TB = BLK // P
        TOP_BIT = 29
        EARLY = 2
        STEPS = 2
        SEARCH = STEPS * EARLY * EXPERTS
        wide = [P, NT, EXPERTS]
        row = lambda ap: ap.unsqueeze(2).broadcast_to(wide)
        col = lambda ap: ap.unsqueeze(1).broadcast_to(wide)
        by_expert = lambda ap: ap.rearrange("p t e -> p e t")
        t1 = [sb(f"d_row{k}", [P, NT]) for k in range(6)]
        prob, w_a, w_b = sb("d_prob", wide), sb("d_wa", wide), sb("d_wb", wide)
        first, second, gate_w = sb("d_first", wide), sb("d_second", wide), sb("d_gate", wide)
        order = sb("d_order", [P, EXPERTS])
        thr, cand, bit, take = (sb(f"d_{s}", [P, EXPERTS], I32) for s in ("thr", "cand", "bit", "take"))
        bit_f, count = sb("d_bit_f", [P, EXPERTS]), sb("d_count", [P, EXPERTS])
        room = sb("d_room", [P, EXPERTS])
        equal_b = sb("d_equal_b", wide, BF16)
        ones_b, before_b = sb("d_ones_b", [P, P], BF16), sb("d_before_b", [P, P], BF16)
        y_early = [M.d_w1[:, :, :].rearrange("p e (t c) -> p e t c", c=DIM),
                   sb("d_y_early", [P, EXPERTS, TB, DIM])]
        pieces = lambda place: [place[:, k * BLK:(k + 1) * BLK].rearrange("p (t c) -> p t c", c=DIM) for k in range(place.shape[1] // BLK)]
        *sums, total0, total1 = pieces(M.b_wqkv[:, :, :].rearrange("p l c -> p (l c)"))
        sum_early, total = [sums[2 * b:2 * b + 2] for b in range(EARLY)], [total0, total1]
        acc = pieces(M.c_wo[:, :, :].rearrange("p c n -> p (c n)"))
        res = pieces(M.b_wo[:, :, :].rearrange("p c n -> p (c n)")) + pieces(M.a_wkv[:, :])
        x_hi, x_lo = ([sb(f"d_x_{part}{p}", [P, BLK], F32R) for p in range(2)] for part in ("hi", "lo"))
        hid = [sb(f"d_hid{p}", [P, KF, BLK]) for p in range(2)]
        gates = sb("d_gates", wide)
        g_blk = [sb(f"d_g_blk{p}", [P, TB, EXPERTS]) for p in range(2)]
        st, mv = [sb(f"d_st{p}", [P, TB, 6]) for p in range(2)], [sb(f"d_mv{p}", [P, TB, 2]) for p in range(2)]
        lnv, rstd = [sb(f"d_lnv{p}", [P, TB]) for p in range(2)], [sb(f"d_rstd{p}", [P, TB]) for p in range(2)]

        MAIN = NBLK - EARLY
        STORE0 = 32
        names = ("shifted exped counted summed equal_ready ranked own h_made h_even h_odd y_made combined var rstd res_ready "
                 "x_high x_split early_h early_y early_gated gates_ready early_sum own_ln own_st own_fin loop spare").split()
        S = {}
        for name in names:
            S[name] = sem("d_" + name)
        stored = [sem(f"d_stored{u}") for u in range(2)]
        H0, Y0 = EARLY * EXPERTS * KF, EARLY * EXPERTS
        bank = M.bank
        block = ctx.enter_context(nc.Block())

        @block.sync
        def _(sp):
            out_v = dram["out"].rearrange("(b s) (j p) c -> b p (s j) c", s=BLK // TOK, p=P)
            with sp.Fori(0, MAIN // 2) as i:
                for u in range(2):
                    sp.wait_ge(S["res_ready"], C + i * 2 + u + 1)
                    sp.dma_start(out_v[bass.ds(i * 2 + u + EARLY, 1), :, :, :].rearrange("b p t c -> p (b t) c"), res[u][:, :, :]).then_inc(stored[u], 16)
            for b in range(EARLY):
                sp.wait_ge(S["res_ready"], C + MAIN + b + 1)
                sp.dma_start(out_v[b, :, :, :], res[b][:, :, :]).then_inc(stored[b], 16)
            for u in range(2):
                sp.wait_ge(stored[u], STORE0 + NBLK // 2 * 16)

        @block.tensor
        def _(pe):
            mm = nc.tensor.matmul
            pe.sem_inc(S["summed"], C)
            pe.wait_ge(M.loaded_d, M.LOADED_D)

            def hidden(out, e, k, u):
                w_hi, w_lo = (w[:, e, k * P:(k + 1) * P] for w in (M.d_w1_hi, M.d_w1_lo))
                mm(out, w_hi, x_lo[u][:, :], start=True, stop=False)
                mm(out, w_hi, x_hi[u][:, :], start=False, stop=False)
                return mm(out, w_lo, x_hi[u][:, :], start=False, stop=True)

            def up_early(b, e, chunks):
                for k in chunks:
                    if b or e:
                        pe.wait_ge(S["early_h"], KF * (b * EXPERTS + e - 1) + k + 1)
                    if k == 0 and e == 0:
                        pe.wait_ge(S["x_split"], C + b + 1)
                    hidden(bank(k), e, k, b % 2).then_inc(S["h_made"], 1)

            def down_early(b, e, tiles, done):
                g = b * EXPERTS + e
                if tiles[0] == 0:
                    pe.wait_ge(S["early_h"], KF * g + KF)
                    if g > 1:
                        pe.wait_ge(S["early_y"], g - 1)
                for t in tiles:
                    for k in range(KF):
                        last = mm(bank(4 + e % 2)[:, t * P:(t + 1) * P], hid[e % 2][:, k, t * P:(t + 1) * P], M.d_w2[:, e, k, :],
                                  start=(k == 0), stop=(k == KF - 1))
                if done:
                    last.then_inc(S["y_made"], 1)

            def count_step(k):
                pe.wait_ge(S["counted"], C + k + 1)
                mm(bank(6)[:, 0:EXPERTS], M.ones[:, :], count[:, :], start=True, stop=True).then_inc(S["summed"], 1)

            up_early(0, 0, range(KF))
            for b in range(EARLY):
                for e in range(EXPERTS):
                    for q in range(4):
                        if q < 2 and (b, e) != (EARLY - 1, EXPERTS - 1):
                            up_early(b + (e + 1) // EXPERTS, (e + 1) % EXPERTS, (2 * q, 2 * q + 1))
                        if q >= 2:
                            down_early(b, e, (2 * q - 4, 2 * q - 3), q == 3)
                        if q % 2 == 1:
                            count_step(STEPS * (b * EXPERTS + e) + q // 2)
            pe.wait_ge(S["equal_ready"], 1)
            mm(bank(6)[:, 0:EXPERTS], M.ones[:, :], count[:, :], start=True, stop=True)
            flat = lambda ap: ap.rearrange("p t e -> p (t e)")
            mm(bank(7)[:, 0:NT * EXPERTS], before_b[:, :], flat(equal_b[:, :, :]), start=True, stop=False)
            for t in range(NT - 1):
                last = mm(bank(7)[:, (t + 1) * EXPERTS:NT * EXPERTS], ones_b[:, :],
                          equal_b[:, t, :].unsqueeze(1).broadcast_to([P, NT - 1 - t, EXPERTS]), start=False, stop=(t == NT - 2))
            last.then_inc(S["ranked"], 1)
            pe.wait_ge(S["early_h"], EARLY * EXPERTS * KF)
            pe.wait_ge(S["early_y"], EARLY * EXPERTS)

            gate(pe, S["spare"])
            def main_block(b, u):
                def up(e):
                    g = b * EXPERTS + e
                    if e == 0:
                        pe.wait_ge(S["x_split"], C + EARLY + b + 1)
                    for k in range(KF):
                        pe.wait_ge(S["h_even"] if k % 2 == 0 else S["h_odd"], C + 2 * (g - 1) + k // 2 + 1)
                        hidden(bank(k), e, k, u).then_inc(S["h_made"], 1)

                def down(e):
                    g = b * EXPERTS + e
                    pe.wait_ge(S["h_even"], C + 2 * g + 2)
                    pe.wait_ge(S["h_odd"], C + 2 * g + 2)
                    pe.wait_ge(S["combined"], C + g - 1)
                    for t in range(TB):
                        for k in range(KF):
                            last = mm(bank(4 + e % 2)[:, t * P:(t + 1) * P], hid[e % 2][:, k, t * P:(t + 1) * P], M.d_w2[:, e, k, :],
                                      start=(k == 0), stop=(k == KF - 1))
                    last.then_inc(S["y_made"], 1)

                up(0)
                for e in range(1, EXPERTS):
                    up(e)
                    down(e - 1)
                down(EXPERTS - 1)

            with pe.Fori(0, MAIN // 2) as i:
                for u in range(2):
                    main_block(i * 2 + u, u)

        @block.scalar
        def _(act):
            a = nc.scalar.activation
            nc.scalar.preload_act_table_set(LN_EXP_SET)
            act.sem_inc(S["h_even"], C)
            act.sem_inc(S["rstd"], C)
            act.wait_ge(S["shifted"], 1)
            a(w_b[:, :, :], w_a[:, :, :], ACT.Exp).then_inc(S["exped"], 1)
            for g in range(EARLY * EXPERTS + 1):
                if g < EARLY * EXPERTS:
                    if g > 1:
                        act.wait_ge(S["y_made"], g - 1)
                    for k in range(KF):
                        act.wait_ge(S["h_made"], KF * g + k + 1)
                        a(hid[g % 2][:, k, :], bank(k), ACT.Relu).then_inc(S["early_h"], 1)
                if g > 0:
                    act.wait_ge(S["y_made"], g)
                    a(y_early[(g - 1) // EXPERTS][:, (g - 1) % EXPERTS, :, :].rearrange("p t c -> p (t c)"), bank(4 + (g - 1) % 2), ACT.Copy).then_inc(S["early_y"], 1)
            own = Steps(act, S["own_ln"], 1)
            def inverse_root(n, u):
                own.at(n)
                act.wait_ge(S["var"], C + n + 1)
                own.link(a(lnv[u][:, :], mv[u][:, :, 1], ACT.Ln, bias=M.eps[:, :]))
                a(rstd[u][:, :], lnv[u][:, :], ACT.Exp, scale=-0.5).then_inc(S["rstd"], 1)

            with act.Fori(0, MAIN // 2) as i:
                for u in range(2):
                    b = i * 2 + u
                    for e in range(EXPERTS):
                        g = b * EXPERTS + e
                        act.wait_ge(S["y_made"], Y0 + g - 1)
                        for k in (0, 2):
                            act.wait_ge(S["h_made"], H0 + KF * g + k + 1)
                            a(hid[e % 2][:, k, :], bank(k), ACT.Relu).then_inc(S["h_even"], 1)
                        if u == 1 and e == 3:
                            inverse_root(b - 1, 0)
                    if u == 1:
                        inverse_root(b, 1)
            for b in range(EARLY):
                inverse_root(MAIN + b, b)

        @block.vector
        def _(dve):
            v = nc.vector
            for s in (S["counted"], S["h_odd"], S["combined"], S["var"], S["res_ready"]):
                dve.sem_inc(s, C)
            for u in range(2):
                dve.sem_inc(stored[u], STORE0)
            own = Steps(dve, S["own"], 1000)
            own.at(0)
            own.link(v.tensor_reduce(t1[0][:, :], M.logits[:, :, :], AX, ALU.max))
            v.tensor_tensor(w_a[:, :, :], M.logits[:, :, :], row(t1[0][:, :]), ALU.subtract).then_inc(S["shifted"], 1)
            for e in range(EXPERTS):
                own.done(v.memset(order[:, e:e + 1], float(EXPERTS - e)))
            own.done(v.memset(thr[:, :], 0))
            own.done(v.memset(bit[:, :], 1 << TOP_BIT))
            own.done(v.memset(bit_f[:, :], float(1 << TOP_BIT)))
            dve.wait_ge(M.loaded_d, M.LOADED_D)
            own.done(v.tensor_copy(ones_b[:, :], M.ones[:, :]))
            own.done(v.tensor_copy(before_b[:, :], M.before[:, :]))
            dve.wait_ge(S["exped"], 1)
            own.link(v.tensor_reduce(t1[1][:, :], w_b[:, :, :], AX, ALU.add))
            own.link(v.reciprocal(t1[2][:, :], t1[1][:, :]))
            own.link(v.tensor_tensor(prob[:, :, :], w_b[:, :, :], row(t1[2][:, :]), ALU.mult))

            def pick(out, src, k):
                own.link(v.tensor_reduce(t1[k][:, :], src, AX, ALU.max))
                own.link(v.tensor_tensor(w_a[:, :, :], src, row(t1[k][:, :]), ALU.is_equal))
                own.link(v.tensor_tensor(w_a[:, :, :], w_a[:, :, :], col(order[:, :]), ALU.mult))
                own.link(v.tensor_reduce(t1[k + 1][:, :], w_a[:, :, :], AX, ALU.max))
                own.link(v.tensor_tensor(out, w_a[:, :, :], row(t1[k + 1][:, :]), ALU.is_equal))

            pick(first[:, :, :], prob[:, :, :], 2)
            own.link(v.scalar_tensor_tensor(w_b[:, :, :], first[:, :, :], -2.0, prob[:, :, :], ALU.mult, ALU.add))
            pick(second[:, :, :], w_b[:, :, :], 4)
            own.link(v.tensor_tensor(first[:, :, :], first[:, :, :], second[:, :, :], ALU.add))
            own.link(v.tensor_tensor(gate_w[:, :, :], prob[:, :, :], first[:, :, :], ALU.mult))

            loop = Steps(dve, S["loop"], 4)
            with dve.Fori(0, SEARCH // 4) as i:
                for q in range(4):
                    k = i * 4 + q
                    loop.at(k)
                    loop.link(v.tensor_tensor(cand[:, :], thr[:, :], bit[:, :], ALU.bitwise_or))
                    loop.link(v.tensor_tensor(w_a[:, :, :], gate_w[:, :, :], col(cand[:, :].bitcast(F32)), ALU.is_ge))
                    v.tensor_reduce(count[:, :], by_expert(w_a[:, :, :]), AX, ALU.add).then_inc(S["counted"], 1)
                    dve.wait_ge(S["summed"], C + k + 1)
                    v.tensor_single_scalar(bit[:, :], bit[:, :], 1, ALU.logical_shift_right)
                    loop.link(v.scalar_tensor_tensor(take[:, :], bank(6)[:, 0:EXPERTS], float(CAP), bit_f[:, :], ALU.is_ge, ALU.mult))
                    v.tensor_scalar(bit_f[:, :], bit_f[:, :], 0.5, None, ALU.mult)
                    loop.link(v.tensor_tensor(thr[:, :], thr[:, :], take[:, :], ALU.bitwise_or))
            thr_f = col(thr[:, :].bitcast(F32))
            own.link(v.tensor_tensor(w_a[:, :, :], gate_w[:, :, :], thr_f, ALU.is_gt))
            own.link(v.tensor_reduce(count[:, :], by_expert(w_a[:, :, :]), AX, ALU.add))
            v.tensor_tensor(equal_b[:, :, :], gate_w[:, :, :], thr_f, ALU.is_equal).then_inc(S["equal_ready"], 1)
            dve.wait_ge(S["ranked"], 1)
            own.link(v.tensor_scalar(room[:, :], bank(6)[:, 0:EXPERTS], -1.0, float(CAP), ALU.mult, ALU.add))
            own.link(v.tensor_tensor(w_b[:, :, :], bank(7)[:, 0:NT * EXPERTS].rearrange("p (t e) -> p t e", e=EXPERTS), col(room[:, :]), ALU.is_lt))
            own.link(v.tensor_tensor(w_b[:, :, :], w_b[:, :, :], equal_b[:, :, :], ALU.mult))
            own.link(v.tensor_tensor(w_b[:, :, :], w_b[:, :, :], w_a[:, :, :], ALU.add))
            v.tensor_tensor(gates[:, :, :], gate_w[:, :, :], w_b[:, :, :], ALU.mult).then_inc(S["gates_ready"], 1)
            dve.wait_ge(S["gates_ready"], 1)

            def statistics(n, fin, u):
                own_f.at(n)
                for t in range(TB):
                    place = own_f.done(v.bn_stats(st[u][:, t, :], fin[:, t, :]))
                own_f.wait_alone(place)
                for t in range(TB):
                    last = v.bn_aggr(mv[u][:, t, :], st[u][:, t, :])
                last.then_inc(S["var"], 1)

            def normalise(n, fin, u):
                dve.wait_ge(S["rstd"], C + n + 1)
                for t in range(TB):
                    last = v.tensor_scalar(res[u][:, t, :], fin[:, t, :], mv[u][:, t, 0:1], rstd[u][:, t:t + 1], ALU.subtract, ALU.mult)
                last.then_inc(S["res_ready"], 1)


            own_s, own_f = Steps(dve, S["own_st"], 1), Steps(dve, S["own_fin"], TB + 1)
            with dve.Fori(0, MAIN // 2) as i:
                for u in range(2):
                    b = i * 2 + u
                    own_s.at(b)
                    place = own_s.done(v.tensor_copy(g_blk[u][:, :, :], gates[:, bass.ds((b + EARLY) * TB, TB), :]))

                    def combine(e, place):
                        g = b * EXPERTS + e
                        dve.wait_ge(S["y_made"], Y0 + g + 1)
                        dve.wait_ge(S["combined"], C + g)
                        if e == 0:
                            own_s.wait(place)
                        out = acc[e % 2] if e < EXPERTS - 1 else total[u]
                        for t in range(TB):
                            before = M.xb[:, 1, bass.ds((b + EARLY) * BLK + t * P, P)] if e == 0 else acc[(e + 1) % 2][:, t, :]
                            last = v.scalar_tensor_tensor(out[:, t, :], bank(4 + e % 2)[:, t * P:(t + 1) * P], g_blk[u][:, t, e:e + 1],
                                                          before, ALU.mult, ALU.add)
                        last.then_inc(S["combined"], 1)

                    for e in range(EXPERTS):
                        g = b * EXPERTS + e
                        dve.wait_ge(S["y_made"], Y0 + g - 1)
                        for k in (1, 3):
                            dve.wait_ge(S["h_made"], H0 + KF * g + k + 1)
                            v.tensor_scalar(hid[e % 2][:, k, :], bank(k), 0.0, None, ALU.max).then_inc(S["h_odd"], 1)
                        if e:
                            combine(e - 1, place)
                        if u == 1 and e == 2:
                            statistics(b - 1, total[0], 0)
                        if u == 1 and e == 4:
                            dve.wait_ge(stored[0], STORE0 + 16 * i)
                            normalise(b - 1, total[0], 0)
                    combine(EXPERTS - 1, place)
                    dve.wait_ge(S["combined"], C + b * EXPERTS + EXPERTS)
                    if u == 1:
                        dve.wait_ge(stored[1], STORE0 + 16 * i)
                        statistics(b, total[1], 1)
                        normalise(b, total[1], 1)
            for b in range(EARLY):
                dve.wait_ge(S["early_sum"], (b + 1) * EXPERTS)
                dve.wait_ge(stored[b], STORE0 + 16 * (MAIN // 2))
                statistics(MAIN + b, sum_early[b][(EXPERTS - 1) % 2], b)
            for b in range(EARLY):
                normalise(MAIN + b, sum_early[b][(EXPERTS - 1) % 2], b)

        @block.gpsimd
        def _(pool):
            pool.sem_inc(S["x_high"], C)
            pool.sem_inc(S["x_split"], C)

            def split(n, x, u):
                gate(pool, S["spare"])
                nc.gpsimd.tensor_copy(x_hi[u][:, :], x).then_inc(S["x_high"], 1)
                pool.wait_ge(S["x_high"], C + n + 1)
                gate(pool, S["spare"])
                nc.gpsimd.tensor_tensor(x_lo[u][:, :], x, x_hi[u][:, :].bitcast(F32), ALU.subtract).then_inc(S["x_split"], 1)

            for b in range(EARLY):
                split(b, M.xb[:, 0, b * BLK:(b + 1) * BLK], b)
            with pool.Fori(0, MAIN // 2) as i:
                for u in range(2):
                    pool.wait_ge(S["h_made"], (i * 2 + u + 1) * EXPERTS * KF)
                    split(i * 2 + u + EARLY, M.xb[:, 0, bass.ds((i * 2 + u + EARLY) * BLK, BLK)], u)
            pool.wait_ge(S["gates_ready"], 1)
            pool.wait_ge(S["early_y"], EARLY * EXPERTS)
            for b in range(EARLY):
                for e in range(EXPERTS):
                    g = b * EXPERTS + e
                    y = y_early[b][:, e, :, :]
                    nc.gpsimd.tensor_tensor(y, y, gates[:, b * TB:(b + 1) * TB, e:e + 1].broadcast_to([P, TB, DIM]), ALU.mult).then_inc(S["early_gated"], 1)
                    pool.wait_ge(S["early_gated"], g + 1)
                    if g:
                        pool.wait_ge(S["early_sum"], g)
                    prior = M.xb[:, 1, b * BLK:(b + 1) * BLK].rearrange("p (t c) -> p t c", c=DIM) if e == 0 else sum_early[b][(e + 1) % 2][:, :, :]
                    nc.gpsimd.tensor_tensor(sum_early[b][e % 2][:, :, :], y, prior, ALU.add).then_inc(S["early_sum"], 1)


class Memory:
    pass


def program(nc, dram):
    ctx = ExitStack()
    with ctx:
        sb = lambda name, shape, dt=F32: ctx.enter_context(nc.sbuf_tensor(name, shape, dt))
        sem = lambda name: ctx.enter_context(nc.semaphore(name))
        M = Memory()
        M.psum = ctx.enter_context(nc.psum_tensor("banks", [P, 8, BANK], F32))
        M.bank = lambda b: M.psum[:, b, :]
        M.xb = sb("xb", [P, 2, SEQ * TOK])
        M.ident = sb("ident", [P, P])
        M.head_sum = sb("head_sum", [P, LA_H])
        M.state_mask = sb("state_mask", [P, P])
        M.eps = sb("eps", [P, 1])
        M.a_wkv = sb("a_wkv", [P, 4 * DIM])
        M.a_wq = sb("a_wq", [P, DIM])
        M.a_wo = sb("a_wo", [P, DIM])
        M.a_bkv = sb("a_bkv", [P, 4 * DIM])
        M.a_bo = sb("a_bo", [P, DIM])
        M.a_cols = sb("a_cols", [P, 3])
        M.a_bq, M.a_lng, M.a_lnb = (M.a_cols[:, k:k + 1] for k in range(3))
        M.masks = sb("masks", [P, 4 * P + WINDOW], BF16)
        masks = sb("masks32", [P, 4 * P + WINDOW])
        cuts = [0, P, 2 * P + WINDOW, 3 * P + WINDOW, 4 * P + WINDOW]
        M.mask_lo0, M.mask_lo1, M.mask_causal, M.identb = (M.masks[:, a:b] for a, b in zip(cuts, cuts[1:]))
        M.center, M.mean = sb("center", [P, 2, P]), sb("mean", [P, P])
        M.rotary = sb("rotary", [P, 4, TILES, LO_D])
        M.b_wqkv = sb("b_wqkv", [P, LAYERS, 3 * LO_H * LO_D])
        M.b_wo = sb("b_wo", [P, LO_H * LO_D // P, DIM])
        M.b_w1 = sb("b_w1", [P, 2 * HID])
        M.b_w2 = sb("b_w2", [P, 3, DIM])
        M.b_cols = sb("b_cols", [P, 9])
        M.loaded_b, M.LOADED_B = sem("loaded_b"), 4 * 16
        M.d_w1 = sb("d_w1", [P, EXPERTS, FFN])
        M.c_w = M.d_w1[:, :, :].rearrange("p e f -> p (e f)")[:, 0:3 * CA_H * CA_D].rearrange("p (w c) -> p w c", w=3)
        M.c_w_hi, M.c_w_lo = (sb(f"c_w_{part}", [P, 3, CA_H * CA_D], F32R) for part in ("hi", "lo"))
        M.c_wo = sb("c_wo", [P, CA_H * CA_D // P, DIM])
        M.d_wr = sb("d_wr", [P, EXPERTS])
        M.ones = sb("ones", [P, P])
        M.before = sb("before", [P, P])
        M.logits = sb("logits", [P, NT, EXPERTS])
        M.loaded_c, M.LOADED_C = sem("loaded_c"), 4 * 16
        loaded_a, M.ready_a = sem("loaded_a"), sem("ready_a")
        M.READY_A = 4
        block = nc.Block()
        with block:
            @block.sync
            def _(sp):
                for dst, src in ((M.a_wkv[:, :], dram["a_wkv"]), (M.a_wq[:, :], dram["a_wq"]), (M.ident[:, :], dram["ident"]),
                                 (M.a_wo[:, :], dram["a_wo"]), (M.head_sum[:, :], dram["head_sum"]),
                                 (M.state_mask[:, :], dram["state_mask"]), (M.a_cols[:, :], dram["a_cols"]),
                                 (masks[:, :], dram["masks"]), (M.a_bkv[:, :], dram["a_bkv"].partition_broadcast(P)), (M.a_bo[:, :], dram["a_bo"].partition_broadcast(P))):
                    sp.dma_start(dst, src).then_inc(loaded_a, 16)
                for dst, src in ((M.b_wqkv[:, :, :], dram["b_wqkv"]), (M.rotary[:, :, :, :], dram["rotary"]),
                                 (M.center[:, :, :], dram["center"]), (M.mean[:, :], dram["mean"])):
                    sp.dma_start(dst, src).then_inc(M.loaded_b, 16)
                for dst, src in ((M.c_w[:, :, :], dram["c_w"]), (M.c_wo[:, :, :], dram["c_wo"]), (M.d_wr[:, :], dram["d_wr"]), (M.before[:, :], dram["before"])):
                    sp.dma_start(dst, src).then_inc(M.loaded_c, 16)

            @block.vector
            def _(dve):
                nc.vector.memset(M.eps[:, :], EPS).then_inc(M.ready_a, 1)
                dve.wait_ge(loaded_a, 10 * 16)
                nc.vector.tensor_tensor(M.a_wkv[:, :].rearrange("p (k c) -> p k c", k=4), M.a_wkv[:, :].rearrange("p (k c) -> p k c", k=4),
                                        M.ident[:, :].unsqueeze(1).broadcast_to([P, 4, DIM]), ALU.add).then_inc(M.ready_a, 1)
                nc.vector.tensor_copy(M.masks[:, :], masks[:, :]).then_inc(M.ready_a, 1)
                nc.vector.tensor_tensor(M.a_wq[:, :], M.a_wq[:, :], M.ident[:, :], ALU.add).then_inc(M.ready_a, 1)
        linear_attention(nc, M, dram)
        local_transformer(nc, M, dram)
        M.d_w2 = sb("d_w2", [P, EXPERTS, FFN // P, DIM])
        M.d_w1_hi, M.d_w1_lo = (sb(f"d_w1_{part}", [P, EXPERTS, FFN], F32R) for part in ("hi", "lo"))
        M.loaded_d, M.LOADED_D = sem("loaded_d"), 3 * 16
        M.d_loads = ((M.ones[:, 0:P], dram["ones"]), (M.d_w1[:, :, :], dram["d_w1"]), (M.d_w2[:, :, :, :], dram["d_w2"]))
        causal_attention(nc, M, dram)
        experts(nc, M, dram)

def later_arrays(g, T):
    import numpy as np
    swap = lambda a: np.roll(a, LO_D // 2, -1)
    def by_cut(a, rows):
        out = np.zeros((len(a), P, 3) + a.shape[2:], a.dtype)
        for k, (off, w) in enumerate(HID_CUT):
            out[:, :w, k] = a[:, off:off + w]
        return out
    b1 = g["L0_ffn_b1"]
    cols = np.concatenate([g["L0_ffn_ln_g"][:, :, None], g["L0_ffn_ln_b"][:, :, None], g["L0_ffn_b2"][:, :, None],
                           by_cut(b1[:, HID:], 0), by_cut(b1[:, :HID], 0)], 2)
    qs, ks = g["L0_ffn_q_scale"], g["L0_ffn_k_scale"]
    chunked = lambda a: a.reshape(a.shape[:-2] + (-1, P, a.shape[-1])).swapaxes(-3, -2)
    return {
        "b_wqkv": g["L0_ffn_wqkv"].transpose(1, 0, 2),
        "b_table_scale": np.stack([qs, swap(qs), ks, swap(ks)], 1),
        "b_wo": chunked(g["L0_ffn_wo"]),
        "b_w1": g["L0_ffn_w1"],
        "b_w2": by_cut(g["L0_ffn_w2"], 0),
        "b_cols": cols,
        "c_w": np.stack([g[k].reshape(-1, DIM).T for k in ("L1_attn_w_q", "L1_attn_w_k", "L1_attn_w_v")], 1),
        "c_wo": chunked(g["L1_attn_w_o"]),
        "d_wr": g["L1_ffn_Wr"],
        "d_w1": g["L1_ffn_W1"].transpose(1, 0, 2),
        "d_w2": g["L1_ffn_W2"].reshape(EXPERTS, FFN // P, P, DIM).transpose(2, 0, 1, 3),
    }


def constants():
    import numpy as np
    d = np.arange(P)
    tri = lambda keep: np.where(keep, 0.0, -1e30).astype(np.float32)
    half = np.arange(0, LO_D, 2, dtype=np.float64)
    freq = np.arange(TOK)[:, None] * (1.0 / 10000.0 ** (half / LO_D))[None, :]
    base = (half + 0.4 * LO_D) / (1.4 * LO_D)
    scale = base[None, :] ** ((np.arange(TOK) - TOK // 2) / float(WINDOW // 2))[:, None]
    two = lambda a: np.concatenate([a, a], 1)
    sin = np.concatenate([-np.sin(freq), np.sin(freq)], 1)
    rotary = np.stack([two(np.cos(freq) * scale), sin * two(scale), two(np.cos(freq) / scale), sin / two(scale)], 1)
    rotary = rotary.reshape(TILES, P, 4, LO_D).transpose(1, 2, 0, 3)
    q_at, k_at = d[:, None], d[None, :]
    k_wide = np.arange(P + WINDOW)[None, :]
    return {
        "ident": np.eye(P, dtype=np.float32),
        "head_sum": (d[:, None] // LA_D == np.arange(LA_H)[None, :]).astype(np.float32),
        "state_mask": (d[:, None] // LA_D == d[None, :] // LA_D).astype(np.float32) / TOK ** 2,
        "rotary": rotary.astype(np.float32),
        "center": np.stack([np.where((d[:, None] < 64) == first, np.eye(P) - 1.0 / P, 0.0) for first in (True, False)], 1).astype(np.float32),
        "mean": np.full((P, P), 1.0 / P, np.float32),
        "ones": np.ones((P, P), np.float32),
        "before": (d[:, None] < d[None, :]).astype(np.float32),
        "masks": np.concatenate([tri((k_at <= q_at) & (k_at >= q_at - WINDOW)), tri((k_wide >= q_at) & (k_wide <= q_at + WINDOW)),
                                 tri(k_at <= q_at), np.eye(P, dtype=np.float32)], 1),
    }


def kernel(**inputs):
    import numpy as np
    import concourse.bacc as bacc
    from concourse.bass_utils import run_bass_kernel_spmd as run

    g = {k: np.asarray(v) for k, v in inputs.items()}
    x = g["L0_attn_x"]
    T = lambda a: np.ascontiguousarray(np.swapaxes(a, -1, -2))
    arrays = {
        "x": x,
        "x_fea": T(x.reshape(SEQ * TOK, DIM)),
        "a_wkv": np.concatenate([T(g["L0_attn_Wk"][0]), T(g["L0_attn_Wk"][1]), T(g["L0_attn_Wv"][0]), T(g["L0_attn_Wv"][1])], 1),
        "a_wq": T(g["L0_attn_Wq"]),
        "a_wo": T(g["L0_attn_Wo"]),
        "a_cols": np.stack([g["L0_attn_bq"], g["L0_attn_ln_g"], g["L0_attn_ln_b"]], 1),
        "a_bkv": np.concatenate([g["L0_attn_bk"].reshape(-1), g["L0_attn_bv"].reshape(-1)]),
        "a_bo": g["L0_attn_bo"],
    }
    arrays.update(constants())
    arrays.update(later_arrays(g, T))
    arrays = {k: np.ascontiguousarray(v) for k, v in arrays.items()}
    nc = bacc.Bacc("TRN2", target_bir_lowering=False, num_devices=1)
    dram = {}
    for name, a in arrays.items():
        dram[name] = nc.dram_tensor("in_" + name, a.shape, mybir.dt.from_np(a.dtype), kind="ExternalInput").ap()
    dram["out"] = nc.dram_tensor("out_x", x.shape, F32, kind="ExternalOutput").ap()
    program(nc, dram)
    return run(nc, [{"in_" + k: a for k, a in arrays.items()}], core_ids=[0]).results[0]["out_x"]
```
